# Optimizing a Trainium2 kernel written in Bass

```python
import numpy as np
import jax
import jax.numpy as jnp

def _softmax(x, axis=-1):
    return jax.nn.softmax(x, axis=axis)

def _gelu(x):
    return jax.nn.gelu(x, approximate=True)

def _silu(x):
    return jax.nn.silu(x)

def _sigmoid(x):
    return jax.nn.sigmoid(x)

def _layernorm(x, axis=-1, eps=1e-05):
    m = jnp.mean(x, axis=axis, keepdims=True)
    v = jnp.var(x, axis=axis, keepdims=True)
    return (x - m) / jnp.sqrt(v + eps)

def _scatter_add(tgt, idx, src, axis=0):
    return tgt.at[idx].add(src)

def _segment_sum(src, seg, n):
    return jax.ops.segment_sum(src, seg, n)
kernel_name = 'mk_early_fusion_embed_d1_tok_img512_r4_51fb14'

def setup_inputs(seed: int=0):
    np.random.seed(seed)
    _w = jnp.asarray

    def _rec_inputs():
        import jax
        import jax.numpy as jnp
        _rk = jax.random.key(seed)
        x = -0.000121822 + 0.999869 * jax.random.normal(jax.random.fold_in(_rk, 1), (64, 3, 196, 196), jnp.float32)
        x_txt = jax.random.randint(jax.random.fold_in(_rk, 51), (64, 32), 0, 64, jnp.int32)
        return (x, x_txt)
    x, x_txt = _rec_inputs()

    def _L0_tok_setup():
        import jax, jax.numpy as jnp
        import numpy as np
        B, C, H, N_P, HID = (64, 3, 196, 14, 128)
        P = H // N_P
        IN_DIM = C * P * P
        SEQ = N_P * N_P + 1

        def sinusoidal_position(length, d):
            pos = jnp.arange(length, dtype=jnp.float32)[:, None]
            i = jnp.arange(d)[None, :]
            angle = pos / jnp.power(10000.0, (2 * (i // 2)).astype(jnp.float32) / d)
            return jnp.where(i % 2 == 0, jnp.sin(angle), jnp.cos(angle)).astype(jnp.float32)
        key = jax.random.key(seed)
        k_img, k_w, k_b, k_tok = jax.random.split(key, 4)
        img = jax.random.normal(k_img, (B, C, H, H), dtype=jnp.float32)
        W = jax.random.normal(k_w, (HID, IN_DIM), dtype=jnp.float32) / np.sqrt(IN_DIM)
        b = jax.random.normal(k_b, (HID,), dtype=jnp.float32) * 0.01
        token = jax.random.uniform(k_tok, (1, HID), dtype=jnp.float32)
        pos = sinusoidal_position(SEQ, HID)
        return {'img': img, 'W': W, 'b': b, 'token': token, 'pos': pos}
    _L0_tok_all = _L0_tok_setup()
    _L0_tok_in = {k: v for k, v in _L0_tok_all.items() if k in ('W', 'b', 'token', 'pos')}
    del _L0_tok_all

    def _L0_txt_setup():
        import jax, jax.numpy as jnp
        import numpy as np
        HASH_VOCAB = 25000
        BASE = 257
        NGRAM_SIZES = (2, 3, 4)

        def _ngram_hash(tokens, n, vocab):
            B, S = tokens.shape
            padded = jnp.pad(tokens, ((0, 0), (n - 1, 0)))
            h = jnp.zeros((B, S), dtype=jnp.int32)
            for i in range(n):
                p = pow(BASE, n - 1 - i, vocab)
                h = h + padded[:, i:i + S] * jnp.int32(p)
            return h % vocab
        key = jax.random.key(seed)
        k1, k2, k3, k4 = jax.random.split(key, 4)
        tokens = jax.random.randint(k1, (8, 1024), 0, 64, dtype=jnp.int32)
        emb2 = jax.random.normal(k2, (HASH_VOCAB, 128), dtype=jnp.float32)
        emb3 = jax.random.normal(k3, (HASH_VOCAB, 128), dtype=jnp.float32)
        emb4 = jax.random.normal(k4, (HASH_VOCAB, 128), dtype=jnp.float32)
        return {'tokens': tokens, 'emb2': emb2, 'emb3': emb3, 'emb4': emb4}
    _L0_txt_all = _L0_txt_setup()
    _L0_txt_in = {k: v for k, v in _L0_txt_all.items() if k in ('emb2', 'emb3', 'emb4')}
    del _L0_txt_all

    def _L0_attn_setup():
        import math
        import jax, jax.numpy as jnp
        import numpy as np
        B, N, D = (32, 256, 128)
        E, S = (256, 128)
        key = jax.random.key(seed)
        ks = jax.random.split(key, 6)
        x = jax.random.normal(ks[0], (B, N, D), dtype=jnp.float32)
        w = jax.random.uniform(ks[1], (2 * N - 1,), dtype=jnp.float32)
        limit = math.sqrt(6.0 / (D + 2 * E + S))
        uv_w = jax.random.uniform(ks[2], (D, 2 * E + S), minval=-limit, maxval=limit, dtype=jnp.float32)
        o_w = jax.random.normal(ks[3], (E, D), dtype=jnp.float32) * 0.02
        gamma = jax.random.uniform(ks[4], (2, S), dtype=jnp.float32)
        beta = jax.random.uniform(ks[5], (2, S), dtype=jnp.float32)
        g = jnp.asarray(math.sqrt(D), dtype=jnp.float32)
        res_scale = jnp.ones((D,), dtype=jnp.float32)
        return {'x': x, 'w': w, 'uv_w': uv_w, 'o_w': o_w, 'gamma': gamma, 'beta': beta, 'g': g, 'res_scale': res_scale}
    _L0_attn_all = _L0_attn_setup()
    _L0_attn_in = {k: v for k, v in _L0_attn_all.items() if k in ('w', 'uv_w', 'o_w', 'gamma', 'beta', 'g', 'res_scale')}
    del _L0_attn_all

    def _L0_ffn_setup():
        import jax, jax.numpy as jnp
        import numpy as np
        B, S, D, F, E, NS, K = (2, 512, 128, 512, 8, 2, 2)
        key = jax.random.key(seed)
        ks = jax.random.split(key, 6)
        scale = 0.02

        def p(k, shape):
            return jax.random.normal(k, shape, jnp.float32) * scale
        return {'x': jax.random.normal(ks[0], (B, S, D), jnp.float32), 'gate_w': p(ks[1], (E, D)), 'gate_b': jnp.zeros((E,), jnp.float32), 'sw1': p(ks[2], (NS, F, D)), 'sb1': jnp.zeros((NS, F), jnp.float32), 'sw2': p(ks[3], (NS, D, F)), 'sb2': jnp.zeros((NS, D), jnp.float32), 'rw1': p(ks[4], (E, F, D)), 'rb1': jnp.zeros((E, F), jnp.float32), 'rw2': p(ks[5], (E, D, F)), 'rb2': jnp.zeros((E, D), jnp.float32)}
    _L0_ffn_all = _L0_ffn_setup()
    _L0_ffn_in = {k: v for k, v in _L0_ffn_all.items() if k in ('gate_w', 'gate_b', 'sw1', 'sb1', 'sw2', 'sb2', 'rw1', 'rb1', 'rw2', 'rb2')}
    del _L0_ffn_all
    return {'x': x, 'x_txt': x_txt, 'L0_tok_W': _L0_tok_in['W'], 'L0_tok_b': _L0_tok_in['b'], 'L0_tok_token': _L0_tok_in['token'], 'L0_tok_pos': _L0_tok_in['pos'], 'L0_txt_emb2': _L0_txt_in['emb2'], 'L0_txt_emb3': _L0_txt_in['emb3'], 'L0_txt_emb4': _L0_txt_in['emb4'], 'L0_attn_w': _L0_attn_in['w'], 'L0_attn_uv_w': _L0_attn_in['uv_w'], 'L0_attn_o_w': _L0_attn_in['o_w'], 'L0_attn_gamma': _L0_attn_in['gamma'], 'L0_attn_beta': _L0_attn_in['beta'], 'L0_attn_g': _L0_attn_in['g'], 'L0_attn_res_scale': _L0_attn_in['res_scale'], 'L0_ffn_gate_w': _L0_ffn_in['gate_w'], 'L0_ffn_gate_b': _L0_ffn_in['gate_b'], 'L0_ffn_sw1': _L0_ffn_in['sw1'], 'L0_ffn_sb1': _L0_ffn_in['sb1'], 'L0_ffn_sw2': _L0_ffn_in['sw2'], 'L0_ffn_sb2': _L0_ffn_in['sb2'], 'L0_ffn_rw1': _L0_ffn_in['rw1'], 'L0_ffn_rb1': _L0_ffn_in['rb1'], 'L0_ffn_rw2': _L0_ffn_in['rw2'], 'L0_ffn_rb2': _L0_ffn_in['rb2']}

def reference(x, x_txt, L0_tok_W, L0_tok_b, L0_tok_token, L0_tok_pos, L0_txt_emb2, L0_txt_emb3, L0_txt_emb4, L0_attn_w, L0_attn_uv_w, L0_attn_o_w, L0_attn_gamma, L0_attn_beta, L0_attn_g, L0_attn_res_scale, L0_ffn_gate_w, L0_ffn_gate_b, L0_ffn_sw1, L0_ffn_sb1, L0_ffn_sw2, L0_ffn_sb2, L0_ffn_rw1, L0_ffn_rb1, L0_ffn_rw2, L0_ffn_rb2):
    import jax
    import jax.numpy as jnp

    def _L0_tok_ref(img, W, b, token, pos):
        import jax, jax.numpy as jnp
        import numpy as np
        B, C, H, N_P, HID = (64, 3, 196, 14, 128)
        P = H // N_P
        IN_DIM = C * P * P
        SEQ = N_P * N_P + 1

        def sinusoidal_position(length, d):
            pos = jnp.arange(length, dtype=jnp.float32)[:, None]
            i = jnp.arange(d)[None, :]
            angle = pos / jnp.power(10000.0, (2 * (i // 2)).astype(jnp.float32) / d)
            return jnp.where(i % 2 == 0, jnp.sin(angle), jnp.cos(angle)).astype(jnp.float32)
        Bn = img.shape[0]
        patches = img.reshape(Bn, C, N_P, P, N_P, P)
        patches = patches.transpose(0, 2, 4, 1, 3, 5).reshape(Bn, N_P * N_P, IN_DIM)
        tokens = jnp.einsum('bsd,hd->bsh', patches, W) + b
        cls = jnp.broadcast_to(token[None, :, :], (Bn, 1, HID))
        out = jnp.concatenate([cls, tokens], axis=1) + pos
        return out

    def _L0_txt_ref(tokens, emb2, emb3, emb4):
        import jax, jax.numpy as jnp
        import numpy as np
        HASH_VOCAB = 25000
        BASE = 257
        NGRAM_SIZES = (2, 3, 4)

        def _ngram_hash(tokens, n, vocab):
            B, S = tokens.shape
            padded = jnp.pad(tokens, ((0, 0), (n - 1, 0)))
            h = jnp.zeros((B, S), dtype=jnp.int32)
            for i in range(n):
                p = pow(BASE, n - 1 - i, vocab)
                h = h + padded[:, i:i + S] * jnp.int32(p)
            return h % vocab
        tables = {2: emb2, 3: emb3, 4: emb4}
        total = None
        for n in NGRAM_SIZES:
            idx = _ngram_hash(tokens, n, HASH_VOCAB)
            e = tables[n][idx]
            total = e if total is None else total + e
        return total

    def _L0_attn_ref(x, w, uv_w, o_w, gamma, beta, g, res_scale):
        import math
        import jax, jax.numpy as jnp
        import numpy as np
        B, N, D = (32, 256, 128)
        E, S = (256, 128)
        eps = 1e-05
        sqrt_s = math.sqrt(S)
        n = x.shape[1]
        norm = jnp.maximum(jnp.linalg.norm(x, axis=-1, keepdims=True), eps)
        xn = x / norm * g
        uv = jax.nn.silu(xn @ uv_w)
        u, v, base = (uv[..., :E], uv[..., E:2 * E], uv[..., 2 * E:])
        qk_base = base[:, :, None, :] * gamma + beta
        q, k = (qk_base[:, :, 0, :], qk_base[:, :, 1, :])
        qk = jnp.einsum('bms,bns->bmn', q, k)
        i = jnp.arange(n)
        idx = n - 1 + i[None, :] - i[:, None]
        qk = qk + w[idx][None, :, :]
        kernel = jnp.square(jax.nn.relu(qk / sqrt_s))
        out = u * jnp.einsum('bmn,bne->bme', kernel, v)
        out = out @ o_w
        return x * res_scale + out

    def _L0_ffn_ref(x, gate_w, gate_b, sw1, sb1, sw2, sb2, rw1, rb1, rw2, rb2):
        import jax, jax.numpy as jnp
        import numpy as np
        B, S, D, F, E, NS, K = (2, 512, 128, 512, 8, 2, 2)
        b, s, d = x.shape
        t = x.reshape(-1, d)
        T = t.shape[0]
        hs = jax.nn.gelu(jnp.einsum('td,nfd->ntf', t, sw1) + sb1[:, None, :], approximate=False)
        shared = jnp.einsum('ntf,ndf->td', hs, sw2) + sb2.sum(axis=0)
        logits = t @ gate_w.T + gate_b
        probs = jax.nn.softmax(logits, axis=-1)
        top_v, top_i = jax.lax.top_k(probs, K)
        cw = jnp.zeros_like(probs).at[jnp.arange(T)[:, None], top_i].add(top_v)
        hr = jax.nn.gelu(jnp.einsum('td,efd->etf', t, rw1) + rb1[:, None, :], approximate=False)
        oe = jnp.einsum('etf,edf->etd', hr, rw2) + rb2[:, None, :]
        routed = jnp.einsum('etd,te->td', oe, cw)
        return (shared + routed).reshape(b, s, d)
    h = _L0_tok_ref(x, L0_tok_W, L0_tok_b, L0_tok_token, L0_tok_pos)
    h = jnp.concatenate([h, _L0_txt_ref(x_txt, L0_txt_emb2, L0_txt_emb3, L0_txt_emb4)], axis=1)
    h = h + _L0_attn_ref(_layernorm(h, axis=-1), L0_attn_w, L0_attn_uv_w, L0_attn_o_w, L0_attn_gamma, L0_attn_beta, L0_attn_g, L0_attn_res_scale)
    h = h + _L0_ffn_ref(_layernorm(h, axis=-1), L0_ffn_gate_w, L0_ffn_gate_b, L0_ffn_sw1, L0_ffn_sb1, L0_ffn_sw2, L0_ffn_sb2, L0_ffn_rw1, L0_ffn_rb1, L0_ffn_rw2, L0_ffn_rb2)
    return h

_drawn_inputs = setup_inputs


def setup_inputs(seed=0):
    import zlib

    import numpy as np

    out = dict(_drawn_inputs(seed))
    spreads = {'L0_attn_res_scale': (1.0, 0.6),
     'L0_ffn_gate_b': (0.0, 0.8),
     'L0_ffn_sb1': (0.0, 0.8),
     'L0_ffn_sb2': (0.0, 2.0),
     'L0_ffn_rb1': (0.0, 2.0),
     'L0_ffn_rb2': (0.0, 2.0)}
    factors = {'L0_tok_b': 2.802,
     'L0_attn_w': 22.361,
     'L0_ffn_gate_w': 8.0,
     'L0_ffn_sw1': 8.0,
     'L0_ffn_sw2': 8.0,
     'L0_ffn_rw1': 8.0,
     'L0_ffn_rw2': 8.0}
    for name, (base, spread) in spreads.items():
        noise = np.random.default_rng([zlib.crc32(name.encode()), seed]).standard_normal(out[name].shape)
        drawn = base * np.exp(spread * noise) if base else spread * noise
        out[name] = jnp.asarray(drawn.astype(out[name].dtype))
    for name, factor in factors.items():
        out[name] = (out[name] * factor).astype(out[name].dtype)
    return out
```

```python
from contextlib import ExitStack

import numpy as np

import concourse.bass as bass
from concourse import mybir

FP32 = mybir.dt.float32
FP16 = mybir.dt.float16
I32 = mybir.dt.int32
U32 = mybir.dt.uint32
ALU = mybir.AluOpType
ACT = mybir.ActivationFunctionType
AXX = mybir.AxisListType.X

P = 128
IMGS, CHANNELS, SIDE, GRID = 64, 3, 196, 14
PATCHES = GRID * GRID
PATCH_DIM = CHANNELS * (SIDE // GRID) ** 2
TEXT = 32
SEQ = 1 + PATCHES + TEXT
CHUNKS = ((0, 117), (117, 112))
assert CHUNKS[1][0] + CHUNKS[1][1] == SEQ
PAIRS = IMGS // 2
PAIR_SEQ = 2 * SEQ
PAIR_PATCHES = 2 * PATCHES
NCH = 2 * IMGS
KP, KN = 126, 4
KREST = PATCH_DIM - KP * KN
HID = 128
E_GAU = 256
VOCAB, BASE = 25000, 257
EXPERTS, SHARED, F = 8, 2, 512
NF = F // P
ALL_EXPERTS = EXPERTS + SHARED
WCOLS = 2 * ALL_EXPERTS * F
WBLOCK = WCOLS // PAIRS
W2_AT = ALL_EXPERTS * F
TOKENS = IMGS * SEQ
TILE = 256
TILE_CH = TILE // P
TILES = (2 * TOKENS + EXPERTS * (TILE - 1)) // TILE
ROW = HID + 2
FILL_ROWS = -(-TILES * TILE // (PAIRS * P)) * P
SLOT_ROWS = FILL_ROWS * PAIRS
UNUSED = float(1 << 20)
EPS = 1e-5


class Own:

    def __init__(self, eng, sem, start=0):
        self.eng, self.sem, self.n = eng, sem, start

    def did(self, instruction):
        instruction.then_inc(self.sem, 1)
        self.n = self.n + 1

    def wait(self):
        self.eng.wait_ge(self.sem, self.n)


def settle(eng):
    eng.nop(nofuse=True)


def pair_loop(eng, step, lo, hi):
    assert lo % 2 == 0 and hi % 2 == 0
    with eng.Fori(lo // 2, hi // 2) as j:
        for parity in range(2):
            step(2 * j + parity, parity)


def build(nc, xmain, xrest, tokw_main, tokw_rest, txt, tokb, token, pos, emb2, emb3, emb4,
          w_rel, uv_w, o_w, gamma, beta, g, res, gate_w, gate_b, ffn_w, ffn_b1, ffn_b2, out,
          stop=5, dbg=None):
    x2t_dram = nc.dram_tensor("x2t_dram", [PAIRS, P, PAIR_SEQ], FP32).ap()
    x2r_dram = nc.dram_tensor("x2r_dram", [PAIRS, P, 4, HID], FP32).ap()
    slots_dram = nc.dram_tensor("slots_dram", [SLOT_ROWS, ROW], FP32).ap()
    y_dram = nc.dram_tensor("y_dram", [2 * TOKENS, HID], FP32).ap()

    with ExitStack() as keep:
        def sbuf(name, shape, dt=FP32, ctx=keep):
            return ctx.enter_context(nc.sbuf_tensor(name, shape, dt))

        bank = [keep.enter_context(nc.psum_tensor(f"bank{b}", [P, 512], FP32)) for b in range(8)]
        acc = sbuf("acc", [P, NCH, HID])
        w_hi = sbuf("w_hi", [P, WCOLS], FP16)
        w_lo = sbuf("w_lo", [P, WCOLS], FP16)
        b1 = sbuf("b1", [P, ALL_EXPERTS * NF])
        b2 = sbuf("b2", [ALL_EXPERTS, HID])
        ident = sbuf("ident", [P, P])
        top8 = sbuf("top8", [P, NCH, 8])
        top_i = sbuf("top_i", [P, NCH, 2])
        token2 = sbuf("token2", [P, NCH])

        embed_and_attend(nc, bank, acc, w_hi, w_lo, b1, b2, ident, top8, top_i, token2,
                         xmain, xrest, tokw_main, tokw_rest, txt, tokb, token, pos, emb2, emb3,
                         emb4, w_rel, uv_w, o_w, gamma, beta, g, res, gate_w, gate_b, ffn_w,
                         ffn_b1, ffn_b2, x2t_dram, x2r_dram, slots_dram)
        if stop >= 2:
            cw = sbuf("cw", [P, NCH, ALL_EXPERTS])
            cw01 = sbuf("cw01", [P, NCH, 2])
            slot_u = sbuf("slot_u", [P, NCH, 2], U32)
            tile_e = sbuf("tile_e", [P, TILES])
            tile_ei = sbuf("tile_ei", [P, TILES], I32)
            route(nc, bank, top8, top_i, cw, cw01, slot_u, tile_e, tile_ei)
        if stop >= 3:
            shared_ffn(nc, bank, acc, w_hi, w_lo, b1, b2, ident, top_i, token2, cw, slot_u,
                       x2t_dram, x2r_dram, slots_dram)
        if stop >= 4:
            routed_ffn(nc, bank, w_hi, w_lo, b1, ident, tile_e, tile_ei, slots_dram, y_dram)
        if stop >= 5:
            combine(nc, acc, cw01, y_dram, out)
        if dbg is not None:
            dbg(nc, locals())


def embed_and_attend(nc, bank, acc, w_hi, w_lo, b1, b2, ident, top8, top_i, token2,
                     xmain, xrest, tokw_main, tokw_rest, txt, tokb, token, pos, emb2, emb3, emb4,
                     w_rel, uv_w, o_w, gamma, beta, g, res, gate_w, gate_b, ffn_w, ffn_b1, ffn_b2,
                     x2t_dram, x2r_dram, slots_dram):
    with ExitStack() as ctx:
        def sb(name, shape, dt=FP32):
            return ctx.enter_context(nc.sbuf_tensor(name, shape, dt))

        def sem(name):
            return ctx.enter_context(nc.semaphore(name))

        tokw = sb("tokw", [P, KN + 1, HID])
        uvw = sb("uvw", [P, 2 * E_GAU + HID])
        ow = sb("ow", [P, 2, HID])
        posb = sb("posb", [P, SEQ - TEXT])
        tokbt = sb("tokbt", [P, 2])
        gb = sb("gb", [P, 4])
        gs = sb("gs", [P, 1])
        resb = sb("resb", [P, HID])
        gatew = sb("gatew", [P, EXPERTS])
        gateb = sb("gateb", [P, EXPERTS])
        rel = sb("rel", [P, 2, SEQ])
        tsh = sb("tsh", [P, 4, 16])
        tshi = sb("tshi", [P, 4, 16], I32)
        hsh = sb("hsh", [P, 3, 16])
        hq = sb("hq", [P, 3, 16])
        hqi = sb("hqi", [P, 3, 16], I32)
        hashes = sb("hashes", [P, 3, 16], U32)
        hash_now = sb("hash_now", [P, 3], U32)
        emb = sb("emb", [P, 3, HID])
        esum = sb("esum", [P, HID])
        xin = sb("xin", [P, 2, KN + 1, PAIR_PATCHES])
        wstage = sb("wstage", [P, 2, WBLOCK])
        hT = sb("hT", [P, 2, 2, SEQ])
        hn = sb("hn", [P, 2, 4, HID])
        stats = sb("stats", [P, 4, 6])
        mv = sb("mv", [P, 4, 2])
        var2 = sb("var2", [P, 2, 4])
        powers = sb("powers", [P, 3, 4])
        rstd = sb("rstd", [P, 2, 4])
        nrm = sb("nrm", [P, 4])
        scl = sb("scl", [P, 4])
        xa = sb("xa", [P, 2, 4, HID])
        xn = sb("xn", [P, 4, HID])
        xnT = sb("xnT", [P, 2, PAIR_SEQ])
        base_s = sb("base_s", [P, PAIR_SEQ])
        qk_sb = sb("qk_sb", [P, 2, PAIR_SEQ])
        uT = sb("uT", [P, 2, PAIR_SEQ])
        v_sb = sb("v_sb", [P, 2, 2, E_GAU])
        sc = sb("sc", [P, 2, 2, SEQ])
        kern = sb("kern", [P, 2, 2, SEQ])
        uav = sb("uav", [P, 2, 2, SEQ])
        hx = sb("hx", [P, 4, HID])
        stats2 = sb("stats2", [P, 4, 6])
        mv2 = sb("mv2", [P, 4, 2])
        rstd2 = sb("rstd2", [P, 4])
        x2f = sb("x2f", [P, 2, 4, HID])
        x2T = sb("x2T", [P, PAIR_SEQ])
        x2T16 = sb("x2T16", [P, 2, 2, PAIR_SEQ], FP16)
        x2r16 = sb("x2r16", [P, 2, 4, 2, HID], FP16)
        lgs = sb("lgs", [P, 4, EXPERTS])
        mx8 = sb("mx8", [P, 4, 8])
        mi8 = sb("mi8", [P, 4, 8], U32)
        fill = sb("fill", [P, FILL_ROWS // P, ROW])

        tokb_bank, tr1_bank, tr2_bank, o_bank = bank[0], bank[1], bank[2], bank[7]
        uv_bank, av_bank = bank[3:5], bank[5:7]

        w_in = sem("w_in")
        w_late = sem("w_late")
        txt_in = sem("txt_in")
        x_in = [sem(f"x_in{n}") for n in range(2)]
        ws_in = [sem(f"ws_in{n}") for n in range(2)]
        emb_in = sem("emb_in")
        t_out = [sem(f"t_out{n}") for n in range(2)]
        r_out = [sem(f"r_out{n}") for n in range(2)]
        fill_out = sem("fill_out")
        zeroed = sem("zeroed")
        tables = sem("tables")
        const_p = sem("const_p")
        hashed = sem("hashed")
        setup_v = sem("setup_v")
        tok_done, tr1_done, tr2_done, txt_done = sem("tok_done"), sem("tr1_done"), sem("tr2_done"), sem("txt_done")
        uv_done, qk_done, av_done, o_done = sem("uv_done"), sem("qk_done"), sem("av_done"), sem("o_done")
        tr3_done, lg_done = sem("tr3_done"), sem("lg_done")
        hT_ready, xn_ready, t_done, kern_ready = sem("hT_ready"), sem("xn_ready"), sem("t_done"), sem("kern_ready")
        uav_ready, mid_ready, x2_ready, lg_read = sem("uav_ready"), sem("mid_ready"), sem("x2_ready"), sem("lg_read")
        top_ready = sem("top_ready")
        bn_front, bn_mid, mv_ready, mv2_ready = sem("bn_front"), sem("bn_mid"), sem("mv_ready"), sem("mv2_ready")
        txt_copied, hn_ready, xnT_ready, sil, qk_ready, x2T_ready = (
            sem("txt_copied"), sem("hn_ready"), sem("xnT_ready"), sem("sil"), sem("qk_ready"), sem("x2T_ready"))
        base_ready = sem("base_ready")
        hash_set, esum1, esum_ready = sem("hash_set"), sem("esum1"), sem("esum_ready")
        hx1, hx_ready, row_hi, row_ready, t_hi, t_ready = (
            sem("hx1"), sem("hx_ready"), sem("row_hi"), sem("row_ready"), sem("t_hi"), sem("t_ready"))
        scl_own, scl_ready, rstd2_own, rstd2_ready = sem("scl_own"), sem("scl_ready"), sem("rstd2_own"), sem("rstd2_ready")
        ws_hi, ws_done, top_kept = sem("ws_hi"), sem("ws_done"), sem("top_kept")

        block = ctx.enter_context(nc.Block())
        N_W, N_LATE = 15, 5

        @block.sync
        def _(sp):
            for k in range(4):
                sp.wait_ge(zeroed, 2)
                for q in range(P // TEXT):
                    sp.dma_start(tshi[q * TEXT + k:(q + 1) * TEXT, k, :],
                                 txt[q * TEXT:(q + 1) * TEXT - k, :]).then_inc(txt_in, 16)

            def load_x(i, parity):
                sp.dma_start(xin[0:KP, parity, 0:KN, :], xmain[i]).then_inc(x_in[parity], 16)
                sp.dma_start(xin[0:KREST, parity, KN, :], xrest[i]).then_inc(x_in[parity], 16)

            def load_w(i, parity):
                sp.dma_start(wstage[:, parity, :], ffn_w[:, bass.ds(i * WBLOCK, WBLOCK)]).then_inc(ws_in[parity], 16)

            load_x(0, 0)
            for dst, src in ((tokw[0:KP, 0:KN, :], tokw_main), (tokw[0:KREST, KN, :], tokw_rest),
                             (posb[:, :], pos), (tokbt[:, 0:1], tokb), (tokbt[:, 1:2], token),
                             (uvw[:, :], uv_w), (gb[:, 0:2], gamma), (gb[:, 2:4], beta),
                             (gs[:, :], g), (resb[:, :], res), (gatew[:, :], gate_w),
                             (gateb[:, :], gate_b), (ow[:, :, :], o_w)):
                sp.dma_start(dst, src).then_inc(w_in, 16)
            for c, (at, n) in enumerate(CHUNKS):
                sp.dma_start(rel[0:n, c, :], w_rel[at:at + n, :]).then_inc(w_in, 16)
            load_x(1, 1)
            load_w(0, 0)
            load_w(1, 1)
            sp.dma_start(b1[:, :], ffn_b1).then_inc(w_late, 16)
            sp.dma_start(b2[:, :], ffn_b2).then_inc(w_late, 16)

            def store_x2(b, parity):
                sp.wait_ge(row_ready, b + 1)
                sp.dma_start(x2r_dram[b], x2r16[:, parity].bitcast(FP32).rearrange("p c h d -> p c (h d)")
                             ).then_inc(r_out[parity], 16)
                sp.wait_ge(t_ready, b + 1)
                sp.dma_start(x2t_dram[b], x2T16[:, parity].bitcast(FP32).rearrange("p h n -> p (h n)")
                             ).then_inc(t_out[parity], 16)

            def step(i, parity, first=False, last=False):
                sp.dma_start(slots_dram[bass.ds(i * FILL_ROWS, FILL_ROWS), :].rearrange("(t p) w -> p t w", p=P),
                             fill[:, :, :]).then_inc(fill_out, 16)
                if not last:
                    sp.wait_ge(tok_done, i + 1)
                    load_x(i + 2, parity)
                    sp.wait_ge(ws_done, i + 1)
                    load_w(i + 2, parity)
                if not first:
                    store_x2(i - 1, 1 - parity)

            sp.wait_ge(tables, 2)
            step(0, 0, first=True)
            step(1, 1)
            pair_loop(sp, step, 2, PAIRS - 2)
            step(PAIRS - 2, 0, last=True)
            step(PAIRS - 1, 1, last=True)
            store_x2(PAIRS - 1, 1)
            for parity in range(2):
                sp.wait_ge(r_out[parity], 16 * PAIRS // 2)
                sp.wait_ge(t_out[parity], 16 * PAIRS // 2)
            sp.wait_ge(fill_out, 16 * PAIRS)
            sp.wait_ge(w_late, 32)

        @block.gpsimd
        def _(pool):
            pool.memset(tshi[:, :, :], 0).then_inc(zeroed, 1)
            pool.memset(rel[:, :, :], 0.0).then_inc(zeroed, 1)
            pool.memset(ident[:, :], 0.0).then_inc(const_p, 1)
            pool.wait_ge(const_p, 1)
            pool.affine_select(out=ident[:, :], in_=ident[:, :], compare_op=ALU.not_equal, fill=1.0,
                               base=0, pattern=[[-1, P]], channel_multiplier=1).then_inc(tables, 1)
            pool.memset(fill[:, :, :], 0.0).then_inc(const_p, 1)
            for c, (at, _) in enumerate(CHUNKS):
                pool.iota(token2[:, c:NCH:2], pattern=[[2 * SEQ, IMGS]], base=2 * at, channel_multiplier=2,
                          allow_small_or_imprecise_dtypes=True).then_inc(const_p, 1)
            for n, power in enumerate((-0.5, 0.5, -1.0)):
                pool.memset(powers[:, n, :], power).then_inc(const_p, 1)
            pool.wait_ge(const_p, 7)
            pool.memset(fill[:, :, HID:HID + 1], UNUSED).then_inc(tables, 1)
            pool.wait_ge(hashed, 1)

            def gather_text(grp):
                if not (isinstance(grp, int) and grp == 0):
                    pool.wait_ge(esum_ready, grp)
                settle(pool)
                pool.tensor_copy(hash_now[:, :].rearrange("p (n o) -> p n o", o=1),
                                 hashes[:, :, bass.ds(grp, 1)]).then_inc(hash_set, 1)
                pool.wait_ge(hash_set, grp + 1)
                settle(pool)
                for n, table in enumerate((emb2, emb3, emb4)):
                    pool.indirect_dma_start(
                        out=emb[:, n, :], out_offset=None, in_=table,
                        in_offset=bass.IndirectOffsetOnAxis(ap=hash_now[:, n:n + 1], axis=0)).then_inc(emb_in, 16)

            def sum_text(grp):
                pool.wait_ge(emb_in, 48 * (grp + 1))
                if not (isinstance(grp, int) and grp == 0):
                    pool.wait_ge(txt_done, grp)
                pool.tensor_tensor(esum[:, :], emb[:, 0, :], emb[:, 1, :], ALU.add).then_inc(esum1, 1)
                pool.wait_ge(esum1, grp + 1)
                pool.tensor_tensor(esum[:, :], esum[:, :], emb[:, 2, :], ALU.add).then_inc(esum_ready, 1)

            def residual(i, parity):
                pool.wait_ge(xn_ready, i + 1)
                pool.wait_ge(hn_ready, i + 1)
                if not (isinstance(i, int) and i == 0):
                    pool.wait_ge(mid_ready, i)
                pool.tensor_tensor(hx[:, :, :], xa[:, parity], resb[:, :].rearrange("p (o d) -> p o d", o=1)
                                   .to_broadcast([P, 4, HID]), ALU.mult).then_inc(hx1, 1)
                pool.wait_ge(hx1, i + 1)
                pool.tensor_tensor(hx[:, :, :], hx[:, :, :], hn[:, parity], ALU.add).then_inc(hx_ready, 1)

            def split_w(i, parity):
                pool.wait_ge(ws_hi, i + 1)
                pool.tensor_tensor(w_lo[:, bass.ds(i * WBLOCK, WBLOCK)], wstage[:, parity, :],
                                   w_hi[:, bass.ds(i * WBLOCK, WBLOCK)], ALU.subtract).then_inc(ws_done, 1)

            def split_x2(b, parity):
                pool.wait_ge(row_hi, b + 1)
                pool.tensor_tensor(x2r16[:, parity, :, 1, :], x2f[:, parity], x2r16[:, parity, :, 0, :],
                                   ALU.subtract).then_inc(row_ready, 1)
                pool.wait_ge(t_hi, b + 1)
                pool.tensor_tensor(x2T16[:, parity, 1, :], x2T[:, :], x2T16[:, parity, 0, :],
                                   ALU.subtract).then_inc(t_ready, 1)
                pool.wait_ge(top_ready, 8 * (b + 1))
                settle(pool)
                pool.tensor_copy(top8[:, bass.ds(4 * b, 4), :], mx8[:, :, :]).then_inc(top_kept, 1)
                pool.tensor_copy(top_i[:, bass.ds(4 * b, 4), :], mi8[:, :, 0:2]).then_inc(top_kept, 1)

            def front_scales(n):
                own = Own(pool, scl_own, 6 * n)
                pool.wait_ge(mv_ready, n + 1)
                settle(pool)
                pool.tensor_scalar(var2[:, 0, :], mv[:, :, 1], EPS, None, ALU.add)
                own.did(pool.tensor_scalar(var2[:, 1, :], mv[:, :, 1], float(HID), None, ALU.mult))
                own.wait()
                own.did(pool.tensor_tensor(rstd[:, :, :], var2[:, :, :], powers[:, 0:2, :], ALU.pow))
                own.wait()
                own.did(pool.tensor_tensor(nrm[:, :], rstd[:, 0, :], rstd[:, 1, :], ALU.mult))
                own.wait()
                settle(pool)
                own.did(pool.tensor_scalar(nrm[:, :], nrm[:, :], EPS, None, ALU.max))
                own.wait()
                own.did(pool.tensor_tensor(nrm[:, :], nrm[:, :], powers[:, 2, :], ALU.pow))
                own.wait()
                settle(pool)
                own.did(pool.tensor_scalar(nrm[:, :], nrm[:, :], gs[:, 0:1], None, ALU.mult))
                own.wait()
                pool.tensor_tensor(scl[:, :], nrm[:, :], rstd[:, 0, :], ALU.mult).then_inc(scl_ready, 1)

            def mid_scales(i):
                pool.wait_ge(mv2_ready, i + 1)
                settle(pool)
                pool.tensor_scalar(rstd2[:, :], mv2[:, :, 1], EPS, None, ALU.add).then_inc(rstd2_own, 1)
                pool.wait_ge(rstd2_own, i + 1)
                pool.tensor_tensor(rstd2[:, :], rstd2[:, :], powers[:, 0, :], ALU.pow).then_inc(rstd2_ready, 1)

            def step(i, parity, first=False, last=False, more_text=True, grp=None):
                residual(i, parity)
                if more_text and parity == 0:
                    grp = i // 2 + 1 if isinstance(i, int) else grp
                    gather_text(grp)
                if not first:
                    split_x2(i - 1, 1 - parity)
                if not last:
                    front_scales(i + 1)
                    if more_text and parity == 0:
                        sum_text(grp)
                split_w(i, parity)
                mid_scales(i)

            gather_text(0)
            sum_text(0)
            pool.wait_ge(w_in, 16 * N_W)
            front_scales(0)
            step(0, 0, first=True)
            step(1, 1)
            with pool.Fori(1, PAIRS // 2 - 1) as j:
                step(2 * j, 0, grp=j + 1)
                step(2 * j + 1, 1)
            step(PAIRS - 2, 0, more_text=False)
            step(PAIRS - 1, 1, last=True)
            split_x2(PAIRS - 1, 1)

        @block.vector
        def _(dve):
            own = Own(dve, setup_v)
            for b in range(8):
                own.did(dve.memset(bank[b][:, :], 0.0))
            own.did(dve.memset(hn[:, :, :, :], 0.0))
            dve.wait_ge(w_in, 16 * N_W)
            own.did(dve.tensor_tensor(tokbt[:, 1:2], tokbt[:, 1:2], posb[:, 0:1], ALU.add))
            own.did(dve.tensor_scalar(posb[:, 1:1 + PATCHES], posb[:, 1:1 + PATCHES], tokbt[:, 0:1], None, ALU.add))
            own.wait()
            own.did(dve.tensor_copy(hT[:, :, :, 0:1].rearrange("p s i o -> p (s i) o"),
                                    tokbt[:, 1:2].rearrange("p (o t) -> p o t", t=1).to_broadcast([P, 4, 1])))
            dve.wait_ge(txt_in, 16 * 16)
            own.did(dve.tensor_copy(tsh[:, :, :], tshi[:, :, :]))
            own.wait()
            own.did(dve.scalar_tensor_tensor(out=hsh[:, 0, :], in0=tsh[:, 1, :], scalar=float(BASE),
                                             in1=tsh[:, 0, :], op0=ALU.mult, op1=ALU.add))
            for n in (1, 2):
                own.wait()
                own.did(dve.scalar_tensor_tensor(out=hsh[:, n, :], in0=tsh[:, n + 1, :],
                                                 scalar=float(pow(BASE, n + 1, VOCAB)),
                                                 in1=hsh[:, n - 1, :], op0=ALU.mult, op1=ALU.add))
            own.wait()
            own.did(dve.tensor_scalar(hq[:, :, :], hsh[:, :, :], 1.0 / VOCAB, None, ALU.mult))
            own.wait()
            own.did(dve.tensor_copy(hqi[:, :, :], hq[:, :, :]))
            own.wait()
            own.did(dve.tensor_copy(hq[:, :, :], hqi[:, :, :]))
            own.wait()
            own.did(dve.scalar_tensor_tensor(out=hsh[:, :, :], in0=hq[:, :, :], scalar=-float(VOCAB),
                                             in1=hsh[:, :, :], op0=ALU.mult, op1=ALU.add))
            own.wait()
            own.did(dve.tensor_scalar(hq[:, :, :], hsh[:, :, :], 0.0, float(VOCAB), ALU.is_lt, ALU.mult))
            own.wait()
            own.did(dve.tensor_tensor(hsh[:, :, :], hsh[:, :, :], hq[:, :, :], ALU.add))
            own.wait()
            own.did(dve.tensor_scalar(hq[:, :, :], hsh[:, :, :], float(VOCAB), float(VOCAB), ALU.is_ge, ALU.mult))
            own.wait()
            dve.tensor_tensor(hashes[:, :, :], hsh[:, :, :], hq[:, :, :], ALU.subtract).then_inc(hashed, 1)

            def assemble(n, parity, early=False):
                dve.wait_ge(tok_done, n + 1)
                if not early:
                    dve.wait_ge(tr1_done, n - 1)
                dve.tensor_tensor(hT[:, parity, :, 1:1 + PATCHES],
                                  tokb_bank[:, 0:PAIR_PATCHES].rearrange("p (i n) -> p i n", i=2),
                                  posb[:, 1:1 + PATCHES].rearrange("p (o n) -> p o n", o=1)
                                  .to_broadcast([P, 2, PATCHES]), ALU.add).then_inc(hT_ready, 1)

            def norm_stats(k, src, stats, mv, sem, done):
                settle(dve)
                for c in range(4):
                    dve.bn_stats(stats[:, c, :], src(c)).then_inc(sem, 1)
                dve.wait_ge(sem, 4 * k + 4)
                settle(dve)
                for c in range(4):
                    last = dve.bn_aggr(mv[:, c, :], stats[:, c, :])
                last.then_inc(done, 1)

            def front(n, parity, early=False):
                dve.wait_ge(hn_ready, n + 1)
                if not (isinstance(n, int) and n == 0):
                    dve.wait_ge(tr2_done, n)
                norm_stats(n, lambda c: hn[:, parity, c, :], stats, mv, bn_front, mv_ready)
                dve.wait_ge(scl_ready, n + 1)
                if not early:
                    dve.wait_ge(hx_ready, n - 1)
                for c in range(4):
                    dve.tensor_scalar(xa[:, parity, c, :], hn[:, parity, c, :], mv[:, c, 0:1], rstd[:, 0, c:c + 1],
                                      ALU.subtract, ALU.mult)
                for c in range(4):
                    last = dve.tensor_scalar(xn[:, c, :], hn[:, parity, c, :], mv[:, c, 0:1], scl[:, c:c + 1],
                                             ALU.subtract, ALU.mult)
                last.then_inc(xn_ready, 1)

            def scores(i, img):
                dve.wait_ge(qk_done, 2 * i + img + 1)
                dve.tensor_tensor(sc[:, img], av_bank[img][:, 0:PAIR_SEQ].rearrange("p (c n) -> p c n", c=2),
                                  rel[:, :, :], ALU.add).then_inc(t_done, 1)
                dve.wait_ge(t_done, 2 * i + img + 1)
                if not (isinstance(i, int) and i == 0):
                    dve.wait_ge(av_done, 2 * i + img - 1)
                dve.scalar_tensor_tensor(out=kern[:, img], in0=sc[:, img], scalar=0.0, in1=sc[:, img],
                                         op0=ALU.max, op1=ALU.mult).then_inc(kern_ready, 1)

            def gate(i, img):
                dve.wait_ge(av_done, 2 * i + img + 1)
                dve.wait_ge(sil, 5 * i + 3)
                if not (isinstance(i, int) and i == 0):
                    dve.wait_ge(o_done, i)
                dve.scalar_tensor_tensor(out=uav[:, img], in0=av_bank[img][:, 0:PAIR_SEQ].rearrange("p (e n) -> p e n", e=2),
                                         scalar=1.0 / HID, in1=uT[:, :, img * SEQ:(img + 1) * SEQ],
                                         op0=ALU.mult, op1=ALU.mult).then_inc(uav_ready, 1)

            def middle(i, parity, early=False):
                dve.wait_ge(o_done, i + 1)
                dve.wait_ge(hx_ready, i + 1)
                dve.tensor_tensor(acc[:, bass.ds(4 * i, 4), :], o_bank[:, :].rearrange("p (c d) -> p c d", c=4),
                                  hx[:, :, :], ALU.add).then_inc(mid_ready, 1)
                dve.wait_ge(mid_ready, i + 1)
                norm_stats(i, lambda c: acc[:, bass.ds(4 * i + c, 1), :], stats2, mv2, bn_mid, mv2_ready)
                dve.wait_ge(rstd2_ready, i + 1)
                if not early:
                    dve.wait_ge(row_ready, i - 1)
                    dve.wait_ge(tr3_done, i - 1)
                for c in range(4):
                    last = dve.tensor_scalar(x2f[:, parity, c, :], acc[:, bass.ds(4 * i + c, 1), :], mv2[:, c, 0:1],
                                             rstd2[:, c:c + 1], ALU.subtract, ALU.mult)
                last.then_inc(x2_ready, 1)

            def top(b):
                dve.wait_ge(lg_done, b + 1)
                if not (isinstance(b, int) and b == 0):
                    dve.wait_ge(top_kept, 2 * b)
                dve.tensor_tensor(lgs[:, :, :], o_bank[:, 0:4 * EXPERTS].rearrange("p (c e) -> p c e", c=4),
                                  gateb[:, :].rearrange("p (o e) -> p o e", o=1).to_broadcast([P, 4, EXPERTS]),
                                  ALU.add).then_inc(lg_read, 1)
                dve.wait_ge(lg_read, b + 1)
                settle(dve)
                for c in range(4):
                    dve.max(mx8[:, c, :], lgs[:, c, :]).then_inc(top_ready, 1)
                dve.wait_ge(top_ready, 8 * b + 4)
                settle(dve)
                for c in range(4):
                    dve.max_index(mi8[:, c, :], mx8[:, c, :], lgs[:, c, :]).then_inc(top_ready, 1)

            def step(i, parity, first=False, last=False):
                early = isinstance(i, int) and i < 2
                if not last:
                    assemble(i + 1, 1 - parity, early=isinstance(i, int) and i < 1)
                scores(i, 0)
                scores(i, 1)
                if not first:
                    top(i - 1)
                if not last:
                    front(i + 1, 1 - parity, early=isinstance(i, int) and i < 1)
                gate(i, 0)
                gate(i, 1)
                middle(i, parity, early=early)

            own.wait()
            assemble(0, 0, early=True)
            front(0, 0, early=True)
            step(0, 0, first=True)
            step(1, 1)
            pair_loop(dve, step, 2, PAIRS - 2)
            step(PAIRS - 2, 0)
            step(PAIRS - 1, 1, last=True)
            top(PAIRS - 1)

        @block.scalar
        def _(act):
            act.wait_ge(w_in, 16 * N_W)
            act.wait_ge(setup_v, 9)

            def copy_text(grp):
                act.wait_ge(txt_done, grp + 1)
                if not (isinstance(grp, int) and grp == 0):
                    act.wait_ge(tr1_done, 2 * grp)
                act.activation(hT[:, :, :, 1 + PATCHES:SEQ],
                               tr1_bank[:, 0:P].rearrange("p (s i n) -> p s i n", s=2, i=2),
                               ACT.Copy).then_inc(txt_copied, 1)

            def copy_h(n, parity, early=False):
                act.wait_ge(tr1_done, n + 1)
                if not early:
                    act.wait_ge(hx_ready, n - 1)
                act.activation(hn[:, parity], tr1_bank[:, :].rearrange("p (c d) -> p c d", c=4),
                               ACT.Copy).then_inc(hn_ready, 1)

            def copy_xnT(n, parity, early=False):
                act.wait_ge(tr2_done, n + 1)
                if not early:
                    act.wait_ge(uv_done, 5 * n - 5)
                act.activation(xnT[:, parity, :], tr2_bank[:, 0:PAIR_SEQ], ACT.Copy).then_inc(xnT_ready, 1)

            def copy_x2T(b):
                act.wait_ge(tr3_done, b + 1)
                if not (isinstance(b, int) and b == 0):
                    act.wait_ge(t_ready, b)
                    act.wait_ge(lg_done, b)
                act.activation(x2T[:, :], tr2_bank[:, 0:PAIR_SEQ], ACT.Copy).then_inc(x2T_ready, 1)

            def uv(i, parity):
                later = not (isinstance(i, int) and i == 0)
                for r in range(5):
                    src = uv_bank[(parity + r) % 2]
                    act.wait_ge(uv_done, 5 * i + r + 1)
                    if r == 0:
                        if later:
                            act.wait_ge(qk_ready, 2 * i)
                        act.activation(base_s[:, :], src[:, 0:PAIR_SEQ], ACT.Silu).then_inc(sil, 1)
                        act.wait_ge(sil, 5 * i + 1)
                        if later:
                            act.wait_ge(qk_done, 2 * i)
                        for n in range(2):
                            act.activation(qk_sb[:, n, :], base_s[:, :], ACT.Identity, bias=gb[:, 2 + n:3 + n],
                                           scale=gb[:, n:n + 1]).then_inc(qk_ready, 1)
                    elif r < 3:
                        if later:
                            act.wait_ge(uav_ready, 2 * i)
                        act.activation(uT[:, r - 1, :], src[:, 0:PAIR_SEQ], ACT.Silu).then_inc(sil, 1)
                    else:
                        if later:
                            act.wait_ge(av_done, 2 * i)
                        act.activation(v_sb[:, r - 3], src[:, :].rearrange("p (c e) -> p c e", c=2),
                                       ACT.Silu).then_inc(sil, 1)

            def rows_hi(b, parity, early=False):
                act.wait_ge(x2_ready, b + 1)
                if not early:
                    act.wait_ge(r_out[parity], 8 * (b - parity))
                act.activation(x2r16[:, parity, :, 0, :], x2f[:, parity], ACT.Copy).then_inc(row_hi, 1)

            def columns_hi(b, parity, early=False):
                copy_x2T(b)
                act.wait_ge(x2T_ready, b + 1)
                if not early:
                    act.wait_ge(t_out[parity], 8 * (b - parity))
                act.activation(x2T16[:, parity, 0, :], x2T[:, :], ACT.Copy).then_inc(t_hi, 1)

            def weights_hi(i, parity):
                act.wait_ge(ws_in[parity], 8 * (i - parity) + 16)
                act.activation(w_hi[:, bass.ds(i * WBLOCK, WBLOCK)], wstage[:, parity, :], ACT.Copy).then_inc(ws_hi, 1)

            def step(i, parity, first=False, last=False, grp=None):
                early = isinstance(i, int) and i <= 2
                uv(i, parity)
                if not last and parity == 1:
                    copy_text((i + 1) // 2 if isinstance(i, int) else grp)
                if not first:
                    columns_hi(i - 1, 1 - parity, early)
                    rows_hi(i - 1, 1 - parity, early)
                weights_hi(i, parity)
                if not last:
                    copy_h(i + 1, 1 - parity, early=isinstance(i, int) and i < 1)
                    copy_xnT(i + 1, 1 - parity, early=isinstance(i, int) and i < 1)

            copy_text(0)
            copy_h(0, 0, early=True)
            copy_xnT(0, 0, early=True)
            step(0, 0, first=True)
            step(1, 1)
            step(2, 0)
            step(3, 1)
            with act.Fori(2, PAIRS // 2 - 1) as j:
                step(2 * j, 0)
                step(2 * j + 1, 1, grp=j + 1)
            step(PAIRS - 2, 0)
            step(PAIRS - 1, 1, last=True)
            columns_hi(PAIRS - 1, 1)
            rows_hi(PAIRS - 1, 1)

        @block.tensor
        def _(pe):
            def text(grp):
                pe.wait_ge(esum_ready, grp + 1)
                if not (isinstance(grp, int) and grp == 0):
                    pe.wait_ge(hn_ready, 2 * grp)
                pe.transpose(tr1_bank[:, 0:P], esum[:, :], ident[:, :]).then_inc(txt_done, 1)

            def patches(n, parity):
                pe.wait_ge(x_in[parity], 16 * (n - parity) + 32)
                if not (isinstance(n, int) and n == 0):
                    pe.wait_ge(hT_ready, n)
                for k in range(KN + 1):
                    rows = KP if k < KN else KREST
                    last = pe.matmul(tokb_bank[:, 0:PAIR_PATCHES], tokw[0:rows, k, :], xin[0:rows, parity, k, :],
                                     start=k == 0, stop=k == KN)
                last.then_inc(tok_done, 1)

            def to_rows(n, parity, grp):
                pe.wait_ge(hT_ready, n + 1)
                pe.wait_ge(txt_copied, grp + 1)
                if not (isinstance(n, int) and n == 0):
                    pe.wait_ge(hn_ready, n)
                for img in range(2):
                    for c, (at, rows) in enumerate(CHUNKS):
                        q = 2 * img + c
                        last = pe.transpose(tr1_bank[0:rows, q * HID:(q + 1) * HID],
                                            hT[:, parity, img, at:at + rows], ident[:, :])
                last.then_inc(tr1_done, 1)

            def to_columns(src, done):
                for img in range(2):
                    for c, (at, rows) in enumerate(CHUNKS):
                        last = pe.transpose(tr2_bank[:, img * SEQ + at:img * SEQ + at + rows],
                                            src[0:rows, 2 * img + c, :], ident[0:rows, 0:rows])
                last.then_inc(done, 1)

            def xn_columns(n, first=False):
                pe.wait_ge(xn_ready, n + 1)
                if not first:
                    pe.wait_ge(x2T_ready, n - 1)
                to_columns(xn, tr2_done)

            def x2_columns(b, parity):
                pe.wait_ge(x2_ready, b + 1)
                pe.wait_ge(xnT_ready, b + 2 if not (isinstance(b, int) and b == PAIRS - 1) else PAIRS)
                to_columns(x2f[:, parity], tr3_done)

            def logits(b):
                pe.wait_ge(x2T_ready, b + 1)
                pe.wait_ge(mid_ready, b + 1)
                for img in range(2):
                    for c, (at, rows) in enumerate(CHUNKS):
                        q = 2 * img + c
                        last = pe.matmul(o_bank[0:rows, q * EXPERTS:(q + 1) * EXPERTS],
                                         x2T[:, img * SEQ + at:img * SEQ + at + rows], gatew[:, :],
                                         start=True, stop=True)
                last.then_inc(lg_done, 1)

            def uv(i, parity, r):
                if not (isinstance(i, int) and i == 0 and r < 2):
                    pe.wait_ge(sil, 5 * i + r - 1)
                dst = uv_bank[(parity + r) % 2]
                if r == 0:
                    pe.wait_ge(xnT_ready, i + 1)
                if r < 3:
                    at = 2 * E_GAU if r == 0 else (r - 1) * P
                    pe.matmul(dst[:, 0:PAIR_SEQ], uvw[:, at:at + P], xnT[:, parity, :],
                              start=True, stop=True).then_inc(uv_done, 1)
                else:
                    for c, (at, rows) in enumerate(CHUNKS):
                        at += (r - 3) * SEQ
                        last = pe.matmul(dst[0:rows, c * E_GAU:(c + 1) * E_GAU], xnT[:, parity, at:at + rows],
                                         uvw[:, E_GAU:2 * E_GAU], start=True, stop=True)
                    last.then_inc(uv_done, 1)

            def qk(i, img):
                pe.wait_ge(qk_ready, 2 * i + 2)
                if not (isinstance(i, int) and i == 0):
                    pe.wait_ge(uav_ready, 2 * i + img - 1)
                for c, (at, rows) in enumerate(CHUNKS):
                    last = pe.matmul(av_bank[img][0:rows, c * SEQ:(c + 1) * SEQ],
                                     qk_sb[:, 1, img * SEQ + at:img * SEQ + at + rows],
                                     qk_sb[:, 0, img * SEQ:(img + 1) * SEQ], start=True, stop=True)
                last.then_inc(qk_done, 1)

            def av(i, img):
                pe.wait_ge(kern_ready, 2 * i + img + 1)
                pe.wait_ge(sil, 5 * i + 5)
                for e in range(2):
                    for c, (at, rows) in enumerate(CHUNKS):
                        last = pe.matmul(av_bank[img][:, e * SEQ:(e + 1) * SEQ],
                                         v_sb[0:rows, img, c, e * P:(e + 1) * P], kern[0:rows, img, c, :],
                                         start=c == 0, stop=c == 1)
                last.then_inc(av_done, 1)

            def project(i, img, first=False):
                pe.wait_ge(uav_ready, 2 * i + img + 1)
                if img == 0 and not first:
                    pe.wait_ge(lg_read, i)
                for c, (at, rows) in enumerate(CHUNKS):
                    q = 2 * img + c
                    for e in range(2):
                        last = pe.matmul(o_bank[0:rows, q * HID:(q + 1) * HID], uav[:, img, e, at:at + rows],
                                         ow[:, e, :], start=e == 0, stop=e == 1)
                if img == 1:
                    last.then_inc(o_done, 1)

            def step(i, parity, first=False, last=False, grp=None):
                if isinstance(i, int):
                    grp = (i + 1) // 2
                for r in range(5):
                    uv(i, parity, r)
                if not last:
                    if parity == 1:
                        text(grp)
                    patches(i + 1, 1 - parity)
                if not first:
                    x2_columns(i - 1, 1 - parity)
                qk(i, 0)
                qk(i, 1)
                if not first:
                    logits(i - 1)
                if not last:
                    to_rows(i + 1, 1 - parity, grp)
                av(i, 0)
                av(i, 1)
                project(i, 0, first)
                if not last:
                    xn_columns(i + 1, first)
                project(i, 1)

            pe.wait_ge(w_in, 16 * N_W)
            pe.wait_ge(tables, 1)
            pe.wait_ge(setup_v, 9)
            text(0)
            patches(0, 0)
            to_rows(0, 0, 0)
            xn_columns(0, first=True)
            step(0, 0, first=True)
            step(1, 1)
            with pe.Fori(1, PAIRS // 2 - 1) as j:
                step(2 * j, 0, grp=j)
                step(2 * j + 1, 1, grp=j + 1)
            step(PAIRS - 2, 0)
            step(PAIRS - 1, 1, last=True)
            x2_columns(PAIRS - 1, 1)
            logits(PAIRS - 1)


def route(nc, bank, top8, top_i, cw, cw01, slot_u, tile_e, tile_ei):
    with ExitStack() as ctx:
        def sb(name, shape, dt=FP32):
            return ctx.enter_context(nc.sbuf_tensor(name, shape, dt))

        def sem(name):
            return ctx.enter_context(nc.semaphore(name))

        expd = sb("expd", [P, NCH, 8])
        esum = sb("esum_r", [P, NCH])
        expert_no = sb("expert_no", [P, EXPERTS])
        valid = sb("valid", [P, 2])
        hot = sb("hot", [P, 2, NCH, EXPERTS])
        both = sb("both", [P, NCH, EXPERTS])
        before = sb("before", [P, P])
        ones = sb("ones", [P, P])
        total = sb("total", [P, NCH, EXPERTS])
        upto = sb("upto", [P, NCH, EXPERTS])
        zeros = sb("zeros", [P, NCH])
        tiles_f = sb("tiles_f", [P, EXPERTS])
        tiles_i = sb("tiles_i", [P, EXPERTS], I32)
        ends = sb("ends", [P, EXPERTS])
        offset = sb("offset", [P, EXPERTS])
        place = sb("place", [P, NCH, EXPERTS])
        picked = sb("picked", [P, NCH, EXPERTS])
        slot_f = sb("slot_f", [P, NCH, 2])
        tile_no = sb("tile_no", [P, TILES])
        past = sb("past", [P, TILES, EXPERTS])

        set_up, ones_up, centred, exps, own_s, both_up, counted, routed = (
            sem("set_up"), sem("ones_up"), sem("centred"), sem("exps"), sem("own_s"), sem("both_up"),
            sem("counted"), sem("routed"))
        block = ctx.enter_context(nc.Block())
        HALF = NCH // 2

        def spread(ap, n):
            return ap.rearrange("p (o e) -> p o e", o=1).to_broadcast([P, n, EXPERTS])

        def repeat(ap, n):
            return ap.rearrange("p (c o) -> p c o", o=1).to_broadcast([P, n, EXPERTS])

        @block.gpsimd
        def _(pool):
            pool.iota(expert_no[:, :], pattern=[[1, EXPERTS]], base=0, channel_multiplier=0,
                      allow_small_or_imprecise_dtypes=True).then_inc(set_up, 1)
            pool.iota(tile_no[:, :], pattern=[[1, TILES]], base=0, channel_multiplier=0,
                      allow_small_or_imprecise_dtypes=True).then_inc(set_up, 1)
            pool.memset(ones[:, :], 1.0).then_inc(ones_up, 1)
            pool.memset(valid[:, :], 1.0).then_inc(ones_up, 1)
            pool.wait_ge(ones_up, 2)
            pool.affine_select(out=before[:, :], in_=ones[:, :], compare_op=ALU.is_gt, fill=0.0, base=0,
                               pattern=[[1, P]], channel_multiplier=-1).then_inc(set_up, 1)
            pool.affine_select(out=valid[:, :], in_=valid[:, :], compare_op=ALU.is_gt, fill=0.0,
                               base=CHUNKS[0][1], pattern=[[CHUNKS[1][1] - CHUNKS[0][1], 2]],
                               channel_multiplier=-1).then_inc(set_up, 1)

        @block.scalar
        def _(act):
            act.wait_ge(centred, 1)
            act.activation(expd[:, :, :], expd[:, :, :], ACT.Exp).then_inc(exps, 1)

        @block.tensor
        def _(pe):
            pe.wait_ge(set_up, 4)
            pe.wait_ge(both_up, 1)
            for n in range(2):
                rhs = both[:, n * HALF:(n + 1) * HALF, :].rearrange("p c e -> p (c e)")
                pe.matmul(bank[n][:, :], before[:, :], rhs, start=True, stop=True)
                last = pe.matmul(bank[2 + n][:, :], ones[:, :], rhs, start=True, stop=True)
            last.then_inc(counted, 1)

        @block.vector
        def _(dve):
            own = Own(dve, own_s)

            def step(instruction):
                own.did(instruction)
                own.wait()

            dve.tensor_tensor(expd[:, :, :], top8[:, :, :], top8[:, :, 0:1].to_broadcast([P, NCH, 8]),
                              ALU.subtract).then_inc(centred, 1)
            dve.wait_ge(set_up, 4)
            for k in range(2):
                own.did(dve.tensor_tensor(hot[:, k], spread(expert_no[:, :], NCH),
                                          repeat(top_i[:, :, k], NCH), ALU.is_equal))
            own.wait()
            for k in range(2):
                for c in range(2):
                    own.did(dve.tensor_scalar(hot[:, k, c:NCH:2, :], hot[:, k, c:NCH:2, :], valid[:, c:c + 1],
                                              None, ALU.mult))
            own.wait()
            dve.tensor_tensor(both[:, :, :], hot[:, 0], hot[:, 1], ALU.add).then_inc(both_up, 1)
            dve.wait_ge(exps, 1)
            step(dve.reduce_sum(esum[:, :], expd[:, :, :], axis=AXX))
            step(dve.reciprocal(esum[:, :], esum[:, :]))
            step(dve.tensor_tensor(cw01[:, :, :], expd[:, :, 0:2],
                                   esum[:, :].rearrange("p (c o) -> p c o", o=1).to_broadcast([P, NCH, 2]), ALU.mult))
            own.did(dve.memset(cw[:, :, EXPERTS:], 1.0))
            own.did(dve.tensor_tensor(cw[:, :, 0:EXPERTS], hot[:, 0], repeat(cw01[:, :, 0], NCH), ALU.mult))
            step(dve.tensor_tensor(picked[:, :, :], hot[:, 1], repeat(cw01[:, :, 1], NCH), ALU.mult))
            step(dve.tensor_tensor(cw[:, :, 0:EXPERTS], cw[:, :, 0:EXPERTS], picked[:, :, :], ALU.add))
            dve.wait_ge(counted, 1)
            own.did(dve.memset(zeros[:, :], 0.0))
            for n in range(2):
                own.did(dve.tensor_copy(total[:, n * HALF:(n + 1) * HALF, :],
                                        bank[2 + n][:, :].rearrange("p (c e) -> p c e", e=EXPERTS)))
            own.wait()
            for e in range(EXPERTS):
                own.did(dve.tensor_tensor_scan(upto[:, :, e], total[:, :, e], zeros[:, :], 0.0, ALU.add, ALU.add))
            own.wait()
            step(dve.tensor_scalar(tiles_i[:, :], upto[:, NCH - 1, :], float(TILE - 1), None, ALU.add))
            step(dve.tensor_scalar(tiles_i[:, :], tiles_i[:, :], TILE.bit_length() - 1, None, ALU.arith_shift_right))
            step(dve.tensor_copy(tiles_f[:, :], tiles_i[:, :]))
            step(dve.tensor_tensor_scan(ends[:, :], tiles_f[:, :], zeros[:, 0:EXPERTS], 0.0, ALU.add, ALU.add))
            step(dve.tensor_tensor(offset[:, :], ends[:, :], tiles_f[:, :], ALU.subtract))
            step(dve.tensor_scalar(offset[:, :], offset[:, :], float(TILE), None, ALU.mult))
            step(dve.tensor_tensor(upto[:, :, :], upto[:, :, :], total[:, :, :], ALU.subtract))
            step(dve.tensor_tensor(place[:, :, :], upto[:, :, :], spread(offset[:, :], NCH), ALU.add))
            for n in range(2):
                part = place[:, n * HALF:(n + 1) * HALF, :]
                own.did(dve.tensor_tensor(part, part, bank[n][:, :].rearrange("p (c e) -> p c e", e=EXPERTS), ALU.add))
            own.wait()
            for k in range(2):
                step(dve.tensor_tensor(picked[:, :, :], place[:, :, :], hot[:, k], ALU.mult))
                step(dve.reduce_sum(slot_f[:, :, k], picked[:, :, :], axis=AXX))
            own.did(dve.tensor_copy(slot_u[:, :, :], slot_f[:, :, :]))
            step(dve.tensor_tensor(past[:, :, :], repeat(tile_no[:, :], TILES), spread(ends[:, :], TILES), ALU.is_ge))
            step(dve.reduce_sum(tile_e[:, :], past[:, :, :], axis=AXX))
            step(dve.tensor_scalar(tile_e[:, :], tile_e[:, :], float(EXPERTS - 1), None, ALU.min))
            step(dve.tensor_copy(tile_ei[:, :], tile_e[:, :]))


def shared_ffn(nc, bank, acc, w_hi, w_lo, b1, b2, ident, top_i, token2, cw, slot_u,
               x2t_dram, x2r_dram, slots_dram):
    NG = SHARED * NF
    with ExitStack() as ctx:
        def sb(name, shape, dt=FP32):
            return ctx.enter_context(nc.sbuf_tensor(name, shape, dt))

        def sem(name):
            return ctx.enter_context(nc.semaphore(name))

        xT = sb("xT", [P, 2, 2, PAIR_SEQ], FP16)
        rows = sb("rows", [P, 2, 4, ROW])
        slot_now = sb("slot_now", [P, 2, 4, 2], U32)
        gel = sb("gel", [P, 2, PAIR_SEQ])
        hid = sb("hid", [P, 2, 2, NG, PAIR_SEQ], FP16)
        cw_now = sb("cw_now", [P, 4, ALL_EXPERTS])
        cwT = sb("cwT", [ALL_EXPERTS, 2, 4, P])

        up_bank, down_bank, cw_bank = bank[0:4], bank[4:6], bank[6]
        xt_in = [sem(f"xt_in{n}") for n in range(2)]
        rows_in = [sem(f"rows_in{n}") for n in range(2)]
        scattered = [sem(f"scattered{n}") for n in range(2)]
        cw_tr, cw_ready, up_done, down_done = sem("cw_tr"), sem("cw_ready"), sem("up_done"), sem("down_done")
        gel_ready, hid_hi, hid_ready, acc_done = sem("gel_ready"), sem("hid_hi"), sem("hid_ready"), sem("acc_done")
        idx_set, cw_set = sem("idx_set"), sem("cw_set")
        block = ctx.enter_context(nc.Block())

        @block.sync
        def _(sp):
            def step(i, parity, first=False):
                if not first:
                    sp.wait_ge(up_done, NG * (i - 1))
                sp.dma_start(xT[:, parity].bitcast(FP32).rearrange("p h n -> p (h n)"), x2t_dram[i]
                             ).then_inc(xt_in[parity], 16)
                if not first:
                    sp.wait_ge(scattered[parity], 64 * (i - parity))
                sp.dma_start(rows[:, parity, :, 0:HID], x2r_dram[i]).then_inc(rows_in[parity], 16)

            step(0, 0, first=True)
            step(1, 1, first=True)
            pair_loop(sp, step, 2, PAIRS)

        @block.gpsimd
        def _(pool):
            def step(i, parity, first=False):
                if not (isinstance(i, int) and i == 0):
                    pool.wait_ge(cw_tr, i)
                    settle(pool)
                pool.tensor_copy(cw_now[:, :, :], cw[:, bass.ds(4 * i, 4), :]).then_inc(cw_set, 1)
                pool.wait_ge(rows_in[parity], 8 * (i - parity) + 16)
                settle(pool)
                pool.tensor_copy(rows[:, parity, :, HID:HID + 1],
                                 token2[:, bass.ds(4 * i, 4)].rearrange("p (c o) -> p c o", o=1)).then_inc(idx_set, 1)
                pool.tensor_copy(rows[:, parity, :, HID + 1:], top_i[:, bass.ds(4 * i, 4), 0:1]).then_inc(idx_set, 1)
                pool.tensor_copy(slot_now[:, parity], slot_u[:, bass.ds(4 * i, 4), :]).then_inc(idx_set, 1)
                pool.wait_ge(idx_set, 3 * (i + 1))
                settle(pool)
                for c in range(4):
                    n = CHUNKS[c % 2][1]
                    for k in range(2):
                        pool.indirect_dma_start(
                            out=slots_dram, in_=rows[0:n, parity, c, :], in_offset=None,
                            out_offset=bass.IndirectOffsetOnAxis(ap=slot_now[0:n, parity, c, k:k + 1], axis=0)
                        ).then_inc(scattered[parity], 16)

            step(0, 0, first=True)
            step(1, 1, first=True)
            pair_loop(pool, step, 2, PAIRS)
            for parity in range(2):
                pool.wait_ge(scattered[parity], 64 * PAIRS)

        @block.scalar
        def _(act):
            def step(i, parity, first=False):
                act.wait_ge(cw_tr, i + 1)
                if not first:
                    act.wait_ge(down_done, 2 * i - 2)
                act.activation(cwT[:, parity], cw_bank[0:ALL_EXPERTS, :].rearrange("p (c n) -> p c n", c=4),
                               ACT.Copy).then_inc(cw_ready, 1)
                for f in range(NG):
                    act.wait_ge(up_done, NG * i + f + 1)
                    if not (isinstance(i, int) and i == 0 and f < 2):
                        act.wait_ge(hid_ready, NG * i + f - 1)
                    act.activation(gel[:, f % 2, :], up_bank[f % 4][:, 0:PAIR_SEQ], ACT.Gelu,
                                   bias=b1[:, f:f + 1]).then_inc(gel_ready, 1)

            step(0, 0, first=True)
            step(1, 1, first=True)
            pair_loop(act, step, 2, PAIRS)

        @block.vector
        def _(dve):
            def split(i, parity, f, first):
                dve.wait_ge(gel_ready, NG * i + f + 1)
                if not first and f == 0:
                    dve.wait_ge(down_done, 2 * i - 2)
                dve.tensor_copy(hid[:, parity, 0, f, :], gel[:, f % 2, :]).then_inc(hid_hi, 1)
                dve.wait_ge(hid_hi, NG * i + f + 1)
                dve.tensor_tensor(hid[:, parity, 1, f, :], gel[:, f % 2, :], hid[:, parity, 0, f, :],
                                  ALU.subtract).then_inc(hid_ready, 1)

            def accumulate(i, img):
                dve.wait_ge(down_done, 2 * i + img + 1)
                part = acc[:, bass.ds(4 * i + 2 * img, 2), :]
                dve.tensor_tensor(part, part, down_bank[img][:, 0:2 * HID].rearrange("p (c d) -> p c d", c=2),
                                  ALU.add).then_inc(acc_done, 1)

            def step(i, parity, first=False, lead=False):
                for f in range(NG):
                    split(i, parity, f, first)
                    if not lead and f == 4:
                        accumulate(i - 1, 0)
                if not lead:
                    accumulate(i - 1, 1)

            step(0, 0, first=True, lead=True)
            step(1, 1, first=True)
            pair_loop(dve, step, 2, PAIRS)
            accumulate(PAIRS - 1, 0)
            accumulate(PAIRS - 1, 1)

        @block.tensor
        def _(pe):
            def up(i, parity, f):
                if f == 0:
                    pe.wait_ge(xt_in[parity], 8 * (i - parity) + 16)
                if not (isinstance(i, int) and i == 0 and f < 4):
                    pe.wait_ge(gel_ready, NG * i + f - 3)
                dst = up_bank[f % 4][:, 0:PAIR_SEQ]
                w = slice(f * P, (f + 1) * P)
                pe.matmul(dst, w_hi[:, w], xT[:, parity, 0, :], start=True, stop=False)
                pe.matmul(dst, w_hi[:, w], xT[:, parity, 1, :], start=False, stop=False)
                pe.matmul(dst, w_lo[:, w], xT[:, parity, 0, :], start=False, stop=True).then_inc(up_done, 1)

            def down(i, parity, c, first):
                img, (at, n) = c // 2, CHUNKS[c % 2]
                at += img * SEQ
                if c == 0:
                    pe.wait_ge(hid_ready, NG * (i + 1))
                    pe.wait_ge(cw_ready, i + 1)
                if c % 2 == 0 and not (isinstance(i, int) and i == 0):
                    pe.wait_ge(acc_done, 2 * i + img - 1)
                dst = down_bank[img][0:n, (c % 2) * HID:(c % 2 + 1) * HID]
                pe.matmul(dst, cwT[:, parity, c, 0:n], b2[:, :], start=True, stop=False)
                for f in range(NG):
                    w = slice(W2_AT + f * P, W2_AT + (f + 1) * P)
                    hi, lo = hid[:, parity, 0, f, at:at + n], hid[:, parity, 1, f, at:at + n]
                    pe.matmul(dst, hi, w_hi[:, w], start=False, stop=False)
                    pe.matmul(dst, hi, w_lo[:, w], start=False, stop=False)
                    last = pe.matmul(dst, lo, w_hi[:, w], start=False, stop=f == NG - 1)
                if c % 2 == 1:
                    last.then_inc(down_done, 1)

            def weights_columns(i):
                pe.wait_ge(cw_set, i + 1)
                if not (isinstance(i, int) and i == 0):
                    pe.wait_ge(cw_ready, i)
                for c in range(4):
                    last = pe.matmul(cw_bank[0:ALL_EXPERTS, c * P:(c + 1) * P],
                                     cw_now[:, c, :], ident[:, :], start=True, stop=True)
                last.then_inc(cw_tr, 1)

            def step(i, parity, first=False, lead=False):
                weights_columns(i)
                for f in range(NG):
                    up(i, parity, f)
                    if not lead and f % 2 == 1:
                        down(i - 1, 1 - parity, f // 2, first)

            step(0, 0, first=True, lead=True)
            step(1, 1, first=True)
            pair_loop(pe, step, 2, PAIRS)
            for c in range(4):
                down(PAIRS - 1, 1, c, False)


def routed_ffn(nc, bank, w_hi, w_lo, b1, ident, tile_e, tile_ei, slots_dram, y_dram):
    with ExitStack() as ctx:
        def sb(name, shape, dt=FP32):
            return ctx.enter_context(nc.sbuf_tensor(name, shape, dt))

        def sem(name):
            return ctx.enter_context(nc.semaphore(name))

        identh = sb("identh", [P, P], FP16)
        rows = sb("rows_r", [P, 2, TILE_CH, ROW])
        xT = sb("xT_r", [P, 2, 2, TILE], FP16)
        gel = sb("gel_r", [P, NF, TILE])
        hid = sb("hid_r", [P, 2, 2, NF, TILE], FP16)
        y_sb = sb("y_sb", [P, 2, TILE_CH, HID])
        y_row = sb("y_row", [P, 2, TILE_CH], U32)

        tr_bank = [ctx_bank[:, :].bitcast(FP16) for ctx_bank in (bank[6], bank[7])]
        up_bank, down_bank = (bank[0:2], bank[2:4]), bank[4:6]
        ident_up = sem("ident_up")
        rows_in = [sem(f"rrows_in{n}") for n in range(2)]
        y_out = [sem(f"y_out{n}") for n in range(2)]
        x_tr, x_ready, up_done, down_done = sem("x_tr"), sem("x_ready"), sem("rup_done"), sem("rdown_done")
        gel_ready, hid_hi, hid_ready = sem("rgel_ready"), sem("rhid_hi"), sem("rhid_ready")
        y_ready, row_set = sem("y_ready"), sem("row_set")
        block = ctx.enter_context(nc.Block())
        slot_v = slots_dram.rearrange("(t c p) w -> t p c w", p=P, c=TILE_CH)

        def tiles(eng, step, lo, hi):
            with eng.Fori(lo // 2, hi // 2) as j:
                for parity in range(2):
                    step(2 * j + parity, parity)

        @block.sync
        def _(sp):
            def step(t, parity, first=False):
                if not first:
                    sp.wait_ge(x_tr, t - 1)
                    sp.wait_ge(row_set, t - 1)
                sp.dma_start(rows[:, parity], slot_v[t]).then_inc(rows_in[parity], 16)

            step(0, 0, first=True)
            step(1, 1, first=True)
            tiles(sp, step, 2, TILES)

        @block.gpsimd
        def _(pool):
            def step(t, parity, first=False):
                pool.wait_ge(y_ready, t + 1)
                pool.wait_ge(row_set, t + 1)
                settle(pool)
                for c in range(TILE_CH):
                    pool.indirect_dma_start(
                        out=y_dram, in_=y_sb[:, parity, c, :], in_offset=None,
                        out_offset=bass.IndirectOffsetOnAxis(ap=y_row[:, parity, c:c + 1], axis=0),
                        bounds_check=2 * TOKENS - 1, oob_is_err=False).then_inc(y_out[parity], 16)

            step(0, 0)
            step(1, 1)
            tiles(pool, step, 2, TILES)
            for parity in range(2):
                pool.wait_ge(y_out[parity], 8 * TILE_CH * TILES)

        @block.scalar
        def _(act):
            act.activation(identh[:, :], ident[:, :], ACT.Copy).then_inc(ident_up, 1)

            def up(t, parity):
                e = act.value_load(tile_ei[0:1, bass.ds(t, 1)], min_val=0, max_val=EXPERTS - 1)
                for f in range(NF):
                    if f % 2 == 0:
                        act.wait_ge(up_done, 2 * t + f // 2 + 1)
                        if not (isinstance(t, int) and t == 0):
                            act.wait_ge(hid_ready, 2 * t - 1 + f // 2)
                    act.activation(gel[:, f, :], up_bank[parity][f // 2][:, (f % 2) * TILE:(f % 2 + 1) * TILE],
                                   ACT.Gelu, bias=b1[:, bass.ds((e + SHARED) * NF + f, 1)]).then_inc(gel_ready, 1)

            def out_y(t, parity, first=False):
                act.wait_ge(down_done, t + 1)
                if not first:
                    act.wait_ge(y_out[parity], 8 * TILE_CH * (t - parity))
                act.activation(y_sb[:, parity], down_bank[parity][:, 0:TILE_CH * HID].rearrange("p (c d) -> p c d", c=TILE_CH),
                               ACT.Copy).then_inc(y_ready, 1)

            def step(t, parity, lead=False, early=False):
                up(t, parity)
                if not lead:
                    out_y(t - 1, 1 - parity, early)

            step(0, 0, lead=True)
            step(1, 1, early=True)
            step(2, 0, early=True)
            step(3, 1)
            tiles(act, step, 4, TILES)
            out_y(TILES - 1, 1)

        @block.vector
        def _(dve):
            def columns(t, parity, first=False):
                dve.wait_ge(x_tr, t + 1)
                if not first:
                    dve.wait_ge(up_done, 2 * (t - 1))
                dve.tensor_copy(xT[:, parity].rearrange("p h n -> p (h n)"),
                                tr_bank[parity][:, 0:2 * TILE]).then_inc(x_ready, 1)

            def y_rows(t, parity, first=False):
                dve.wait_ge(rows_in[parity], 8 * (t - parity) + 16)
                if not first:
                    dve.wait_ge(y_out[parity], 8 * TILE_CH * (t - parity))
                dve.scalar_tensor_tensor(out=y_row[:, parity, :], in0=rows[:, parity, :, HID + 1],
                                         scalar=tile_e[:, bass.ds(t, 1)], in1=rows[:, parity, :, HID],
                                         op0=ALU.not_equal, op1=ALU.add).then_inc(row_set, 1)

            def split(t, parity, half, first=False):
                f = slice(2 * half, 2 * half + 2)
                dve.wait_ge(gel_ready, NF * t + 2 * half + 2)
                if not first:
                    dve.wait_ge(down_done, t - 1)
                dve.tensor_copy(hid[:, parity, 0, f, :], gel[:, f, :]).then_inc(hid_hi, 1)
                dve.wait_ge(hid_hi, 2 * t + half + 1)
                dve.tensor_tensor(hid[:, parity, 1, f, :], gel[:, f, :], hid[:, parity, 0, f, :],
                                  ALU.subtract).then_inc(hid_ready, 1)

            def step(t, parity, first=False, last=False):
                if not last:
                    columns(t + 1, 1 - parity, first=isinstance(t, int) and t < 1)
                split(t, parity, 0, first)
                if not last:
                    y_rows(t + 1, 1 - parity, first=isinstance(t, int) and t < 1)
                split(t, parity, 1, first)

            columns(0, 0, first=True)
            y_rows(0, 0, first=True)
            step(0, 0, first=True)
            step(1, 1, first=True)
            tiles(dve, step, 2, TILES - 2)
            step(TILES - 2, 0)
            step(TILES - 1, 1, last=True)

        @block.tensor
        def _(pe):
            def transposes(t, parity, first=False):
                pe.wait_ge(rows_in[parity], 8 * (t - parity) + 16)
                if not first:
                    pe.wait_ge(x_ready, t - 1)
                for h in range(2):
                    for c in range(TILE_CH):
                        x16 = rows[:, parity, c, h * HID // 2:(h + 1) * HID // 2].bitcast(FP16)
                        last = pe.transpose(tr_bank[parity][:, h * TILE + c * P:h * TILE + (c + 1) * P], x16, identh[:, :])
                last.then_inc(x_tr, 1)

            def up(t, parity, e, f, first=False):
                if f == 0:
                    pe.wait_ge(x_ready, t + 1)
                if f % 2 == 0 and not first:
                    pe.wait_ge(gel_ready, NF * (t - 2) + f + 2)
                dst = up_bank[parity][f // 2][:, (f % 2) * TILE:(f % 2 + 1) * TILE]
                hi = w_hi[:, bass.ds((e + SHARED) * F + f * P, P)]
                lo = w_lo[:, bass.ds((e + SHARED) * F + f * P, P)]
                pe.matmul(dst, hi, xT[:, parity, 0, :], start=True, stop=False)
                pe.matmul(dst, hi, xT[:, parity, 1, :], start=False, stop=False)
                last = pe.matmul(dst, lo, xT[:, parity, 0, :], start=False, stop=True)
                if f % 2 == 1:
                    last.then_inc(up_done, 1)

            def down(t, parity, e, first=False):
                pe.wait_ge(hid_ready, 2 * t + 2)
                if not first:
                    pe.wait_ge(y_ready, t - 1)
                for c in range(TILE_CH):
                    dst = down_bank[parity][:, c * HID:(c + 1) * HID]
                    for f in range(NF):
                        at = W2_AT + (e + SHARED) * F + f * P
                        w2_hi, w2_lo = w_hi[:, bass.ds(at, P)], w_lo[:, bass.ds(at, P)]
                        h_hi, h_lo = hid[:, parity, 0, f, c * P:(c + 1) * P], hid[:, parity, 1, f, c * P:(c + 1) * P]
                        pe.matmul(dst, h_hi, w2_hi, start=f == 0, stop=False)
                        pe.matmul(dst, h_hi, w2_lo, start=False, stop=False)
                        last = pe.matmul(dst, h_lo, w2_hi, start=False, stop=f == NF - 1)
                last.then_inc(down_done, 1)

            def expert(t):
                return pe.value_load(tile_ei[0:1, bass.ds(t, 1)], min_val=0, max_val=EXPERTS - 1)

            def step(t, parity, first=False, lead=False, last=False):
                e = expert(t)
                for f in range(NF):
                    up(t, parity, e, f, first)
                    if f == 1 and not last:
                        transposes(t + 1, 1 - parity, first=isinstance(t, int) and t < 1)
                if not lead:
                    down(t - 1, 1 - parity, expert(t - 1), first=isinstance(t, int) and t < 3)

            pe.wait_ge(ident_up, 1)
            transposes(0, 0, first=True)
            step(0, 0, first=True, lead=True)
            step(1, 1, first=True)
            step(2, 0)
            step(3, 1)
            tiles(pe, step, 4, TILES - 2)
            step(TILES - 2, 0)
            step(TILES - 1, 1, last=True)
            down(TILES - 1, 1, expert(TILES - 1))


def combine(nc, acc, cw01, y_dram, out):
    with ExitStack() as ctx:
        def sem(name):
            return ctx.enter_context(nc.semaphore(name))

        y = ctx.enter_context(nc.sbuf_tensor("y", [P, 2, 4, 2, HID], FP32))
        y_in = [sem(f"y_in{n}") for n in range(2)]
        stored = [sem(f"stored{n}") for n in range(2)]
        part, ready, cleared = sem("part"), sem("ready"), sem("cleared")
        block = ctx.enter_context(nc.Block())
        y_v = y_dram.rearrange("(b i s k) d -> b s i k d", i=2, s=SEQ, k=2)
        out_v = out.rearrange("(b i) s d -> b s i d", i=2)

        @block.sync
        def _(sp):
            sp.wait_ge(cleared, 1)

            def step(i, parity, first=False):
                if not first:
                    sp.wait_ge(ready, i - 1)
                for c, (at, n) in enumerate(CHUNKS):
                    for img in range(2):
                        sp.dma_start(y[0:n, parity, 2 * img + c], y_v[i, at:at + n, img]).then_inc(y_in[parity], 16)

            step(0, 0, first=True)
            step(1, 1, first=True)
            pair_loop(sp, step, 2, PAIRS)

        @block.vector
        def _(dve):
            dve.memset(y[:, :, :, :, :], 0.0).then_inc(cleared, 1)

            def step(i, parity):
                dve.wait_ge(y_in[parity], 32 * (i - parity) + 64)
                for k in range(2):
                    for c in range(4):
                        row = acc[:, bass.ds(4 * i + c, 1), :]
                        last = dve.scalar_tensor_tensor(
                            out=row, in0=y[:, parity, c, k, :].rearrange("p (o d) -> p o d", o=1),
                            scalar=cw01[:, bass.ds(4 * i + c, 1), k:k + 1].rearrange("p o k -> p (o k)"),
                            in1=row, op0=ALU.mult, op1=ALU.add)
                    if k == 0:
                        last.then_inc(part, 1)
                        dve.wait_ge(part, i + 1)
                last.then_inc(ready, 1)

            pair_loop(dve, step, 0, PAIRS)

        @block.scalar
        def _(act):
            def step(i, parity):
                act.wait_ge(ready, i + 1)
                for c, (at, n) in enumerate(CHUNKS):
                    act.dma_start(out_v[i, at:at + n], acc[0:n, bass.ds(4 * i, 4), :].rearrange("p (i c) d -> p i c d", c=2)[:, :, c, :]
                                  ).then_inc(stored[parity], 16)

            pair_loop(act, step, 0, PAIRS)
            for parity in range(2):
                act.wait_ge(stored[parity], 16 * PAIRS)


def layouts(x, x_txt, L0_tok_W, L0_tok_b, L0_tok_token, L0_tok_pos, L0_txt_emb2, L0_txt_emb3,
            L0_txt_emb4, L0_attn_w, L0_attn_uv_w, L0_attn_o_w, L0_attn_gamma, L0_attn_beta,
            L0_attn_g, L0_attn_res_scale, L0_ffn_gate_w, L0_ffn_gate_b, L0_ffn_sw1, L0_ffn_sb1,
            L0_ffn_sw2, L0_ffn_sb2, L0_ffn_rw1, L0_ffn_rb1, L0_ffn_rw2, L0_ffn_rb2):
    side = SIDE // GRID
    cols = (np.asarray(x).reshape(PAIRS, 2, CHANNELS, GRID, side, GRID, side)
            .transpose(0, 2, 4, 6, 1, 3, 5).reshape(PAIRS, PATCH_DIM, PAIR_PATCHES))
    tokw = np.asarray(L0_tok_W).T
    w1 = np.concatenate([np.asarray(L0_ffn_sw1), np.asarray(L0_ffn_rw1)])
    w2 = np.concatenate([np.asarray(L0_ffn_sw2), np.asarray(L0_ffn_rw2)])
    b1 = np.concatenate([np.asarray(L0_ffn_sb1), np.asarray(L0_ffn_rb1)])
    arrays = {
        "xmain": cols[:, :KN * KP].reshape(PAIRS, KN, KP, PAIR_PATCHES).transpose(0, 2, 1, 3),
        "xrest": cols[:, KN * KP:],
        "tokw_main": tokw[:KN * KP].reshape(KN, KP, HID).transpose(1, 0, 2),
        "tokw_rest": tokw[KN * KP:],
        "txt": np.asarray(x_txt).reshape(16, 4, TEXT).transpose(1, 2, 0).reshape(P, 16),
        "tokb": np.asarray(L0_tok_b).reshape(P, 1),
        "token": np.asarray(L0_tok_token).reshape(P, 1),
        "pos": np.asarray(L0_tok_pos).T,
        "emb2": np.asarray(L0_txt_emb2),
        "emb3": np.asarray(L0_txt_emb3),
        "emb4": np.asarray(L0_txt_emb4),
        "w_rel": np.asarray(L0_attn_w)[SEQ - 1 + np.arange(SEQ)[:, None] - np.arange(SEQ)[None, :]],
        "uv_w": np.asarray(L0_attn_uv_w),
        "o_w": np.asarray(L0_attn_o_w).reshape(2, P, HID).transpose(1, 0, 2),
        "gamma": np.asarray(L0_attn_gamma).T,
        "beta": np.asarray(L0_attn_beta).T,
        "g": np.broadcast_to(np.asarray(L0_attn_g).reshape(1, 1), (P, 1)),
        "res": np.broadcast_to(np.asarray(L0_attn_res_scale), (P, HID)),
        "gate_w": np.asarray(L0_ffn_gate_w).T,
        "gate_b": np.broadcast_to(np.asarray(L0_ffn_gate_b), (P, EXPERTS)),
        "ffn_w": np.concatenate([w1.transpose(2, 0, 1).reshape(P, -1),
                                 w2.transpose(0, 2, 1).reshape(ALL_EXPERTS, NF, P, HID).transpose(2, 0, 1, 3)
                                 .reshape(P, -1)], axis=1),
        "ffn_b1": b1.reshape(ALL_EXPERTS * NF, P).T,
        "ffn_b2": np.concatenate([np.asarray(L0_ffn_rb2), np.asarray(L0_ffn_sb2)]),
    }
    return {name: np.ascontiguousarray(a) for name, a in arrays.items()}


def kernel(**inputs):
    import concourse.bacc as bacc
    from concourse.bass_utils import run_bass_kernel_spmd

    arrays = layouts(**inputs)
    nc = bacc.Bacc("TRN2", target_bir_lowering=False, num_devices=1)
    args = [nc.dram_tensor(f"in_{name}", a.shape, mybir.dt.from_np(a.dtype), kind="ExternalInput").ap()
            for name, a in arrays.items()]
    out = nc.dram_tensor("out", (IMGS, SEQ, HID), FP32, kind="ExternalOutput").ap()
    build(nc, *args, out)
    r = run_bass_kernel_spmd(nc, [{f"in_{name}": a for name, a in arrays.items()}], core_ids=[0])
    return r.results[0]["out"]
```

```python
from contextlib import ExitStack

import numpy as np

import concourse.bass as bass
from concourse import mybir

FP32 = mybir.dt.float32
FP16 = mybir.dt.float16
I32 = mybir.dt.int32
U32 = mybir.dt.uint32
ALU = mybir.AluOpType
ACT = mybir.ActivationFunctionType
AXX = mybir.AxisListType.X

P = 128
IMGS, CHANNELS, SIDE, GRID = 64, 3, 196, 14
PATCHES = GRID * GRID
PATCH_DIM = CHANNELS * (SIDE // GRID) ** 2
TEXT = 32
SEQ = 1 + PATCHES + TEXT
CHUNKS = ((0, 117), (117, 112))
assert CHUNKS[1][0] + CHUNKS[1][1] == SEQ
PAIRS = IMGS // 2
PAIR_SEQ = 2 * SEQ
PAIR_PATCHES = 2 * PATCHES
NCH = 2 * IMGS
KP, KN = 126, 4
KREST = PATCH_DIM - KP * KN
HID = 128
E_GAU = 256
VOCAB, BASE = 25000, 257
EXPERTS, SHARED, F = 8, 2, 512
NF = F // P
ALL_EXPERTS = EXPERTS + SHARED
WCOLS = 2 * ALL_EXPERTS * F
WBLOCK = WCOLS // PAIRS
W2_AT = ALL_EXPERTS * F
TOKENS = IMGS * SEQ
TILE = 256
TILE_CH = TILE // P
TILES = (2 * TOKENS + EXPERTS * (TILE - 1)) // TILE
WORDS = -(-TILES // 4)
ROW = HID + 2
FILL_ROWS = -(-TILES * TILE // (PAIRS * P)) * P
SLOT_ROWS = FILL_ROWS * PAIRS
UNUSED = float(1 << 20)
EPS = 1e-5


class Own:

    def __init__(self, eng, sem, start=0):
        self.eng, self.sem, self.n = eng, sem, start

    def did(self, instruction):
        instruction.then_inc(self.sem, 1)
        self.n = self.n + 1

    def wait(self):
        self.eng.wait_ge(self.sem, self.n)


def settle(eng):
    eng.nop(nofuse=True)


def pair_loop(eng, step, lo, hi):
    assert lo % 2 == 0 and hi % 2 == 0
    with eng.Fori(lo // 2, hi // 2) as j:
        for parity in range(2):
            step(2 * j + parity, parity)


def build(nc, xmain, xrest, tokw_main, tokw_rest, txt, tokb, token, pos, emb2, emb3, emb4,
          w_rel, uv_w, o_w, gamma, beta, g, res, gate_w, gate_b, ffn_w, ffn_b1, ffn_b2, out,
          stop=5, dbg=None):
    x2t_dram = nc.dram_tensor("x2t_dram", [PAIRS, P, PAIR_SEQ], FP32).ap()
    x2r_dram = nc.dram_tensor("x2r_dram", [PAIRS, P, 4, HID], FP32).ap()
    slots_dram = nc.dram_tensor("slots_dram", [SLOT_ROWS, ROW], FP32).ap()
    y_dram = nc.dram_tensor("y_dram", [2 * TOKENS, HID], FP32).ap()

    with ExitStack() as keep:
        def sbuf(name, shape, dt=FP32, ctx=keep):
            return ctx.enter_context(nc.sbuf_tensor(name, shape, dt))

        bank = [keep.enter_context(nc.psum_tensor(f"bank{b}", [P, 512], FP32)) for b in range(8)]
        acc = sbuf("acc", [P, NCH, HID])
        w_hi = sbuf("w_hi", [P, WCOLS], FP16)
        w_lo = sbuf("w_lo", [P, WCOLS], FP16)
        b1 = sbuf("b1", [P, ALL_EXPERTS * NF])
        b2 = sbuf("b2", [ALL_EXPERTS, HID])
        ident = sbuf("ident", [P, P])
        top8 = sbuf("top8", [P, NCH, 8])
        top_i = sbuf("top_i", [P, NCH, 2])
        token2 = sbuf("token2", [P, NCH])

        embed_and_attend(nc, bank, acc, w_hi, w_lo, b1, b2, ident, top8, top_i, token2,
                         xmain, xrest, tokw_main, tokw_rest, txt, tokb, token, pos, emb2, emb3,
                         emb4, w_rel, uv_w, o_w, gamma, beta, g, res, gate_w, gate_b, ffn_w,
                         ffn_b1, ffn_b2, x2t_dram, x2r_dram, slots_dram)
        if stop >= 2:
            cw = sbuf("cw", [P, NCH, ALL_EXPERTS])
            cw01 = sbuf("cw01", [P, NCH, 2])
            slot_u = sbuf("slot_u", [P, NCH, 2], U32)
            tile_e = sbuf("tile_e", [P, 2 + 4 * WORDS])
            experts_word = sbuf("experts_word", [P, WORDS], I32)
            route(nc, bank, top8, top_i, cw, cw01, slot_u, tile_e, experts_word)
        if stop >= 3:
            shared_ffn(nc, bank, acc, w_hi, w_lo, b1, b2, ident, top_i, token2, cw, slot_u,
                       x2t_dram, x2r_dram, slots_dram)
        if stop >= 4:
            routed_ffn(nc, bank, w_hi, w_lo, b1, ident, tile_e, experts_word, slots_dram, y_dram)
        if stop >= 5:
            combine(nc, acc, cw01, y_dram, out)
        if dbg is not None:
            dbg(nc, locals())


def embed_and_attend(nc, bank, acc, w_hi, w_lo, b1, b2, ident, top8, top_i, token2,
                     xmain, xrest, tokw_main, tokw_rest, txt, tokb, token, pos, emb2, emb3, emb4,
                     w_rel, uv_w, o_w, gamma, beta, g, res, gate_w, gate_b, ffn_w, ffn_b1, ffn_b2,
                     x2t_dram, x2r_dram, slots_dram):
    with ExitStack() as ctx:
        def sb(name, shape, dt=FP32):
            return ctx.enter_context(nc.sbuf_tensor(name, shape, dt))

        def sem(name):
            return ctx.enter_context(nc.semaphore(name))

        tokw = sb("tokw", [P, KN + 1, HID])
        uvw = sb("uvw", [P, 2 * E_GAU + HID])
        ow = sb("ow", [P, 2, HID])
        posb = sb("posb", [P, SEQ - TEXT])
        tokbt = sb("tokbt", [P, 2])
        gb = sb("gb", [P, 4])
        gs = sb("gs", [P, 1])
        resb = sb("resb", [P, HID])
        gatew = sb("gatew", [P, EXPERTS])
        gateb = sb("gateb", [P, EXPERTS])
        rel = sb("rel", [P, 2, SEQ])
        tsh = sb("tsh", [P, 4, 16])
        tshi = sb("tshi", [P, 4, 16], I32)
        hsh = sb("hsh", [P, 3, 16])
        hq = sb("hq", [P, 3, 16])
        hqi = sb("hqi", [P, 3, 16], I32)
        hashes = sb("hashes", [P, 3, 16], U32)
        hash_now = sb("hash_now", [P, 3], U32)
        emb = sb("emb", [P, 3, HID])
        esum = sb("esum", [P, HID])
        xin = sb("xin", [P, 2, KN + 1, PAIR_PATCHES])
        wstage = sb("wstage", [P, 2, WBLOCK])
        hT = sb("hT", [P, 2, 2, SEQ])
        hn = sb("hn", [P, 2, 4, HID])
        stats = sb("stats", [P, 4, 6])
        mv = sb("mv", [P, 4, 2])
        var2 = sb("var2", [P, 2, 4])
        powers = sb("powers", [P, 3, 4])
        rstd = sb("rstd", [P, 2, 4])
        nrm = sb("nrm", [P, 4])
        scl = sb("scl", [P, 4])
        xa = sb("xa", [P, 2, 4, HID])
        xn = sb("xn", [P, 4, HID])
        xnT = sb("xnT", [P, 2, PAIR_SEQ])
        base_s = sb("base_s", [P, PAIR_SEQ])
        qk_sb = sb("qk_sb", [P, 2, PAIR_SEQ])
        uT = sb("uT", [P, 2, PAIR_SEQ])
        v_sb = sb("v_sb", [P, 2, 2, E_GAU])
        sc = sb("sc", [P, 2, 2, SEQ])
        kern = sb("kern", [P, 2, 2, SEQ])
        uav = sb("uav", [P, 2, 2, SEQ])
        hx = sb("hx", [P, 4, HID])
        stats2 = sb("stats2", [P, 4, 6])
        mv2 = sb("mv2", [P, 4, 2])
        rstd2 = sb("rstd2", [P, 4])
        x2f = sb("x2f", [P, 2, 4, HID])
        x2T = sb("x2T", [P, PAIR_SEQ])
        x2T16 = sb("x2T16", [P, 2, 2, PAIR_SEQ], FP16)
        x2r16 = sb("x2r16", [P, 2, 4, 2, HID], FP16)
        lgs = sb("lgs", [P, 4, EXPERTS])
        mx8 = sb("mx8", [P, 4, 8])
        mi8 = sb("mi8", [P, 4, 8], U32)
        fill = sb("fill", [P, FILL_ROWS // P, ROW])

        tokb_bank, tr1_bank, tr2_bank, o_bank = bank[0], bank[1], bank[2], bank[7]
        uv_bank, av_bank = bank[3:5], bank[5:7]

        w_in = sem("w_in")
        w_late = sem("w_late")
        txt_in = sem("txt_in")
        x_in = [sem(f"x_in{n}") for n in range(2)]
        ws_in = [sem(f"ws_in{n}") for n in range(2)]
        emb_in = sem("emb_in")
        t_out = [sem(f"t_out{n}") for n in range(2)]
        r_out = [sem(f"r_out{n}") for n in range(2)]
        fill_out = sem("fill_out")
        zeroed = sem("zeroed")
        tables = sem("tables")
        const_p = sem("const_p")
        hashed = sem("hashed")
        setup_v = sem("setup_v")
        tok_done, tr1_done, tr2_done, txt_done = sem("tok_done"), sem("tr1_done"), sem("tr2_done"), sem("txt_done")
        uv_done, qk_done, av_done, o_done = sem("uv_done"), sem("qk_done"), sem("av_done"), sem("o_done")
        tr3_done, lg_done = sem("tr3_done"), sem("lg_done")
        hT_ready, xn_ready, t_done, kern_ready = sem("hT_ready"), sem("xn_ready"), sem("t_done"), sem("kern_ready")
        uav_ready, mid_ready, x2_ready, lg_read = sem("uav_ready"), sem("mid_ready"), sem("x2_ready"), sem("lg_read")
        top_ready = sem("top_ready")
        bn_front, bn_mid, mv_ready, mv2_ready = sem("bn_front"), sem("bn_mid"), sem("mv_ready"), sem("mv2_ready")
        txt_copied, hn_ready, xnT_ready, sil, qk_ready, x2T_ready = (
            sem("txt_copied"), sem("hn_ready"), sem("xnT_ready"), sem("sil"), sem("qk_ready"), sem("x2T_ready"))
        base_ready = sem("base_ready")
        hash_set, esum1, esum_ready = sem("hash_set"), sem("esum1"), sem("esum_ready")
        hx1, hx_ready, row_hi, row_ready, t_hi, t_ready = (
            sem("hx1"), sem("hx_ready"), sem("row_hi"), sem("row_ready"), sem("t_hi"), sem("t_ready"))
        scl_own, scl_ready, rstd2_own, rstd2_ready = sem("scl_own"), sem("scl_ready"), sem("rstd2_own"), sem("rstd2_ready")
        ws_hi, ws_done, top_kept = sem("ws_hi"), sem("ws_done"), sem("top_kept")

        block = ctx.enter_context(nc.Block())
        N_W, N_LATE = 15, 5

        @block.sync
        def _(sp):
            for k in range(4):
                sp.wait_ge(zeroed, 2)
                for q in range(P // TEXT):
                    sp.dma_start(tshi[q * TEXT + k:(q + 1) * TEXT, k, :],
                                 txt[q * TEXT:(q + 1) * TEXT - k, :]).then_inc(txt_in, 16)

            def load_x(i, parity):
                sp.dma_start(xin[0:KP, parity, 0:KN, :], xmain[i]).then_inc(x_in[parity], 16)
                sp.dma_start(xin[0:KREST, parity, KN, :], xrest[i]).then_inc(x_in[parity], 16)

            def load_w(i, parity):
                sp.dma_start(wstage[:, parity, :], ffn_w[:, bass.ds(i * WBLOCK, WBLOCK)]).then_inc(ws_in[parity], 16)

            load_x(0, 0)
            for dst, src in ((tokw[0:KP, 0:KN, :], tokw_main), (tokw[0:KREST, KN, :], tokw_rest),
                             (posb[:, :], pos), (tokbt[:, 0:1], tokb), (tokbt[:, 1:2], token),
                             (uvw[:, :], uv_w), (gb[:, 0:2], gamma), (gb[:, 2:4], beta),
                             (gs[:, :], g), (resb[:, :], res), (gatew[:, :], gate_w),
                             (gateb[:, :], gate_b), (ow[:, :, :], o_w)):
                sp.dma_start(dst, src).then_inc(w_in, 16)
            for c, (at, n) in enumerate(CHUNKS):
                sp.dma_start(rel[0:n, c, :], w_rel[at:at + n, :]).then_inc(w_in, 16)
            load_x(1, 1)
            load_w(0, 0)
            load_w(1, 1)
            sp.dma_start(b1[:, :], ffn_b1).then_inc(w_late, 16)
            sp.dma_start(b2[:, :], ffn_b2).then_inc(w_late, 16)

            def store_x2(b, parity):
                sp.wait_ge(row_ready, b + 1)
                sp.dma_start(x2r_dram[b], x2r16[:, parity].bitcast(FP32).rearrange("p c h d -> p c (h d)")
                             ).then_inc(r_out[parity], 16)
                sp.wait_ge(t_ready, b + 1)
                sp.dma_start(x2t_dram[b], x2T16[:, parity].bitcast(FP32).rearrange("p h n -> p (h n)")
                             ).then_inc(t_out[parity], 16)

            def step(i, parity, first=False, last=False):
                sp.dma_start(slots_dram[bass.ds(i * FILL_ROWS, FILL_ROWS), :].rearrange("(t p) w -> p t w", p=P),
                             fill[:, :, :]).then_inc(fill_out, 16)
                if not last:
                    sp.wait_ge(tok_done, i + 1)
                    load_x(i + 2, parity)
                    sp.wait_ge(ws_done, i + 1)
                    load_w(i + 2, parity)
                if not first:
                    store_x2(i - 1, 1 - parity)

            sp.wait_ge(tables, 2)
            step(0, 0, first=True)
            step(1, 1)
            pair_loop(sp, step, 2, PAIRS - 2)
            step(PAIRS - 2, 0, last=True)
            step(PAIRS - 1, 1, last=True)
            store_x2(PAIRS - 1, 1)
            for parity in range(2):
                sp.wait_ge(r_out[parity], 16 * PAIRS // 2)
                sp.wait_ge(t_out[parity], 16 * PAIRS // 2)
            sp.wait_ge(fill_out, 16 * PAIRS)
            sp.wait_ge(w_late, 32)

        @block.gpsimd
        def _(pool):
            pool.memset(tshi[:, :, :], 0).then_inc(zeroed, 1)
            pool.memset(rel[:, :, :], 0.0).then_inc(zeroed, 1)
            pool.memset(ident[:, :], 0.0).then_inc(const_p, 1)
            pool.wait_ge(const_p, 1)
            pool.affine_select(out=ident[:, :], in_=ident[:, :], compare_op=ALU.not_equal, fill=1.0,
                               base=0, pattern=[[-1, P]], channel_multiplier=1).then_inc(tables, 1)
            pool.memset(fill[:, :, :], 0.0).then_inc(const_p, 1)
            for c, (at, _) in enumerate(CHUNKS):
                pool.iota(token2[:, c:NCH:2], pattern=[[2 * SEQ, IMGS]], base=2 * at, channel_multiplier=2,
                          allow_small_or_imprecise_dtypes=True).then_inc(const_p, 1)
            for n, power in enumerate((-0.5, 0.5, -1.0)):
                pool.memset(powers[:, n, :], power).then_inc(const_p, 1)
            pool.wait_ge(const_p, 7)
            pool.memset(fill[:, :, HID:HID + 1], UNUSED).then_inc(tables, 1)
            pool.wait_ge(hashed, 1)

            def gather_text(grp):
                if not (isinstance(grp, int) and grp == 0):
                    pool.wait_ge(esum_ready, grp)
                settle(pool)
                pool.tensor_copy(hash_now[:, :].rearrange("p (n o) -> p n o", o=1),
                                 hashes[:, :, bass.ds(grp, 1)]).then_inc(hash_set, 1)
                pool.wait_ge(hash_set, grp + 1)
                settle(pool)
                for n, table in enumerate((emb2, emb3, emb4)):
                    pool.indirect_dma_start(
                        out=emb[:, n, :], out_offset=None, in_=table,
                        in_offset=bass.IndirectOffsetOnAxis(ap=hash_now[:, n:n + 1], axis=0)).then_inc(emb_in, 16)

            def sum_text(grp):
                pool.wait_ge(emb_in, 48 * (grp + 1))
                if not (isinstance(grp, int) and grp == 0):
                    pool.wait_ge(txt_done, grp)
                pool.tensor_tensor(esum[:, :], emb[:, 0, :], emb[:, 1, :], ALU.add).then_inc(esum1, 1)
                pool.wait_ge(esum1, grp + 1)
                pool.tensor_tensor(esum[:, :], esum[:, :], emb[:, 2, :], ALU.add).then_inc(esum_ready, 1)

            def residual(i, parity):
                pool.wait_ge(xn_ready, i + 1)
                pool.wait_ge(hn_ready, i + 1)
                if not (isinstance(i, int) and i == 0):
                    pool.wait_ge(mid_ready, i)
                pool.tensor_tensor(hx[:, :, :], xa[:, parity], resb[:, :].rearrange("p (o d) -> p o d", o=1)
                                   .to_broadcast([P, 4, HID]), ALU.mult).then_inc(hx1, 1)
                pool.wait_ge(hx1, i + 1)
                pool.tensor_tensor(hx[:, :, :], hx[:, :, :], hn[:, parity], ALU.add).then_inc(hx_ready, 1)

            def split_w(i, parity):
                pool.wait_ge(ws_hi, i + 1)
                pool.tensor_tensor(w_lo[:, bass.ds(i * WBLOCK, WBLOCK)], wstage[:, parity, :],
                                   w_hi[:, bass.ds(i * WBLOCK, WBLOCK)], ALU.subtract).then_inc(ws_done, 1)

            def split_x2(b, parity):
                pool.wait_ge(row_hi, b + 1)
                pool.tensor_tensor(x2r16[:, parity, :, 1, :], x2f[:, parity], x2r16[:, parity, :, 0, :],
                                   ALU.subtract).then_inc(row_ready, 1)
                pool.wait_ge(t_hi, b + 1)
                pool.tensor_tensor(x2T16[:, parity, 1, :], x2T[:, :], x2T16[:, parity, 0, :],
                                   ALU.subtract).then_inc(t_ready, 1)
                pool.wait_ge(top_ready, 8 * (b + 1))
                settle(pool)
                pool.tensor_copy(top8[:, bass.ds(4 * b, 4), :], mx8[:, :, :]).then_inc(top_kept, 1)
                pool.tensor_copy(top_i[:, bass.ds(4 * b, 4), :], mi8[:, :, 0:2]).then_inc(top_kept, 1)

            def front_scales(n):
                own = Own(pool, scl_own, 6 * n)
                pool.wait_ge(mv_ready, n + 1)
                settle(pool)
                pool.tensor_scalar(var2[:, 0, :], mv[:, :, 1], EPS, None, ALU.add)
                own.did(pool.tensor_scalar(var2[:, 1, :], mv[:, :, 1], float(HID), None, ALU.mult))
                own.wait()
                own.did(pool.tensor_tensor(rstd[:, :, :], var2[:, :, :], powers[:, 0:2, :], ALU.pow))
                own.wait()
                own.did(pool.tensor_tensor(nrm[:, :], rstd[:, 0, :], rstd[:, 1, :], ALU.mult))
                own.wait()
                settle(pool)
                own.did(pool.tensor_scalar(nrm[:, :], nrm[:, :], EPS, None, ALU.max))
                own.wait()
                own.did(pool.tensor_tensor(nrm[:, :], nrm[:, :], powers[:, 2, :], ALU.pow))
                own.wait()
                settle(pool)
                own.did(pool.tensor_scalar(nrm[:, :], nrm[:, :], gs[:, 0:1], None, ALU.mult))
                own.wait()
                pool.tensor_tensor(scl[:, :], nrm[:, :], rstd[:, 0, :], ALU.mult).then_inc(scl_ready, 1)

            def mid_scales(i):
                pool.wait_ge(mv2_ready, i + 1)
                settle(pool)
                pool.tensor_scalar(rstd2[:, :], mv2[:, :, 1], EPS, None, ALU.add).then_inc(rstd2_own, 1)
                pool.wait_ge(rstd2_own, i + 1)
                pool.tensor_tensor(rstd2[:, :], rstd2[:, :], powers[:, 0, :], ALU.pow).then_inc(rstd2_ready, 1)

            def step(i, parity, first=False, last=False, more_text=True, grp=None):
                residual(i, parity)
                if more_text and parity == 0:
                    grp = i // 2 + 1 if isinstance(i, int) else grp
                    gather_text(grp)
                if not first:
                    split_x2(i - 1, 1 - parity)
                if not last:
                    front_scales(i + 1)
                    if more_text and parity == 0:
                        sum_text(grp)
                split_w(i, parity)
                mid_scales(i)

            gather_text(0)
            sum_text(0)
            pool.wait_ge(w_in, 16 * N_W)
            front_scales(0)
            step(0, 0, first=True)
            step(1, 1)
            with pool.Fori(1, PAIRS // 2 - 1) as j:
                step(2 * j, 0, grp=j + 1)
                step(2 * j + 1, 1)
            step(PAIRS - 2, 0, more_text=False)
            step(PAIRS - 1, 1, last=True)
            split_x2(PAIRS - 1, 1)

        @block.vector
        def _(dve):
            own = Own(dve, setup_v)
            for b in range(8):
                own.did(dve.memset(bank[b][:, :], 0.0))
            own.did(dve.memset(hn[:, :, :, :], 0.0))
            dve.wait_ge(w_in, 16 * N_W)
            own.did(dve.tensor_tensor(tokbt[:, 1:2], tokbt[:, 1:2], posb[:, 0:1], ALU.add))
            own.did(dve.tensor_scalar(posb[:, 1:1 + PATCHES], posb[:, 1:1 + PATCHES], tokbt[:, 0:1], None, ALU.add))
            own.wait()
            own.did(dve.tensor_copy(hT[:, :, :, 0:1].rearrange("p s i o -> p (s i) o"),
                                    tokbt[:, 1:2].rearrange("p (o t) -> p o t", t=1).to_broadcast([P, 4, 1])))
            dve.wait_ge(txt_in, 16 * 16)
            own.did(dve.tensor_copy(tsh[:, :, :], tshi[:, :, :]))
            own.wait()
            own.did(dve.scalar_tensor_tensor(out=hsh[:, 0, :], in0=tsh[:, 1, :], scalar=float(BASE),
                                             in1=tsh[:, 0, :], op0=ALU.mult, op1=ALU.add))
            for n in (1, 2):
                own.wait()
                own.did(dve.scalar_tensor_tensor(out=hsh[:, n, :], in0=tsh[:, n + 1, :],
                                                 scalar=float(pow(BASE, n + 1, VOCAB)),
                                                 in1=hsh[:, n - 1, :], op0=ALU.mult, op1=ALU.add))
            own.wait()
            own.did(dve.tensor_scalar(hq[:, :, :], hsh[:, :, :], 1.0 / VOCAB, None, ALU.mult))
            own.wait()
            own.did(dve.tensor_copy(hqi[:, :, :], hq[:, :, :]))
            own.wait()
            own.did(dve.tensor_copy(hq[:, :, :], hqi[:, :, :]))
            own.wait()
            own.did(dve.scalar_tensor_tensor(out=hsh[:, :, :], in0=hq[:, :, :], scalar=-float(VOCAB),
                                             in1=hsh[:, :, :], op0=ALU.mult, op1=ALU.add))
            own.wait()
            own.did(dve.tensor_scalar(hq[:, :, :], hsh[:, :, :], 0.0, float(VOCAB), ALU.is_lt, ALU.mult))
            own.wait()
            own.did(dve.tensor_tensor(hsh[:, :, :], hsh[:, :, :], hq[:, :, :], ALU.add))
            own.wait()
            own.did(dve.tensor_scalar(hq[:, :, :], hsh[:, :, :], float(VOCAB), float(VOCAB), ALU.is_ge, ALU.mult))
            own.wait()
            dve.tensor_tensor(hashes[:, :, :], hsh[:, :, :], hq[:, :, :], ALU.subtract).then_inc(hashed, 1)

            def assemble(n, parity, early=False):
                dve.wait_ge(tok_done, n + 1)
                if not early:
                    dve.wait_ge(tr1_done, n - 1)
                dve.tensor_tensor(hT[:, parity, :, 1:1 + PATCHES],
                                  tokb_bank[:, 0:PAIR_PATCHES].rearrange("p (i n) -> p i n", i=2),
                                  posb[:, 1:1 + PATCHES].rearrange("p (o n) -> p o n", o=1)
                                  .to_broadcast([P, 2, PATCHES]), ALU.add).then_inc(hT_ready, 1)

            def norm_stats(k, src, stats, mv, sem, done):
                settle(dve)
                for c in range(4):
                    dve.bn_stats(stats[:, c, :], src(c)).then_inc(sem, 1)
                dve.wait_ge(sem, 4 * k + 4)
                settle(dve)
                for c in range(4):
                    last = dve.bn_aggr(mv[:, c, :], stats[:, c, :])
                last.then_inc(done, 1)

            def front(n, parity, early=False):
                dve.wait_ge(hn_ready, n + 1)
                if not (isinstance(n, int) and n == 0):
                    dve.wait_ge(tr2_done, n)
                norm_stats(n, lambda c: hn[:, parity, c, :], stats, mv, bn_front, mv_ready)
                dve.wait_ge(scl_ready, n + 1)
                if not early:
                    dve.wait_ge(hx_ready, n - 1)
                for c in range(4):
                    dve.tensor_scalar(xa[:, parity, c, :], hn[:, parity, c, :], mv[:, c, 0:1], rstd[:, 0, c:c + 1],
                                      ALU.subtract, ALU.mult)
                for c in range(4):
                    last = dve.tensor_scalar(xn[:, c, :], hn[:, parity, c, :], mv[:, c, 0:1], scl[:, c:c + 1],
                                             ALU.subtract, ALU.mult)
                last.then_inc(xn_ready, 1)

            def scores(i, img):
                dve.wait_ge(qk_done, 2 * i + img + 1)
                dve.tensor_tensor(sc[:, img], av_bank[img][:, 0:PAIR_SEQ].rearrange("p (c n) -> p c n", c=2),
                                  rel[:, :, :], ALU.add).then_inc(t_done, 1)
                dve.wait_ge(t_done, 2 * i + img + 1)
                if not (isinstance(i, int) and i == 0):
                    dve.wait_ge(av_done, 2 * i + img - 1)
                dve.scalar_tensor_tensor(out=kern[:, img], in0=sc[:, img], scalar=0.0, in1=sc[:, img],
                                         op0=ALU.max, op1=ALU.mult).then_inc(kern_ready, 1)

            def gate(i, img):
                dve.wait_ge(av_done, 2 * i + img + 1)
                dve.wait_ge(sil, 5 * i + 3)
                if not (isinstance(i, int) and i == 0):
                    dve.wait_ge(o_done, i)
                dve.scalar_tensor_tensor(out=uav[:, img], in0=av_bank[img][:, 0:PAIR_SEQ].rearrange("p (e n) -> p e n", e=2),
                                         scalar=1.0 / HID, in1=uT[:, :, img * SEQ:(img + 1) * SEQ],
                                         op0=ALU.mult, op1=ALU.mult).then_inc(uav_ready, 1)

            def middle(i, parity, early=False):
                dve.wait_ge(o_done, i + 1)
                dve.wait_ge(hx_ready, i + 1)
                dve.tensor_tensor(acc[:, bass.ds(4 * i, 4), :], o_bank[:, :].rearrange("p (c d) -> p c d", c=4),
                                  hx[:, :, :], ALU.add).then_inc(mid_ready, 1)
                dve.wait_ge(mid_ready, i + 1)
                norm_stats(i, lambda c: acc[:, bass.ds(4 * i + c, 1), :], stats2, mv2, bn_mid, mv2_ready)
                dve.wait_ge(rstd2_ready, i + 1)
                if not early:
                    dve.wait_ge(row_ready, i - 1)
                    dve.wait_ge(tr3_done, i - 1)
                for c in range(4):
                    last = dve.tensor_scalar(x2f[:, parity, c, :], acc[:, bass.ds(4 * i + c, 1), :], mv2[:, c, 0:1],
                                             rstd2[:, c:c + 1], ALU.subtract, ALU.mult)
                last.then_inc(x2_ready, 1)

            def top(b):
                dve.wait_ge(lg_done, b + 1)
                if not (isinstance(b, int) and b == 0):
                    dve.wait_ge(top_kept, 2 * b)
                dve.tensor_tensor(lgs[:, :, :], o_bank[:, 0:4 * EXPERTS].rearrange("p (c e) -> p c e", c=4),
                                  gateb[:, :].rearrange("p (o e) -> p o e", o=1).to_broadcast([P, 4, EXPERTS]),
                                  ALU.add).then_inc(lg_read, 1)
                dve.wait_ge(lg_read, b + 1)
                settle(dve)
                for c in range(4):
                    dve.max(mx8[:, c, :], lgs[:, c, :]).then_inc(top_ready, 1)
                dve.wait_ge(top_ready, 8 * b + 4)
                settle(dve)
                for c in range(4):
                    dve.max_index(mi8[:, c, :], mx8[:, c, :], lgs[:, c, :]).then_inc(top_ready, 1)

            def step(i, parity, first=False, last=False):
                early = isinstance(i, int) and i < 2
                if not last:
                    assemble(i + 1, 1 - parity, early=isinstance(i, int) and i < 1)
                scores(i, 0)
                scores(i, 1)
                if not first:
                    top(i - 1)
                if not last:
                    front(i + 1, 1 - parity, early=isinstance(i, int) and i < 1)
                gate(i, 0)
                gate(i, 1)
                middle(i, parity, early=early)

            own.wait()
            assemble(0, 0, early=True)
            front(0, 0, early=True)
            step(0, 0, first=True)
            step(1, 1)
            pair_loop(dve, step, 2, PAIRS - 2)
            step(PAIRS - 2, 0)
            step(PAIRS - 1, 1, last=True)
            top(PAIRS - 1)

        @block.scalar
        def _(act):
            act.wait_ge(w_in, 16 * N_W)
            act.wait_ge(setup_v, 9)

            def copy_text(grp):
                act.wait_ge(txt_done, grp + 1)
                if not (isinstance(grp, int) and grp == 0):
                    act.wait_ge(tr1_done, 2 * grp)
                act.activation(hT[:, :, :, 1 + PATCHES:SEQ],
                               tr1_bank[:, 0:P].rearrange("p (s i n) -> p s i n", s=2, i=2),
                               ACT.Copy).then_inc(txt_copied, 1)

            def copy_h(n, parity, early=False):
                act.wait_ge(tr1_done, n + 1)
                if not early:
                    act.wait_ge(hx_ready, n - 1)
                act.activation(hn[:, parity], tr1_bank[:, :].rearrange("p (c d) -> p c d", c=4),
                               ACT.Copy).then_inc(hn_ready, 1)

            def copy_xnT(n, parity, early=False):
                act.wait_ge(tr2_done, n + 1)
                if not early:
                    act.wait_ge(uv_done, 5 * n - 5)
                act.activation(xnT[:, parity, :], tr2_bank[:, 0:PAIR_SEQ], ACT.Copy).then_inc(xnT_ready, 1)

            def copy_x2T(b):
                act.wait_ge(tr3_done, b + 1)
                if not (isinstance(b, int) and b == 0):
                    act.wait_ge(t_ready, b)
                    act.wait_ge(lg_done, b)
                act.activation(x2T[:, :], tr2_bank[:, 0:PAIR_SEQ], ACT.Copy).then_inc(x2T_ready, 1)

            def uv(i, parity):
                later = not (isinstance(i, int) and i == 0)
                for r in range(5):
                    src = uv_bank[(parity + r) % 2]
                    act.wait_ge(uv_done, 5 * i + r + 1)
                    if r == 0:
                        if later:
                            act.wait_ge(qk_ready, 2 * i)
                        act.activation(base_s[:, :], src[:, 0:PAIR_SEQ], ACT.Silu).then_inc(sil, 1)
                        act.wait_ge(sil, 5 * i + 1)
                        if later:
                            act.wait_ge(qk_done, 2 * i)
                        for n in range(2):
                            act.activation(qk_sb[:, n, :], base_s[:, :], ACT.Identity, bias=gb[:, 2 + n:3 + n],
                                           scale=gb[:, n:n + 1]).then_inc(qk_ready, 1)
                    elif r < 3:
                        if later:
                            act.wait_ge(uav_ready, 2 * i)
                        act.activation(uT[:, r - 1, :], src[:, 0:PAIR_SEQ], ACT.Silu).then_inc(sil, 1)
                    else:
                        if later:
                            act.wait_ge(av_done, 2 * i)
                        act.activation(v_sb[:, r - 3], src[:, :].rearrange("p (c e) -> p c e", c=2),
                                       ACT.Silu).then_inc(sil, 1)

            def rows_hi(b, parity, early=False):
                act.wait_ge(x2_ready, b + 1)
                if not early:
                    act.wait_ge(r_out[parity], 8 * (b - parity))
                act.activation(x2r16[:, parity, :, 0, :], x2f[:, parity], ACT.Copy).then_inc(row_hi, 1)

            def columns_hi(b, parity, early=False):
                copy_x2T(b)
                act.wait_ge(x2T_ready, b + 1)
                if not early:
                    act.wait_ge(t_out[parity], 8 * (b - parity))
                act.activation(x2T16[:, parity, 0, :], x2T[:, :], ACT.Copy).then_inc(t_hi, 1)

            def weights_hi(i, parity):
                act.wait_ge(ws_in[parity], 8 * (i - parity) + 16)
                act.activation(w_hi[:, bass.ds(i * WBLOCK, WBLOCK)], wstage[:, parity, :], ACT.Copy).then_inc(ws_hi, 1)

            def step(i, parity, first=False, last=False, grp=None):
                early = isinstance(i, int) and i <= 2
                uv(i, parity)
                if not last and parity == 1:
                    copy_text((i + 1) // 2 if isinstance(i, int) else grp)
                if not first:
                    columns_hi(i - 1, 1 - parity, early)
                    rows_hi(i - 1, 1 - parity, early)
                weights_hi(i, parity)
                if not last:
                    copy_h(i + 1, 1 - parity, early=isinstance(i, int) and i < 1)
                    copy_xnT(i + 1, 1 - parity, early=isinstance(i, int) and i < 1)

            copy_text(0)
            copy_h(0, 0, early=True)
            copy_xnT(0, 0, early=True)
            step(0, 0, first=True)
            step(1, 1)
            step(2, 0)
            step(3, 1)
            with act.Fori(2, PAIRS // 2 - 1) as j:
                step(2 * j, 0)
                step(2 * j + 1, 1, grp=j + 1)
            step(PAIRS - 2, 0)
            step(PAIRS - 1, 1, last=True)
            columns_hi(PAIRS - 1, 1)
            rows_hi(PAIRS - 1, 1)

        @block.tensor
        def _(pe):
            def text(grp):
                pe.wait_ge(esum_ready, grp + 1)
                if not (isinstance(grp, int) and grp == 0):
                    pe.wait_ge(hn_ready, 2 * grp)
                pe.transpose(tr1_bank[:, 0:P], esum[:, :], ident[:, :]).then_inc(txt_done, 1)

            def patches(n, parity):
                pe.wait_ge(x_in[parity], 16 * (n - parity) + 32)
                if not (isinstance(n, int) and n == 0):
                    pe.wait_ge(hT_ready, n)
                for k in range(KN + 1):
                    rows = KP if k < KN else KREST
                    last = pe.matmul(tokb_bank[:, 0:PAIR_PATCHES], tokw[0:rows, k, :], xin[0:rows, parity, k, :],
                                     start=k == 0, stop=k == KN)
                last.then_inc(tok_done, 1)

            def to_rows(n, parity, grp):
                pe.wait_ge(hT_ready, n + 1)
                pe.wait_ge(txt_copied, grp + 1)
                if not (isinstance(n, int) and n == 0):
                    pe.wait_ge(hn_ready, n)
                for img in range(2):
                    for c, (at, rows) in enumerate(CHUNKS):
                        q = 2 * img + c
                        last = pe.transpose(tr1_bank[0:rows, q * HID:(q + 1) * HID],
                                            hT[:, parity, img, at:at + rows], ident[:, :])
                last.then_inc(tr1_done, 1)

            def to_columns(src, done):
                for img in range(2):
                    for c, (at, rows) in enumerate(CHUNKS):
                        last = pe.transpose(tr2_bank[:, img * SEQ + at:img * SEQ + at + rows],
                                            src[0:rows, 2 * img + c, :], ident[0:rows, 0:rows])
                last.then_inc(done, 1)

            def xn_columns(n, first=False):
                pe.wait_ge(xn_ready, n + 1)
                if not first:
                    pe.wait_ge(x2T_ready, n - 1)
                to_columns(xn, tr2_done)

            def x2_columns(b, parity):
                pe.wait_ge(x2_ready, b + 1)
                pe.wait_ge(xnT_ready, b + 2 if not (isinstance(b, int) and b == PAIRS - 1) else PAIRS)
                to_columns(x2f[:, parity], tr3_done)

            def logits(b):
                pe.wait_ge(x2T_ready, b + 1)
                pe.wait_ge(mid_ready, b + 1)
                for img in range(2):
                    for c, (at, rows) in enumerate(CHUNKS):
                        q = 2 * img + c
                        last = pe.matmul(o_bank[0:rows, q * EXPERTS:(q + 1) * EXPERTS],
                                         x2T[:, img * SEQ + at:img * SEQ + at + rows], gatew[:, :],
                                         start=True, stop=True)
                last.then_inc(lg_done, 1)

            def uv(i, parity, r):
                if not (isinstance(i, int) and i == 0 and r < 2):
                    pe.wait_ge(sil, 5 * i + r - 1)
                dst = uv_bank[(parity + r) % 2]
                if r == 0:
                    pe.wait_ge(xnT_ready, i + 1)
                if r < 3:
                    at = 2 * E_GAU if r == 0 else (r - 1) * P
                    pe.matmul(dst[:, 0:PAIR_SEQ], uvw[:, at:at + P], xnT[:, parity, :],
                              start=True, stop=True).then_inc(uv_done, 1)
                else:
                    for c, (at, rows) in enumerate(CHUNKS):
                        at += (r - 3) * SEQ
                        last = pe.matmul(dst[0:rows, c * E_GAU:(c + 1) * E_GAU], xnT[:, parity, at:at + rows],
                                         uvw[:, E_GAU:2 * E_GAU], start=True, stop=True)
                    last.then_inc(uv_done, 1)

            def qk(i, img):
                pe.wait_ge(qk_ready, 2 * i + 2)
                if not (isinstance(i, int) and i == 0):
                    pe.wait_ge(uav_ready, 2 * i + img - 1)
                for c, (at, rows) in enumerate(CHUNKS):
                    last = pe.matmul(av_bank[img][0:rows, c * SEQ:(c + 1) * SEQ],
                                     qk_sb[:, 1, img * SEQ + at:img * SEQ + at + rows],
                                     qk_sb[:, 0, img * SEQ:(img + 1) * SEQ], start=True, stop=True)
                last.then_inc(qk_done, 1)

            def av(i, img):
                pe.wait_ge(kern_ready, 2 * i + img + 1)
                pe.wait_ge(sil, 5 * i + 5)
                for e in range(2):
                    for c, (at, rows) in enumerate(CHUNKS):
                        last = pe.matmul(av_bank[img][:, e * SEQ:(e + 1) * SEQ],
                                         v_sb[0:rows, img, c, e * P:(e + 1) * P], kern[0:rows, img, c, :],
                                         start=c == 0, stop=c == 1)
                last.then_inc(av_done, 1)

            def project(i, img, first=False):
                pe.wait_ge(uav_ready, 2 * i + img + 1)
                if img == 0 and not first:
                    pe.wait_ge(lg_read, i)
                for c, (at, rows) in enumerate(CHUNKS):
                    q = 2 * img + c
                    for e in range(2):
                        last = pe.matmul(o_bank[0:rows, q * HID:(q + 1) * HID], uav[:, img, e, at:at + rows],
                                         ow[:, e, :], start=e == 0, stop=e == 1)
                if img == 1:
                    last.then_inc(o_done, 1)

            def step(i, parity, first=False, last=False, grp=None):
                if isinstance(i, int):
                    grp = (i + 1) // 2
                for r in range(5):
                    uv(i, parity, r)
                if not last:
                    if parity == 1:
                        text(grp)
                    patches(i + 1, 1 - parity)
                if not first:
                    x2_columns(i - 1, 1 - parity)
                qk(i, 0)
                qk(i, 1)
                if not first:
                    logits(i - 1)
                if not last:
                    to_rows(i + 1, 1 - parity, grp)
                av(i, 0)
                av(i, 1)
                project(i, 0, first)
                if not last:
                    xn_columns(i + 1, first)
                project(i, 1)

            pe.wait_ge(w_in, 16 * N_W)
            pe.wait_ge(tables, 1)
            pe.wait_ge(setup_v, 9)
            text(0)
            patches(0, 0)
            to_rows(0, 0, 0)
            xn_columns(0, first=True)
            step(0, 0, first=True)
            step(1, 1)
            with pe.Fori(1, PAIRS // 2 - 1) as j:
                step(2 * j, 0, grp=j)
                step(2 * j + 1, 1, grp=j + 1)
            step(PAIRS - 2, 0)
            step(PAIRS - 1, 1, last=True)
            x2_columns(PAIRS - 1, 1)
            logits(PAIRS - 1)


def route(nc, bank, top8, top_i, cw, cw01, slot_u, tile_e, experts_word):
    with ExitStack() as ctx:
        def sb(name, shape, dt=FP32):
            return ctx.enter_context(nc.sbuf_tensor(name, shape, dt))

        def sem(name):
            return ctx.enter_context(nc.semaphore(name))

        expd = sb("expd", [P, NCH, 8])
        esum = sb("esum_r", [P, NCH])
        expert_no = sb("expert_no", [P, EXPERTS])
        valid = sb("valid", [P, 2])
        hot = sb("hot", [P, 2, NCH, EXPERTS])
        both = sb("both", [P, NCH, EXPERTS])
        before = sb("before", [P, P])
        ones = sb("ones", [P, P])
        total = sb("total", [P, NCH, EXPERTS])
        upto = sb("upto", [P, NCH, EXPERTS])
        zeros = sb("zeros", [P, NCH])
        tiles_f = sb("tiles_f", [P, EXPERTS])
        tiles_i = sb("tiles_i", [P, EXPERTS], I32)
        ends = sb("ends", [P, EXPERTS])
        offset = sb("offset", [P, EXPERTS])
        place = sb("place", [P, NCH, EXPERTS])
        picked = sb("picked", [P, NCH, EXPERTS])
        slot_f = sb("slot_f", [P, NCH, 2])
        tile_no = sb("tile_no", [P, TILES])
        past = sb("past", [P, TILES, EXPERTS])

        set_up, ones_up, centred, exps, own_s, both_up, counted, routed = (
            sem("set_up"), sem("ones_up"), sem("centred"), sem("exps"), sem("own_s"), sem("both_up"),
            sem("counted"), sem("routed"))
        block = ctx.enter_context(nc.Block())
        HALF = NCH // 2

        def spread(ap, n):
            return ap.rearrange("p (o e) -> p o e", o=1).to_broadcast([P, n, EXPERTS])

        def repeat(ap, n):
            return ap.rearrange("p (c o) -> p c o", o=1).to_broadcast([P, n, EXPERTS])

        @block.gpsimd
        def _(pool):
            pool.iota(expert_no[:, :], pattern=[[1, EXPERTS]], base=0, channel_multiplier=0,
                      allow_small_or_imprecise_dtypes=True).then_inc(set_up, 1)
            pool.iota(tile_no[:, :], pattern=[[1, TILES]], base=0, channel_multiplier=0,
                      allow_small_or_imprecise_dtypes=True).then_inc(set_up, 1)
            pool.memset(ones[:, :], 1.0).then_inc(ones_up, 1)
            pool.memset(valid[:, :], 1.0).then_inc(ones_up, 1)
            pool.wait_ge(ones_up, 2)
            pool.affine_select(out=before[:, :], in_=ones[:, :], compare_op=ALU.is_gt, fill=0.0, base=0,
                               pattern=[[1, P]], channel_multiplier=-1).then_inc(set_up, 1)
            pool.affine_select(out=valid[:, :], in_=valid[:, :], compare_op=ALU.is_gt, fill=0.0,
                               base=CHUNKS[0][1], pattern=[[CHUNKS[1][1] - CHUNKS[0][1], 2]],
                               channel_multiplier=-1).then_inc(set_up, 1)

        @block.scalar
        def _(act):
            act.wait_ge(centred, 1)
            act.activation(expd[:, :, :], expd[:, :, :], ACT.Exp).then_inc(exps, 1)

        @block.tensor
        def _(pe):
            pe.wait_ge(set_up, 4)
            pe.wait_ge(both_up, 1)
            for n in range(2):
                rhs = both[:, n * HALF:(n + 1) * HALF, :].rearrange("p c e -> p (c e)")
                pe.matmul(bank[n][:, :], before[:, :], rhs, start=True, stop=True)
                last = pe.matmul(bank[2 + n][:, :], ones[:, :], rhs, start=True, stop=True)
            last.then_inc(counted, 1)

        @block.vector
        def _(dve):
            own = Own(dve, own_s)

            def step(instruction):
                own.did(instruction)
                own.wait()

            dve.tensor_tensor(expd[:, :, :], top8[:, :, :], top8[:, :, 0:1].to_broadcast([P, NCH, 8]),
                              ALU.subtract).then_inc(centred, 1)
            dve.wait_ge(set_up, 4)
            for k in range(2):
                own.did(dve.tensor_tensor(hot[:, k], spread(expert_no[:, :], NCH),
                                          repeat(top_i[:, :, k], NCH), ALU.is_equal))
            own.wait()
            for k in range(2):
                for c in range(2):
                    own.did(dve.tensor_scalar(hot[:, k, c:NCH:2, :], hot[:, k, c:NCH:2, :], valid[:, c:c + 1],
                                              None, ALU.mult))
            own.wait()
            dve.tensor_tensor(both[:, :, :], hot[:, 0], hot[:, 1], ALU.add).then_inc(both_up, 1)
            dve.wait_ge(exps, 1)
            step(dve.reduce_sum(esum[:, :], expd[:, :, :], axis=AXX))
            step(dve.reciprocal(esum[:, :], esum[:, :]))
            step(dve.tensor_tensor(cw01[:, :, :], expd[:, :, 0:2],
                                   esum[:, :].rearrange("p (c o) -> p c o", o=1).to_broadcast([P, NCH, 2]), ALU.mult))
            own.did(dve.memset(cw[:, :, EXPERTS:], 1.0))
            own.did(dve.tensor_tensor(cw[:, :, 0:EXPERTS], hot[:, 0], repeat(cw01[:, :, 0], NCH), ALU.mult))
            step(dve.tensor_tensor(picked[:, :, :], hot[:, 1], repeat(cw01[:, :, 1], NCH), ALU.mult))
            step(dve.tensor_tensor(cw[:, :, 0:EXPERTS], cw[:, :, 0:EXPERTS], picked[:, :, :], ALU.add))
            dve.wait_ge(counted, 1)
            own.did(dve.memset(zeros[:, :], 0.0))
            for n in range(2):
                own.did(dve.tensor_copy(total[:, n * HALF:(n + 1) * HALF, :],
                                        bank[2 + n][:, :].rearrange("p (c e) -> p c e", e=EXPERTS)))
            own.wait()
            for e in range(EXPERTS):
                own.did(dve.tensor_tensor_scan(upto[:, :, e], total[:, :, e], zeros[:, :], 0.0, ALU.add, ALU.add))
            own.wait()
            step(dve.tensor_scalar(tiles_i[:, :], upto[:, NCH - 1, :], float(TILE - 1), None, ALU.add))
            step(dve.tensor_scalar(tiles_i[:, :], tiles_i[:, :], TILE.bit_length() - 1, None, ALU.arith_shift_right))
            step(dve.tensor_copy(tiles_f[:, :], tiles_i[:, :]))
            step(dve.tensor_tensor_scan(ends[:, :], tiles_f[:, :], zeros[:, 0:EXPERTS], 0.0, ALU.add, ALU.add))
            step(dve.tensor_tensor(offset[:, :], ends[:, :], tiles_f[:, :], ALU.subtract))
            step(dve.tensor_scalar(offset[:, :], offset[:, :], float(TILE), None, ALU.mult))
            step(dve.tensor_tensor(upto[:, :, :], upto[:, :, :], total[:, :, :], ALU.subtract))
            step(dve.tensor_tensor(place[:, :, :], upto[:, :, :], spread(offset[:, :], NCH), ALU.add))
            for n in range(2):
                part = place[:, n * HALF:(n + 1) * HALF, :]
                own.did(dve.tensor_tensor(part, part, bank[n][:, :].rearrange("p (c e) -> p c e", e=EXPERTS), ALU.add))
            own.wait()
            for k in range(2):
                step(dve.tensor_tensor(picked[:, :, :], place[:, :, :], hot[:, k], ALU.mult))
                step(dve.reduce_sum(slot_f[:, :, k], picked[:, :, :], axis=AXX))
            own.did(dve.tensor_copy(slot_u[:, :, :], slot_f[:, :, :]))
            step(dve.tensor_tensor(past[:, :, :], repeat(tile_no[:, :], TILES), spread(ends[:, :], TILES), ALU.is_ge))
            step(dve.memset(tile_e[:, :], 0.0))
            step(dve.reduce_sum(tile_e[:, 2:2 + TILES], past[:, :, :], axis=AXX))
            step(dve.tensor_scalar(tile_e[:, 2:2 + TILES], tile_e[:, 2:2 + TILES], float(EXPERTS - 1), None, ALU.min))
            word_f = tile_no[:, 0:WORDS]
            step(dve.tensor_copy(word_f, tile_e[:, 0:4 * WORDS:4]))
            for n in range(1, 6):
                step(dve.scalar_tensor_tensor(out=word_f, in0=tile_e[:, n:n + 4 * WORDS - 3:4], scalar=float(EXPERTS ** n),
                                              in1=word_f, op0=ALU.mult, op1=ALU.add))
            step(dve.tensor_copy(experts_word[:, :], word_f))


def shared_ffn(nc, bank, acc, w_hi, w_lo, b1, b2, ident, top_i, token2, cw, slot_u,
               x2t_dram, x2r_dram, slots_dram):
    NG = SHARED * NF
    with ExitStack() as ctx:
        def sb(name, shape, dt=FP32):
            return ctx.enter_context(nc.sbuf_tensor(name, shape, dt))

        def sem(name):
            return ctx.enter_context(nc.semaphore(name))

        xT = sb("xT", [P, 2, 2, PAIR_SEQ], FP16)
        rows = sb("rows", [P, 2, 4, ROW])
        slot_now = sb("slot_now", [P, 2, 4, 2], U32)
        gel = sb("gel", [P, 2, PAIR_SEQ])
        hid = sb("hid", [P, 2, 2, NG, PAIR_SEQ], FP16)
        cw_now = sb("cw_now", [P, 4, ALL_EXPERTS])
        cwT = sb("cwT", [ALL_EXPERTS, 2, 4, P])

        up_bank, down_bank, cw_bank = bank[0:4], bank[4:6], bank[6]
        xt_in = [sem(f"xt_in{n}") for n in range(2)]
        rows_in = [sem(f"rows_in{n}") for n in range(2)]
        scattered = [sem(f"scattered{n}") for n in range(2)]
        cw_tr, cw_ready, up_done, down_done = sem("cw_tr"), sem("cw_ready"), sem("up_done"), sem("down_done")
        gel_ready, hid_hi, hid_ready, acc_done = sem("gel_ready"), sem("hid_hi"), sem("hid_ready"), sem("acc_done")
        idx_set, cw_set = sem("idx_set"), sem("cw_set")
        block = ctx.enter_context(nc.Block())

        @block.sync
        def _(sp):
            def step(i, parity, first=False):
                if not first:
                    sp.wait_ge(up_done, NG * (i - 1))
                sp.dma_start(xT[:, parity].bitcast(FP32).rearrange("p h n -> p (h n)"), x2t_dram[i]
                             ).then_inc(xt_in[parity], 16)
                if not first:
                    sp.wait_ge(scattered[parity], 64 * (i - parity))
                sp.dma_start(rows[:, parity, :, 0:HID], x2r_dram[i]).then_inc(rows_in[parity], 16)

            step(0, 0, first=True)
            step(1, 1, first=True)
            pair_loop(sp, step, 2, PAIRS)

        @block.gpsimd
        def _(pool):
            def step(i, parity, first=False):
                if not (isinstance(i, int) and i == 0):
                    pool.wait_ge(cw_tr, i)
                    settle(pool)
                pool.tensor_copy(cw_now[:, :, :], cw[:, bass.ds(4 * i, 4), :]).then_inc(cw_set, 1)
                pool.wait_ge(rows_in[parity], 8 * (i - parity) + 16)
                settle(pool)
                pool.tensor_copy(rows[:, parity, :, HID:HID + 1],
                                 token2[:, bass.ds(4 * i, 4)].rearrange("p (c o) -> p c o", o=1)).then_inc(idx_set, 1)
                pool.tensor_copy(rows[:, parity, :, HID + 1:], top_i[:, bass.ds(4 * i, 4), 0:1]).then_inc(idx_set, 1)
                pool.tensor_copy(slot_now[:, parity], slot_u[:, bass.ds(4 * i, 4), :]).then_inc(idx_set, 1)
                pool.wait_ge(idx_set, 3 * (i + 1))
                settle(pool)
                for c in range(4):
                    n = CHUNKS[c % 2][1]
                    for k in range(2):
                        pool.indirect_dma_start(
                            out=slots_dram, in_=rows[0:n, parity, c, :], in_offset=None,
                            out_offset=bass.IndirectOffsetOnAxis(ap=slot_now[0:n, parity, c, k:k + 1], axis=0)
                        ).then_inc(scattered[parity], 16)

            step(0, 0, first=True)
            step(1, 1, first=True)
            pair_loop(pool, step, 2, PAIRS)
            for parity in range(2):
                pool.wait_ge(scattered[parity], 64 * PAIRS)

        @block.scalar
        def _(act):
            def step(i, parity, first=False):
                act.wait_ge(cw_tr, i + 1)
                if not first:
                    act.wait_ge(down_done, 2 * i - 2)
                act.activation(cwT[:, parity], cw_bank[0:ALL_EXPERTS, :].rearrange("p (c n) -> p c n", c=4),
                               ACT.Copy).then_inc(cw_ready, 1)
                for f in range(NG):
                    act.wait_ge(up_done, NG * i + f + 1)
                    if not (isinstance(i, int) and i == 0 and f < 2):
                        act.wait_ge(hid_ready, NG * i + f - 1)
                    act.activation(gel[:, f % 2, :], up_bank[f % 4][:, 0:PAIR_SEQ], ACT.Gelu,
                                   bias=b1[:, f:f + 1]).then_inc(gel_ready, 1)

            step(0, 0, first=True)
            step(1, 1, first=True)
            pair_loop(act, step, 2, PAIRS)

        @block.vector
        def _(dve):
            def split(i, parity, f, first):
                dve.wait_ge(gel_ready, NG * i + f + 1)
                if not first and f == 0:
                    dve.wait_ge(down_done, 2 * i - 2)
                dve.tensor_copy(hid[:, parity, 0, f, :], gel[:, f % 2, :]).then_inc(hid_hi, 1)
                dve.wait_ge(hid_hi, NG * i + f + 1)
                dve.tensor_tensor(hid[:, parity, 1, f, :], gel[:, f % 2, :], hid[:, parity, 0, f, :],
                                  ALU.subtract).then_inc(hid_ready, 1)

            def accumulate(i, img):
                dve.wait_ge(down_done, 2 * i + img + 1)
                part = acc[:, bass.ds(4 * i + 2 * img, 2), :]
                dve.tensor_tensor(part, part, down_bank[img][:, 0:2 * HID].rearrange("p (c d) -> p c d", c=2),
                                  ALU.add).then_inc(acc_done, 1)

            def step(i, parity, first=False, lead=False):
                for f in range(NG):
                    split(i, parity, f, first)
                    if not lead and f == 4:
                        accumulate(i - 1, 0)
                if not lead:
                    accumulate(i - 1, 1)

            step(0, 0, first=True, lead=True)
            step(1, 1, first=True)
            pair_loop(dve, step, 2, PAIRS)
            accumulate(PAIRS - 1, 0)
            accumulate(PAIRS - 1, 1)

        @block.tensor
        def _(pe):
            def up(i, parity, f):
                if f == 0:
                    pe.wait_ge(xt_in[parity], 8 * (i - parity) + 16)
                if not (isinstance(i, int) and i == 0 and f < 4):
                    pe.wait_ge(gel_ready, NG * i + f - 3)
                dst = up_bank[f % 4][:, 0:PAIR_SEQ]
                w = slice(f * P, (f + 1) * P)
                pe.matmul(dst, w_hi[:, w], xT[:, parity, 0, :], start=True, stop=False)
                pe.matmul(dst, w_hi[:, w], xT[:, parity, 1, :], start=False, stop=False)
                pe.matmul(dst, w_lo[:, w], xT[:, parity, 0, :], start=False, stop=True).then_inc(up_done, 1)

            def down(i, parity, c, first):
                img, (at, n) = c // 2, CHUNKS[c % 2]
                at += img * SEQ
                if c == 0:
                    pe.wait_ge(hid_ready, NG * (i + 1))
                    pe.wait_ge(cw_ready, i + 1)
                if c % 2 == 0 and not (isinstance(i, int) and i == 0):
                    pe.wait_ge(acc_done, 2 * i + img - 1)
                dst = down_bank[img][0:n, (c % 2) * HID:(c % 2 + 1) * HID]
                pe.matmul(dst, cwT[:, parity, c, 0:n], b2[:, :], start=True, stop=False)
                for f in range(NG):
                    w = slice(W2_AT + f * P, W2_AT + (f + 1) * P)
                    hi, lo = hid[:, parity, 0, f, at:at + n], hid[:, parity, 1, f, at:at + n]
                    pe.matmul(dst, hi, w_hi[:, w], start=False, stop=False)
                    pe.matmul(dst, hi, w_lo[:, w], start=False, stop=False)
                    last = pe.matmul(dst, lo, w_hi[:, w], start=False, stop=f == NG - 1)
                if c % 2 == 1:
                    last.then_inc(down_done, 1)

            def weights_columns(i):
                pe.wait_ge(cw_set, i + 1)
                if not (isinstance(i, int) and i == 0):
                    pe.wait_ge(cw_ready, i)
                for c in range(4):
                    last = pe.matmul(cw_bank[0:ALL_EXPERTS, c * P:(c + 1) * P],
                                     cw_now[:, c, :], ident[:, :], start=True, stop=True)
                last.then_inc(cw_tr, 1)

            def step(i, parity, first=False, lead=False):
                weights_columns(i)
                for f in range(NG):
                    up(i, parity, f)
                    if not lead and f % 2 == 1:
                        down(i - 1, 1 - parity, f // 2, first)

            step(0, 0, first=True, lead=True)
            step(1, 1, first=True)
            pair_loop(pe, step, 2, PAIRS)
            for c in range(4):
                down(PAIRS - 1, 1, c, False)


def routed_ffn(nc, bank, w_hi, w_lo, b1, ident, tile_e, experts_word, slots_dram, y_dram):
    LAG, AHEAD = 2, 2
    with ExitStack() as ctx:
        def sb(name, shape, dt=FP32):
            return ctx.enter_context(nc.sbuf_tensor(name, shape, dt))

        def sem(name):
            return ctx.enter_context(nc.semaphore(name))

        identh = sb("identh", [P, P], FP16)
        rows = sb("rows_r", [P, 4, TILE_CH, ROW])
        xT = sb("xT_r", [P, 4, 2, TILE], FP16)
        gel = sb("gel_r", [P, 2, NF, TILE])
        hid = sb("hid_r", [P, 4, 2, NF, TILE], FP16)
        y_sb = sb("y_sb", [P, 4, TILE_CH, HID])
        y_row = sb("y_row", [P, 4, TILE_CH], U32)

        tr_bank = [ctx_bank[:, :].bitcast(FP16) for ctx_bank in (bank[6], bank[7])]
        up_bank, down_bank = (bank[0:2], bank[2:4]), bank[4:6]
        ident_up = sem("ident_up")
        rows_in = [sem(f"rrows_in{n}") for n in range(4)]
        y_out = [sem(f"y_out{n}") for n in range(4)]
        x_tr, x_ready, up_done, down_done = sem("x_tr"), sem("x_ready"), sem("rup_done"), sem("rdown_done")
        gel_ready, hid_hi, hid_ready = sem("rgel_ready"), sem("rhid_hi"), sem("rhid_ready")
        y_ready, row_set = sem("y_ready"), sem("row_set")
        block = ctx.enter_context(nc.Block())
        slot_v = slots_dram.rearrange("(t c p) w -> t p c w", p=P, c=TILE_CH)

        def experts_of_four(eng, j):
            word = eng.value_load(experts_word[0:1, bass.ds(j, 1)], min_val=0, max_val=EXPERTS ** 6 - 1)
            return [eng.snap((word >> (3 * n)) & (EXPERTS - 1), min_val=0, max_val=EXPERTS - 1) for n in range(6)]

        def tiles(eng, step):
            whole = TILES // 4 * 4
            for t in range(4):
                step(t, t)
            with eng.Fori(1, whole // 4) as j:
                for slot in range(4):
                    step(4 * j + slot, slot)
            for t in range(whole, TILES):
                step(t, t % 4)

        def reaches(t, n):
            return not (isinstance(t, int) and t < n)

        @block.sync
        def _(sp):
            def step(t, slot):
                if reaches(t, 4):
                    sp.wait_ge(x_tr, t - 3)
                    sp.wait_ge(row_set, t - 3)
                sp.dma_start(rows[:, slot], slot_v[t]).then_inc(rows_in[slot], 16)

            tiles(sp, step)

        @block.gpsimd
        def _(pool):
            def step(t, slot):
                pool.wait_ge(row_set, t + 1)
                pool.wait_ge(y_ready, t + 1)
                settle(pool)
                for c in range(TILE_CH):
                    pool.indirect_dma_start(
                        out=y_dram, in_=y_sb[:, slot, c, :], in_offset=None,
                        out_offset=bass.IndirectOffsetOnAxis(ap=y_row[:, slot, c:c + 1], axis=0),
                        bounds_check=2 * TOKENS - 1, oob_is_err=False).then_inc(y_out[slot], 16)

            tiles(pool, step)
            for slot in range(4):
                pool.wait_ge(y_out[slot], 16 * TILE_CH * len(range(slot, TILES, 4)))

        @block.scalar
        def _(act):
            act.activation(identh[:, :], ident[:, :], ACT.Copy).then_inc(ident_up, 1)

            def columns(t, slot):
                act.wait_ge(x_tr, t + 1)
                if reaches(t, 4):
                    act.wait_ge(up_done, 2 * (t - 3))
                act.activation(xT[:, slot % 4].rearrange("p h n -> p (h n)"),
                               tr_bank[slot % 2][:, 0:2 * TILE], ACT.Copy).then_inc(x_ready, 1)

            def gelu(t, slot, e, half):
                act.wait_ge(up_done, 2 * t + half + 1)
                if reaches(t, 2):
                    act.wait_ge(hid_ready, 2 * t - 3 + half)
                for f in (2 * half, 2 * half + 1):
                    act.activation(gel[:, slot % 2, f, :], up_bank[slot % 2][half][:, (f % 2) * TILE:(f % 2 + 1) * TILE],
                                   ACT.Gelu, bias=b1[:, bass.ds((e + SHARED) * NF + f, 1)]).then_inc(gel_ready, 1)

            def step(t, slot):
                if slot == 0:
                    experts[:] = experts_of_four(act, t // 4)
                e = experts[slot + 2]
                gelu(t, slot, e, 0)
                gelu(t, slot, e, 1)
                if not (isinstance(t, int) and t + AHEAD >= TILES):
                    columns(t + AHEAD, (slot + AHEAD) % 4)

            experts = []
            for t in range(AHEAD):
                columns(t, t)
            tiles(act, step)

        @block.vector
        def _(dve):
            def y_rows(t, slot):
                dve.wait_ge(rows_in[slot], 4 * (t - slot) + 16)
                if reaches(t, 4):
                    dve.wait_ge(y_out[slot], 4 * TILE_CH * (t - slot))
                dve.scalar_tensor_tensor(out=y_row[:, slot, :], in0=rows[:, slot, :, HID + 1],
                                         scalar=tile_e[:, bass.ds(t + 2, 1)], in1=rows[:, slot, :, HID],
                                         op0=ALU.not_equal, op1=ALU.add).then_inc(row_set, 1)

            def split(t, slot, half):
                f = slice(2 * half, 2 * half + 2)
                dve.wait_ge(gel_ready, NF * t + 2 * half + 2)
                if reaches(t, 4) and half == 0:
                    dve.wait_ge(down_done, t - 3)
                dve.tensor_copy(hid[:, slot, 0, f, :], gel[:, slot % 2, f, :]).then_inc(hid_hi, 1)
                dve.wait_ge(hid_hi, 2 * t + half + 1)
                dve.tensor_tensor(hid[:, slot, 1, f, :], gel[:, slot % 2, f, :], hid[:, slot, 0, f, :],
                                  ALU.subtract).then_inc(hid_ready, 1)

            def out_y(t, slot):
                dve.wait_ge(down_done, t + 1)
                if reaches(t, 4):
                    dve.wait_ge(y_out[slot], 4 * TILE_CH * (t - slot))
                dve.tensor_copy(y_sb[:, slot], down_bank[slot % 2][:, 0:TILE_CH * HID].rearrange(
                    "p (c d) -> p c d", c=TILE_CH)).then_inc(y_ready, 1)

            def step(t, slot):
                split(t, slot, 0)
                if reaches(t, LAG + 1):
                    out_y(t - LAG - 1, (slot - LAG - 1) % 4)
                split(t, slot, 1)
                y_rows(t, slot)

            tiles(dve, step)
            for t in range(TILES - LAG - 1, TILES):
                out_y(t, t % 4)

        @block.tensor
        def _(pe):
            def transposes(t, slot):
                pe.wait_ge(rows_in[slot], 4 * (t - slot) + 16)
                if reaches(t, 2):
                    pe.wait_ge(x_ready, t - 1)
                for h in range(2):
                    for c in range(TILE_CH):
                        x16 = rows[:, slot, c, h * HID // 2:(h + 1) * HID // 2].bitcast(FP16)
                        last = pe.transpose(tr_bank[slot % 2][:, h * TILE + c * P:h * TILE + (c + 1) * P], x16, identh[:, :])
                last.then_inc(x_tr, 1)

            def up(t, slot, e, f):
                if f == 0:
                    pe.wait_ge(x_ready, t + 1)
                if f % 2 == 0 and reaches(t, 2):
                    pe.wait_ge(gel_ready, NF * (t - 2) + f + 2)
                dst = up_bank[slot % 2][f // 2][:, (f % 2) * TILE:(f % 2 + 1) * TILE]
                hi = w_hi[:, bass.ds((e + SHARED) * F + f * P, P)]
                lo = w_lo[:, bass.ds((e + SHARED) * F + f * P, P)]
                pe.matmul(dst, hi, xT[:, slot, 0, :], start=True, stop=False)
                pe.matmul(dst, hi, xT[:, slot, 1, :], start=False, stop=False)
                last = pe.matmul(dst, lo, xT[:, slot, 0, :], start=False, stop=True)
                if f % 2 == 1:
                    last.then_inc(up_done, 1)

            def down(t, slot, e):
                pe.wait_ge(hid_ready, 2 * t + 2)
                if reaches(t, 2):
                    pe.wait_ge(y_ready, t - 1)
                for c in range(TILE_CH):
                    dst = down_bank[slot % 2][:, c * HID:(c + 1) * HID]
                    for f in range(NF):
                        at = W2_AT + (e + SHARED) * F + f * P
                        w2_hi, w2_lo = w_hi[:, bass.ds(at, P)], w_lo[:, bass.ds(at, P)]
                        h_hi, h_lo = hid[:, slot, 0, f, c * P:(c + 1) * P], hid[:, slot, 1, f, c * P:(c + 1) * P]
                        pe.matmul(dst, h_hi, w2_hi, start=f == 0, stop=False)
                        pe.matmul(dst, h_hi, w2_lo, start=False, stop=False)
                        last = pe.matmul(dst, h_lo, w2_hi, start=False, stop=f == NF - 1)
                last.then_inc(down_done, 1)

            experts = []

            def step(t, slot):
                if slot == 0:
                    experts[:] = experts_of_four(pe, t // 4)
                e = experts[slot + 2]
                up(t, slot, e, 0)
                up(t, slot, e, 1)
                if not (isinstance(t, int) and t + AHEAD >= TILES):
                    transposes(t + AHEAD, (slot + AHEAD) % 4)
                up(t, slot, e, 2)
                up(t, slot, e, 3)
                if reaches(t, LAG):
                    down(t - LAG, (slot - LAG) % 4, experts[slot])

            pe.wait_ge(ident_up, 1)
            for t in range(AHEAD):
                transposes(t, t)
            tiles(pe, step)
            for t in range(TILES - LAG, TILES):
                down(t, t % 4, experts[t % 4 + 2])


def combine(nc, acc, cw01, y_dram, out):
    with ExitStack() as ctx:
        def sem(name):
            return ctx.enter_context(nc.semaphore(name))

        y = ctx.enter_context(nc.sbuf_tensor("y", [P, 2, 4, 2, HID], FP32))
        y_in = [sem(f"y_in{n}") for n in range(2)]
        stored = [sem(f"stored{n}") for n in range(2)]
        part, ready, cleared = sem("part"), sem("ready"), sem("cleared")
        block = ctx.enter_context(nc.Block())
        y_v = y_dram.rearrange("(b i s k) d -> b s i k d", i=2, s=SEQ, k=2)
        out_v = out.rearrange("(b i) s d -> b s i d", i=2)

        @block.sync
        def _(sp):
            sp.wait_ge(cleared, 1)

            def step(i, parity, first=False):
                if not first:
                    sp.wait_ge(ready, i - 1)
                for c, (at, n) in enumerate(CHUNKS):
                    for img in range(2):
                        sp.dma_start(y[0:n, parity, 2 * img + c], y_v[i, at:at + n, img]).then_inc(y_in[parity], 16)

            step(0, 0, first=True)
            step(1, 1, first=True)
            pair_loop(sp, step, 2, PAIRS)

        @block.vector
        def _(dve):
            dve.memset(y[:, :, :, :, :], 0.0).then_inc(cleared, 1)

            def step(i, parity):
                dve.wait_ge(y_in[parity], 32 * (i - parity) + 64)
                for k in range(2):
                    for c in range(4):
                        row = acc[:, bass.ds(4 * i + c, 1), :]
                        last = dve.scalar_tensor_tensor(
                            out=row, in0=y[:, parity, c, k, :].rearrange("p (o d) -> p o d", o=1),
                            scalar=cw01[:, bass.ds(4 * i + c, 1), k:k + 1].rearrange("p o k -> p (o k)"),
                            in1=row, op0=ALU.mult, op1=ALU.add)
                    if k == 0:
                        last.then_inc(part, 1)
                        dve.wait_ge(part, i + 1)
                last.then_inc(ready, 1)

            pair_loop(dve, step, 0, PAIRS)

        @block.scalar
        def _(act):
            def step(i, parity):
                act.wait_ge(ready, i + 1)
                for c, (at, n) in enumerate(CHUNKS):
                    act.dma_start(out_v[i, at:at + n], acc[0:n, bass.ds(4 * i, 4), :].rearrange("p (i c) d -> p i c d", c=2)[:, :, c, :]
                                  ).then_inc(stored[parity], 16)

            pair_loop(act, step, 0, PAIRS)
            for parity in range(2):
                act.wait_ge(stored[parity], 16 * PAIRS)


def layouts(x, x_txt, L0_tok_W, L0_tok_b, L0_tok_token, L0_tok_pos, L0_txt_emb2, L0_txt_emb3,
            L0_txt_emb4, L0_attn_w, L0_attn_uv_w, L0_attn_o_w, L0_attn_gamma, L0_attn_beta,
            L0_attn_g, L0_attn_res_scale, L0_ffn_gate_w, L0_ffn_gate_b, L0_ffn_sw1, L0_ffn_sb1,
            L0_ffn_sw2, L0_ffn_sb2, L0_ffn_rw1, L0_ffn_rb1, L0_ffn_rw2, L0_ffn_rb2):
    side = SIDE // GRID
    cols = (np.asarray(x).reshape(PAIRS, 2, CHANNELS, GRID, side, GRID, side)
            .transpose(0, 2, 4, 6, 1, 3, 5).reshape(PAIRS, PATCH_DIM, PAIR_PATCHES))
    tokw = np.asarray(L0_tok_W).T
    w1 = np.concatenate([np.asarray(L0_ffn_sw1), np.asarray(L0_ffn_rw1)])
    w2 = np.concatenate([np.asarray(L0_ffn_sw2), np.asarray(L0_ffn_rw2)])
    b1 = np.concatenate([np.asarray(L0_ffn_sb1), np.asarray(L0_ffn_rb1)])
    arrays = {
        "xmain": cols[:, :KN * KP].reshape(PAIRS, KN, KP, PAIR_PATCHES).transpose(0, 2, 1, 3),
        "xrest": cols[:, KN * KP:],
        "tokw_main": tokw[:KN * KP].reshape(KN, KP, HID).transpose(1, 0, 2),
        "tokw_rest": tokw[KN * KP:],
        "txt": np.asarray(x_txt).reshape(16, 4, TEXT).transpose(1, 2, 0).reshape(P, 16),
        "tokb": np.asarray(L0_tok_b).reshape(P, 1),
        "token": np.asarray(L0_tok_token).reshape(P, 1),
        "pos": np.asarray(L0_tok_pos).T,
        "emb2": np.asarray(L0_txt_emb2),
        "emb3": np.asarray(L0_txt_emb3),
        "emb4": np.asarray(L0_txt_emb4),
        "w_rel": np.asarray(L0_attn_w)[SEQ - 1 + np.arange(SEQ)[:, None] - np.arange(SEQ)[None, :]],
        "uv_w": np.asarray(L0_attn_uv_w),
        "o_w": np.asarray(L0_attn_o_w).reshape(2, P, HID).transpose(1, 0, 2),
        "gamma": np.asarray(L0_attn_gamma).T,
        "beta": np.asarray(L0_attn_beta).T,
        "g": np.broadcast_to(np.asarray(L0_attn_g).reshape(1, 1), (P, 1)),
        "res": np.broadcast_to(np.asarray(L0_attn_res_scale), (P, HID)),
        "gate_w": np.asarray(L0_ffn_gate_w).T,
        "gate_b": np.broadcast_to(np.asarray(L0_ffn_gate_b), (P, EXPERTS)),
        "ffn_w": np.concatenate([w1.transpose(2, 0, 1).reshape(P, -1),
                                 w2.transpose(0, 2, 1).reshape(ALL_EXPERTS, NF, P, HID).transpose(2, 0, 1, 3)
                                 .reshape(P, -1)], axis=1),
        "ffn_b1": b1.reshape(ALL_EXPERTS * NF, P).T,
        "ffn_b2": np.concatenate([np.asarray(L0_ffn_rb2), np.asarray(L0_ffn_sb2)]),
    }
    return {name: np.ascontiguousarray(a) for name, a in arrays.items()}


def kernel(**inputs):
    import concourse.bacc as bacc
    from concourse.bass_utils import run_bass_kernel_spmd

    arrays = layouts(**inputs)
    nc = bacc.Bacc("TRN2", target_bir_lowering=False, num_devices=1)
    args = [nc.dram_tensor(f"in_{name}", a.shape, mybir.dt.from_np(a.dtype), kind="ExternalInput").ap()
            for name, a in arrays.items()]
    out = nc.dram_tensor("out", (IMGS, SEQ, HID), FP32, kind="ExternalOutput").ap()
    build(nc, *args, out)
    r = run_bass_kernel_spmd(nc, [{f"in_{name}": a for name, a in arrays.items()}], core_ids=[0])
    return r.results[0]["out"]
```

```python
from contextlib import ExitStack

import numpy as np

import concourse.bass as bass
from concourse import mybir

FP32 = mybir.dt.float32
FP16 = mybir.dt.float16
I32 = mybir.dt.int32
U32 = mybir.dt.uint32
ALU = mybir.AluOpType
ACT = mybir.ActivationFunctionType
AXX = mybir.AxisListType.X

P = 128
IMGS, CHANNELS, SIDE, GRID = 64, 3, 196, 14
PATCHES = GRID * GRID
PATCH_DIM = CHANNELS * (SIDE // GRID) ** 2
TEXT = 32
SEQ = 1 + PATCHES + TEXT
CHUNKS = ((0, 117), (117, 112))
assert CHUNKS[1][0] + CHUNKS[1][1] == SEQ
PAIRS = IMGS // 2
PAIR_SEQ = 2 * SEQ
PAIR_PATCHES = 2 * PATCHES
NCH = 2 * IMGS
KP, KN = 126, 4
KREST = PATCH_DIM - KP * KN
HID = 128
E_GAU = 256
VOCAB, BASE = 25000, 257
EXPERTS, SHARED, F = 8, 2, 512
NF = F // P
ALL_EXPERTS = EXPERTS + SHARED
WCOLS = 2 * ALL_EXPERTS * F
WBLOCK = WCOLS // PAIRS
W2_AT = ALL_EXPERTS * F
TOKENS = IMGS * SEQ
TILE = 256
TILE_CH = TILE // P
TILES = (2 * TOKENS + EXPERTS * (TILE - 1)) // TILE
WORDS = -(-TILES // 4)
B2_ROWS = 64
B2_LO = 32
EARLY_PAIRS = 28
LOGITS_AT = PAIR_PATCHES
ROW = HID + 2
FILL_ROWS = -(-TILES * TILE // (PAIRS * P)) * P
SLOT_ROWS = FILL_ROWS * PAIRS
UNUSED = float(1 << 20)
EPS = 1e-5


class Own:

    def __init__(self, eng, sem, start=0):
        self.eng, self.sem, self.n = eng, sem, start

    def did(self, instruction):
        instruction.then_inc(self.sem, 1)
        self.n = self.n + 1

    def wait(self):
        self.eng.wait_ge(self.sem, self.n)


def settle(eng):
    eng.nop(nofuse=True)


def pair_loop(eng, step, lo, hi):
    assert lo % 2 == 0 and hi % 2 == 0
    with eng.Fori(lo // 2, hi // 2) as j:
        for parity in range(2):
            step(2 * j + parity, parity)


def build(nc, xmain, xrest, tokw_main, tokw_rest, txt, tokb, token, pos, emb2, emb3, emb4,
          w_rel, uv_w, o_w, gamma, beta, g, res, gate_w, gate_b, ffn_w, ffn_b1, shared_b2, routed_b2, out):
    x2t_dram = nc.dram_tensor("x2t_dram", [PAIRS, P, PAIR_SEQ], FP32).ap()
    x2r_dram = nc.dram_tensor("x2r_dram", [PAIRS, P, 4, HID], FP32).ap()
    slots_dram = nc.dram_tensor("slots_dram", [SLOT_ROWS, ROW], FP32).ap()
    y_dram = nc.dram_tensor("y_dram", [2 * TOKENS, HID], FP32).ap()

    with ExitStack() as keep:
        def sbuf(name, shape, dt=FP32):
            return keep.enter_context(nc.sbuf_tensor(name, shape, dt))

        bank = [keep.enter_context(nc.psum_tensor(f"bank{b}", [P, 512], FP32)) for b in range(8)]
        acc = sbuf("acc", [P, NCH, HID])
        w_hi = sbuf("w_hi", [P, WCOLS], FP16)
        w_lo = sbuf("w_lo", [P, WCOLS], FP16)
        b1 = sbuf("b1", [P, ALL_EXPERTS * NF])
        ident = sbuf("ident", [P, P])
        top8 = sbuf("top8", [P, NCH, 8])
        top_i = sbuf("top_i", [P, NCH, 2])
        token2 = sbuf("token2", [P, NCH])

        embed_and_attend(nc, bank, acc, w_hi, w_lo, b1, ident, top8, top_i, token2,
                         xmain, xrest, tokw_main, tokw_rest, txt, tokb, token, pos, emb2, emb3,
                         emb4, w_rel, uv_w, o_w, gamma, beta, g, res, gate_w, gate_b, ffn_w,
                         ffn_b1, x2t_dram, x2r_dram, slots_dram)
        b2 = sbuf("b2", [B2_ROWS, HID], FP16)
        b2_rows = sbuf("b2_rows", [P, EXPERTS * HID])
        ones2 = sbuf("ones2", [B2_ROWS, P], FP16)
        cw01 = sbuf("cw01", [P, NCH, 2])
        tile_e = sbuf("tile_e", [P, 2 + 4 * WORDS])
        experts_word = sbuf("experts_word", [P, WORDS], I32)
        route_and_share(nc, bank, acc, w_hi, w_lo, b1, shared_b2, routed_b2, b2, b2_rows, ones2, top8, top_i,
                        token2, cw01, tile_e, experts_word, x2t_dram, x2r_dram, slots_dram)
        y_out = [keep.enter_context(nc.semaphore(f"y_out{n}")) for n in range(4)]
        routed_ffn(nc, bank, w_hi, w_lo, b1, b2_rows, ident, tile_e, experts_word, slots_dram, y_dram,
                   y_out)
        share_and_combine(nc, bank, acc, w_hi, w_lo, b1, b2, ones2, cw01, x2t_dram, y_dram, y_out, out)


def embed_and_attend(nc, bank, acc, w_hi, w_lo, b1, ident, top8, top_i, token2,
                     xmain, xrest, tokw_main, tokw_rest, txt, tokb, token, pos, emb2, emb3, emb4,
                     w_rel, uv_w, o_w, gamma, beta, g, res, gate_w, gate_b, ffn_w, ffn_b1,
                     x2t_dram, x2r_dram, slots_dram):
    with ExitStack() as ctx:
        def sb(name, shape, dt=FP32):
            return ctx.enter_context(nc.sbuf_tensor(name, shape, dt))

        def sem(name):
            return ctx.enter_context(nc.semaphore(name))

        tokw = sb("tokw", [P, KN + 1, HID])
        uvw = sb("uvw", [P, 2 * E_GAU + HID])
        uvw16 = sb("uvw16", [P, 2, 2 * E_GAU + HID], FP16)
        ow = sb("ow", [P, 2, HID])
        posb = sb("posb", [P, SEQ - TEXT])
        tokbt = sb("tokbt", [P, 2])
        gb = sb("gb", [P, 4])
        gs = sb("gs", [P, 1])
        resb = sb("resb", [P, HID])
        gatew = sb("gatew", [P, EXPERTS])
        gateb = sb("gateb", [P, EXPERTS])
        rel = sb("rel", [P, 2, SEQ])
        tsh = sb("tsh", [P, 4, 16])
        tshi = sb("tshi", [P, 4, 16], I32)
        hsh = sb("hsh", [P, 3, 16])
        hq = sb("hq", [P, 3, 16])
        hqi = sb("hqi", [P, 3, 16], I32)
        hashes = sb("hashes", [P, 3, 16], U32)
        hash_now = sb("hash_now", [P, 3], U32)
        emb = sb("emb", [P, 3, HID])
        esum = sb("esum", [P, HID])
        xin = sb("xin", [P, 2, KN + 1, PAIR_PATCHES])
        wstage = sb("wstage", [P, 2, WBLOCK])
        hT = sb("hT", [P, 2, 2, SEQ])
        hn = sb("hn", [P, 2, 4, HID])
        stats = sb("stats", [P, 4, 6])
        mv = sb("mv", [P, 4, 2])
        var2 = sb("var2", [P, 2, 4])
        powers = sb("powers", [P, 3, 4])
        rstd = sb("rstd", [P, 2, 4])
        nrm = sb("nrm", [P, 4])
        scl = sb("scl", [P, 4])
        xa = sb("xa", [P, 2, 4, HID])
        xn = sb("xn", [P, 4, HID])
        xnT = sb("xnT", [P, 2, 2, PAIR_SEQ], FP16)
        base_s = sb("base_s", [P, PAIR_SEQ])
        qk_sb = sb("qk_sb", [P, 2, PAIR_SEQ])
        uT = sb("uT", [P, 2, 2, PAIR_SEQ])
        v_sb = sb("v_sb", [P, 2, 2, E_GAU])
        sc = sb("sc", [P, 2, 2, SEQ])
        kern = sb("kern", [P, 2, 2, SEQ])
        uav = sb("uav", [P, 2, 2, SEQ])
        stats2 = sb("stats2", [P, 4, 6])
        mv2 = sb("mv2", [P, 4, 2])
        rstd2 = sb("rstd2", [P, 4])
        x2f = sb("x2f", [P, 2, 4, HID])
        x2T = sb("x2T", [P, PAIR_SEQ])
        x2T16 = sb("x2T16", [P, 2, 2, PAIR_SEQ], FP16)
        x2r16 = sb("x2r16", [P, 2, 4, 2, HID], FP16)
        lgs = sb("lgs", [P, 4, EXPERTS])
        mx8 = sb("mx8", [P, 4, 8])
        mi8 = sb("mi8", [P, 4, 8], U32)
        fill = sb("fill", [P, FILL_ROWS // P, ROW])

        tokb_bank, tr1_bank, tr2_bank, o_bank = bank[0], bank[1], bank[2], bank[7]
        uv_bank, av_bank = bank[3:5], bank[5:7]

        tokw_in, pos_in = sem("tokw_in"), sem("pos_in")
        w_in = sem("w_in")
        w_late = sem("w_late")
        txt_in = sem("txt_in")
        x_in = [sem(f"x_in{n}") for n in range(2)]
        ws_in = [sem(f"ws_in{n}") for n in range(2)]
        emb_in = sem("emb_in")
        t_out = [sem(f"t_out{n}") for n in range(2)]
        r_out = [sem(f"r_out{n}") for n in range(2)]
        fill_out = sem("fill_out")
        zeroed = sem("zeroed")
        tables = sem("tables")
        const_p = sem("const_p")
        hashed = sem("hashed")
        setup_v = sem("setup_v")
        tok_done, tr1_done, tr2_done, txt_done = sem("tok_done"), sem("tr1_done"), sem("tr2_done"), sem("txt_done")
        uv_done, qk_done, av_done, o_done = sem("uv_done"), sem("qk_done"), sem("av_done"), sem("o_done")
        tr3_done, lg_done = sem("tr3_done"), sem("lg_done")
        hT_ready, xn_ready, t_done, kern_ready = sem("hT_ready"), sem("xn_ready"), sem("t_done"), sem("kern_ready")
        xa_ready, xnT_hi, uvw_hi, uvw_ready = sem("xa_ready"), sem("xnT_hi"), sem("uvw_hi"), sem("uvw_ready")
        uav_ready, mid_ready, x2_ready, lg_read = sem("uav_ready"), sem("mid_ready"), sem("x2_ready"), sem("lg_read")
        top_ready = sem("top_ready")
        bn_front, bn_mid, mv_ready, mv2_ready = sem("bn_front"), sem("bn_mid"), sem("mv_ready"), sem("mv2_ready")
        txt_copied, hn_ready, xnT_ready, sil, qk_ready, x2T_ready = (
            sem("txt_copied"), sem("hn_ready"), sem("xnT_ready"), sem("sil"), sem("qk_ready"), sem("x2T_ready"))
        base_ready = sem("base_ready")
        hash_set, esum1, esum_ready = sem("hash_set"), sem("esum1"), sem("esum_ready")
        scaled_ready, residual_ready, row_hi, row_ready, t_hi, t_ready = (
            sem("scaled_ready"), sem("residual_ready"), sem("row_hi"), sem("row_ready"), sem("t_hi"), sem("t_ready"))
        scl_own, scl_ready, rstd2_own, rstd2_ready = sem("scl_own"), sem("scl_ready"), sem("rstd2_own"), sem("rstd2_ready")
        ws_hi, ws_done, top_kept = sem("ws_hi"), sem("ws_done"), sem("top_kept")

        block = ctx.enter_context(nc.Block())
        N_W = 10

        def exists(n):
            return not isinstance(n, int) or 0 <= n < PAIRS

        def reaches(n, k):
            return not isinstance(n, int) or n >= k

        def steps(eng, step):
            lo, hi = 4, PAIRS - 6
            for i in range(-3, lo):
                step(i, i % 2, i // 2)
            with eng.Fori(lo // 2, hi // 2) as j:
                for p in range(2):
                    step(2 * j + p, p, j)
            for i in range(hi, PAIRS + 1):
                step(i, i % 2, i // 2)

        @block.sync
        def _(sp):
            def load_x(i, parity):
                sp.dma_start(xin[0:KP, parity, 0:KN, :], xmain[i]).then_inc(x_in[parity], 16)
                sp.dma_start(xin[0:KREST, parity, KN, :], xrest[i]).then_inc(x_in[parity], 16)

            def load_w(i, parity):
                sp.dma_start(wstage[:, parity, :], ffn_w[:, bass.ds(i * WBLOCK, WBLOCK)]).then_inc(ws_in[parity], 16)

            sp.dma_start(tshi[:, :, :], txt).then_inc(txt_in, 16)
            load_x(0, 0)
            for dst, src in ((tokw[0:KP, 0:KN, :], tokw_main), (tokw[0:KREST, KN, :], tokw_rest)):
                sp.dma_start(dst, src).then_inc(tokw_in, 16)
            for dst, src in ((posb[:, :], pos), (tokbt[:, 0:1], tokb), (tokbt[:, 1:2], token)):
                sp.dma_start(dst, src).then_inc(pos_in, 16)
            sp.wait_ge(zeroed, 1)
            for dst, src in ((uvw[:, :], uv_w), (gb[:, 0:2], gamma), (gb[:, 2:4], beta),
                             (gs[:, :], g), (resb[:, :], res), (gatew[:, :], gate_w),
                             (gateb[:, :], gate_b), (ow[:, :, :], o_w)):
                sp.dma_start(dst, src).then_inc(w_in, 16)
            for c, (at, n) in enumerate(CHUNKS):
                sp.dma_start(rel[0:n, c, :], w_rel[at:at + n, :]).then_inc(w_in, 16)
            load_x(1, 1)
            load_w(0, 0)
            load_w(1, 1)
            sp.dma_start(b1[:, :], ffn_b1).then_inc(w_late, 16)

            def store_x2(b, parity):
                sp.wait_ge(row_ready, b + 1)
                sp.dma_start(x2r_dram[b], x2r16[:, parity].bitcast(FP32).rearrange("p c h d -> p c (h d)")
                             ).then_inc(r_out[parity], 16)
                sp.wait_ge(t_ready, b + 1)
                sp.dma_start(x2t_dram[b], x2T16[:, parity].bitcast(FP32).rearrange("p h n -> p (h n)")
                             ).then_inc(t_out[parity], 16)

            def step(i, p, j):
                if exists(i):
                    sp.dma_start(slots_dram[bass.ds(i * FILL_ROWS, FILL_ROWS), :].rearrange("(t p) w -> p t w", p=P),
                                 fill[:, :, :]).then_inc(fill_out, 16)
                if exists(i + 5):
                    sp.wait_ge(tok_done, i + 4)
                    load_x(i + 5, (p + 5) % 2)
                if exists(i) and exists(i + 2):
                    sp.wait_ge(ws_done, i + 1)
                    load_w(i + 2, p)
                if exists(i - 1):
                    store_x2(i - 1, 1 - p)

            sp.wait_ge(tables, 2)
            steps(sp, step)
            for parity in range(2):
                sp.wait_ge(r_out[parity], 16 * PAIRS // 2)
                sp.wait_ge(t_out[parity], 16 * PAIRS // 2)
            sp.wait_ge(fill_out, 16 * PAIRS)
            sp.wait_ge(w_late, 16)

        @block.gpsimd
        def _(pool):
            pool.memset(rel[:, :, :], 0.0).then_inc(zeroed, 1)
            pool.memset(ident[:, :], 0.0).then_inc(const_p, 1)
            pool.wait_ge(const_p, 1)
            pool.affine_select(out=ident[:, :], in_=ident[:, :], compare_op=ALU.not_equal, fill=1.0,
                               base=0, pattern=[[-1, P]], channel_multiplier=1).then_inc(tables, 1)
            pool.memset(fill[:, :, :], 0.0).then_inc(const_p, 1)
            for c, (at, _) in enumerate(CHUNKS):
                pool.iota(token2[:, c:NCH:2], pattern=[[2 * SEQ, IMGS]], base=2 * at, channel_multiplier=2,
                          allow_small_or_imprecise_dtypes=True).then_inc(const_p, 1)
            for n, power in enumerate((-0.5, 0.5, -1.0)):
                pool.memset(powers[:, n, :], power).then_inc(const_p, 1)
            pool.wait_ge(const_p, 7)
            pool.memset(fill[:, :, HID:HID + 1], UNUSED).then_inc(tables, 1)
            pool.wait_ge(hashed, 1)

            def gather_text(grp):
                if not (isinstance(grp, int) and grp == 0):
                    pool.wait_ge(esum_ready, grp)
                settle(pool)
                pool.tensor_copy(hash_now[:, :].rearrange("p (n o) -> p n o", o=1),
                                 hashes[:, :, bass.ds(grp, 1)]).then_inc(hash_set, 1)
                pool.wait_ge(hash_set, grp + 1)
                settle(pool)
                for n, table in enumerate((emb2, emb3, emb4)):
                    pool.indirect_dma_start(
                        out=emb[:, n, :], out_offset=None, in_=table,
                        in_offset=bass.IndirectOffsetOnAxis(ap=hash_now[:, n:n + 1], axis=0)).then_inc(emb_in, 16)

            def sum_text(grp):
                pool.wait_ge(emb_in, 48 * (grp + 1))
                if not (isinstance(grp, int) and grp == 0):
                    pool.wait_ge(txt_done, grp)
                pool.tensor_tensor(esum[:, :], emb[:, 0, :], emb[:, 1, :], ALU.add).then_inc(esum1, 1)
                pool.wait_ge(esum1, grp + 1)
                pool.tensor_tensor(esum[:, :], esum[:, :], emb[:, 2, :], ALU.add).then_inc(esum_ready, 1)

            def residual(n, parity):
                pool.wait_ge(xa_ready, n + 1)
                settle(pool)
                part = acc[:, bass.ds(4 * n, 4), :]
                pool.tensor_tensor(part, xa[:, parity], resb[:, :].rearrange("p (o d) -> p o d", o=1)
                                   .to_broadcast([P, 4, HID]), ALU.mult).then_inc(scaled_ready, 1)
                pool.wait_ge(scaled_ready, n + 1)
                settle(pool)
                pool.tensor_tensor(part, part, hn[:, parity], ALU.add).then_inc(residual_ready, 1)

            def split_w(i, parity):
                pool.wait_ge(ws_hi, i + 1)
                pool.tensor_tensor(w_lo[:, bass.ds(i * WBLOCK, WBLOCK)], wstage[:, parity, :],
                                   w_hi[:, bass.ds(i * WBLOCK, WBLOCK)], ALU.subtract).then_inc(ws_done, 1)

            def split_rows(b, parity):
                pool.wait_ge(row_hi, b + 1)
                pool.tensor_tensor(x2r16[:, parity, :, 1, :], x2f[:, parity], x2r16[:, parity, :, 0, :],
                                   ALU.subtract).then_inc(row_ready, 1)

            def split_columns(b, parity):
                pool.wait_ge(t_hi, b + 1)
                pool.tensor_tensor(x2T16[:, parity, 1, :], x2T[:, :], x2T16[:, parity, 0, :],
                                   ALU.subtract).then_inc(t_ready, 1)

            def keep_top(b):
                pool.wait_ge(top_ready, 8 * (b + 1))
                settle(pool)
                pool.tensor_copy(top8[:, bass.ds(4 * b, 4), :], mx8[:, :, :]).then_inc(top_kept, 1)
                pool.tensor_copy(top_i[:, bass.ds(4 * b, 4), :], mi8[:, :, 0:2]).then_inc(top_kept, 1)

            def front_scales(n):
                own = Own(pool, scl_own, 6 * n)
                pool.wait_ge(mv_ready, n + 1)
                settle(pool)
                pool.tensor_scalar(var2[:, 0, :], mv[:, :, 1], EPS, None, ALU.add)
                own.did(pool.tensor_scalar(var2[:, 1, :], mv[:, :, 1], float(HID), None, ALU.mult))
                own.wait()
                own.did(pool.tensor_tensor(rstd[:, :, :], var2[:, :, :], powers[:, 0:2, :], ALU.pow))
                own.wait()
                own.did(pool.tensor_tensor(nrm[:, :], rstd[:, 0, :], rstd[:, 1, :], ALU.mult))
                own.wait()
                settle(pool)
                own.did(pool.tensor_scalar(nrm[:, :], nrm[:, :], EPS, None, ALU.max))
                own.wait()
                own.did(pool.tensor_tensor(nrm[:, :], nrm[:, :], powers[:, 2, :], ALU.pow))
                own.wait()
                settle(pool)
                own.did(pool.tensor_scalar(nrm[:, :], nrm[:, :], gs[:, 0:1], None, ALU.mult))
                own.wait()
                pool.tensor_tensor(scl[:, :], nrm[:, :], rstd[:, 0, :], ALU.mult).then_inc(scl_ready, 1)

            def mid_scales(i):
                pool.wait_ge(mv2_ready, i + 1)
                settle(pool)
                pool.tensor_scalar(rstd2[:, :], mv2[:, :, 1], EPS, None, ALU.add).then_inc(rstd2_own, 1)
                pool.wait_ge(rstd2_own, i + 1)
                pool.tensor_tensor(rstd2[:, :], rstd2[:, :], powers[:, 0, :], ALU.pow).then_inc(rstd2_ready, 1)

            def step(i, p, j):
                text_ahead = p == 0 and (not isinstance(j, int) or 0 <= j + 2 < IMGS // 4)
                if exists(i - 2):
                    keep_top(i - 2)
                if text_ahead:
                    gather_text(j + 2)
                if exists(i - 1):
                    split_columns(i - 1, 1 - p)
                if exists(i + 2):
                    residual(i + 2, p)
                if exists(i - 1):
                    split_rows(i - 1, 1 - p)
                if exists(i):
                    split_w(i, p)
                if text_ahead:
                    sum_text(j + 2)
                if exists(i):
                    mid_scales(i)
                if exists(i + 3):
                    front_scales(i + 3)

            gather_text(0)
            sum_text(0)
            pool.wait_ge(w_in, 16 * N_W)
            steps(pool, step)
            keep_top(PAIRS - 1)

        @block.vector
        def _(dve):
            own = Own(dve, setup_v)
            for b in range(8):
                own.did(dve.memset(bank[b][:, :], 0.0))
            own.did(dve.memset(hn[:, :, :, :], 0.0))
            dve.wait_ge(pos_in, 48)
            own.did(dve.tensor_tensor(tokbt[:, 1:2], tokbt[:, 1:2], posb[:, 0:1], ALU.add))
            own.did(dve.tensor_scalar(posb[:, 1:1 + PATCHES], posb[:, 1:1 + PATCHES], tokbt[:, 0:1], None, ALU.add))
            own.wait()
            own.did(dve.tensor_copy(hT[:, :, :, 0:1].rearrange("p s i o -> p (s i) o"),
                                    tokbt[:, 1:2].rearrange("p (o t) -> p o t", t=1).to_broadcast([P, 4, 1])))
            dve.wait_ge(txt_in, 16)
            own.did(dve.tensor_copy(tsh[:, :, :], tshi[:, :, :]))
            own.wait()
            own.did(dve.scalar_tensor_tensor(out=hsh[:, 0, :], in0=tsh[:, 1, :], scalar=float(BASE),
                                             in1=tsh[:, 0, :], op0=ALU.mult, op1=ALU.add))
            for n in (1, 2):
                own.wait()
                own.did(dve.scalar_tensor_tensor(out=hsh[:, n, :], in0=tsh[:, n + 1, :],
                                                 scalar=float(pow(BASE, n + 1, VOCAB)),
                                                 in1=hsh[:, n - 1, :], op0=ALU.mult, op1=ALU.add))
            own.wait()
            own.did(dve.tensor_scalar(hq[:, :, :], hsh[:, :, :], 1.0 / VOCAB, None, ALU.mult))
            own.wait()
            own.did(dve.tensor_copy(hqi[:, :, :], hq[:, :, :]))
            own.wait()
            own.did(dve.tensor_copy(hq[:, :, :], hqi[:, :, :]))
            own.wait()
            own.did(dve.scalar_tensor_tensor(out=hsh[:, :, :], in0=hq[:, :, :], scalar=-float(VOCAB),
                                             in1=hsh[:, :, :], op0=ALU.mult, op1=ALU.add))
            own.wait()
            own.did(dve.tensor_scalar(hq[:, :, :], hsh[:, :, :], 0.0, float(VOCAB), ALU.is_lt, ALU.mult))
            own.wait()
            own.did(dve.tensor_tensor(hsh[:, :, :], hsh[:, :, :], hq[:, :, :], ALU.add))
            own.wait()
            own.did(dve.tensor_scalar(hq[:, :, :], hsh[:, :, :], float(VOCAB), float(VOCAB), ALU.is_ge, ALU.mult))
            own.wait()
            dve.tensor_tensor(hashes[:, :, :], hsh[:, :, :], hq[:, :, :], ALU.subtract).then_inc(hashed, 1)

            def xnT_low(n, parity):
                dve.wait_ge(xnT_hi, n + 1)
                dve.tensor_tensor(xnT[:, parity, 1, :], tr2_bank[:, 0:PAIR_SEQ], xnT[:, parity, 0, :],
                                  ALU.subtract).then_inc(xnT_ready, 1)

            def assemble(n, parity):
                dve.wait_ge(tok_done, n + 1)
                if reaches(n, 2):
                    dve.wait_ge(tr1_done, n - 1)
                dve.tensor_tensor(hT[:, parity, :, 1:1 + PATCHES],
                                  tokb_bank[:, 0:PAIR_PATCHES].rearrange("p (i n) -> p i n", i=2),
                                  posb[:, 1:1 + PATCHES].rearrange("p (o n) -> p o n", o=1)
                                  .to_broadcast([P, 2, PATCHES]), ALU.add).then_inc(hT_ready, 1)

            def norm_stats(k, src, stats, mv, sem, done):
                settle(dve)
                for c in range(4):
                    dve.bn_stats(stats[:, c, :], src(c)).then_inc(sem, 1)
                dve.wait_ge(sem, 4 * k + 4)
                settle(dve)
                for c in range(4):
                    last = dve.bn_aggr(mv[:, c, :], stats[:, c, :])
                last.then_inc(done, 1)

            def front_stats(n, parity):
                dve.wait_ge(hn_ready, n + 1)
                norm_stats(n, lambda c: hn[:, parity, c, :], stats, mv, bn_front, mv_ready)

            def front_norm(n, parity):
                dve.wait_ge(scl_ready, n + 1)
                if reaches(n, 2):
                    dve.wait_ge(residual_ready, n - 1)
                if reaches(n, 1):
                    dve.wait_ge(tr2_done, n)
                for c in range(4):
                    last = dve.tensor_scalar(xn[:, c, :], hn[:, parity, c, :], mv[:, c, 0:1], scl[:, c:c + 1],
                                             ALU.subtract, ALU.mult)
                last.then_inc(xn_ready, 1)
                for c in range(4):
                    last = dve.tensor_scalar(xa[:, parity, c, :], hn[:, parity, c, :], mv[:, c, 0:1], rstd[:, 0, c:c + 1],
                                             ALU.subtract, ALU.mult)
                last.then_inc(xa_ready, 1)

            def scores(i, img):
                dve.wait_ge(qk_done, 2 * i + img + 1)
                dve.tensor_tensor(sc[:, img], av_bank[img][:, 0:PAIR_SEQ].rearrange("p (c n) -> p c n", c=2),
                                  rel[:, :, :], ALU.add).then_inc(t_done, 1)
                dve.wait_ge(t_done, 2 * i + img + 1)
                if not (isinstance(i, int) and i == 0):
                    dve.wait_ge(av_done, 2 * i + img - 1)
                dve.scalar_tensor_tensor(out=kern[:, img], in0=sc[:, img], scalar=0.0, in1=sc[:, img],
                                         op0=ALU.max, op1=ALU.mult).then_inc(kern_ready, 1)

            def gate(i, img, parity):
                dve.wait_ge(av_done, 2 * i + img + 1)
                dve.wait_ge(sil, 5 * i + 3)
                if reaches(i, 1):
                    dve.wait_ge(o_done, i)
                dve.scalar_tensor_tensor(out=uav[:, img], in0=av_bank[img][:, 0:PAIR_SEQ].rearrange("p (e n) -> p e n", e=2),
                                         scalar=1.0 / HID, in1=uT[:, parity, :, img * SEQ:(img + 1) * SEQ],
                                         op0=ALU.mult, op1=ALU.mult).then_inc(uav_ready, 1)

            def middle(i):
                dve.wait_ge(o_done, i + 1)
                dve.wait_ge(residual_ready, i + 1)
                part = acc[:, bass.ds(4 * i, 4), :]
                dve.tensor_tensor(part, o_bank[:, :].rearrange("p (c d) -> p c d", c=4), part,
                                  ALU.add).then_inc(mid_ready, 1)
                dve.wait_ge(mid_ready, i + 1)
                norm_stats(i, lambda c: acc[:, bass.ds(4 * i + c, 1), :], stats2, mv2, bn_mid, mv2_ready)

            def second_norm(i, parity):
                dve.wait_ge(rstd2_ready, i + 1)
                if reaches(i, 2):
                    dve.wait_ge(row_ready, i - 1)
                    dve.wait_ge(tr3_done, i - 1)
                for c in range(4):
                    last = dve.tensor_scalar(x2f[:, parity, c, :], acc[:, bass.ds(4 * i + c, 1), :], mv2[:, c, 0:1],
                                             rstd2[:, c:c + 1], ALU.subtract, ALU.mult)
                last.then_inc(x2_ready, 1)

            def top(b):
                dve.wait_ge(lg_done, b + 1)
                if not (isinstance(b, int) and b == 0):
                    dve.wait_ge(top_kept, 2 * b)
                dve.tensor_tensor(lgs[:, :, :], tokb_bank[:, LOGITS_AT:LOGITS_AT + 4 * EXPERTS].rearrange("p (c e) -> p c e", c=4),
                                  gateb[:, :].rearrange("p (o e) -> p o e", o=1).to_broadcast([P, 4, EXPERTS]),
                                  ALU.add).then_inc(lg_read, 1)
                dve.wait_ge(lg_read, b + 1)
                settle(dve)
                for c in range(4):
                    dve.max(mx8[:, c, :], lgs[:, c, :]).then_inc(top_ready, 1)
                dve.wait_ge(top_ready, 8 * b + 4)
                settle(dve)
                for c in range(4):
                    dve.max_index(mi8[:, c, :], mx8[:, c, :], lgs[:, c, :]).then_inc(top_ready, 1)

            def step(i, p, j):
                if exists(i - 1):
                    second_norm(i - 1, 1 - p)
                if exists(i):
                    gate(i, 0, p)
                if exists(i + 3):
                    assemble(i + 3, 1 - p)
                if exists(i):
                    gate(i, 1, p)
                if exists(i + 2):
                    front_norm(i + 2, p)
                for img in range(2):
                    if exists(i + 1):
                        scores(i + 1, img)
                if exists(i - 1):
                    top(i - 1)
                if exists(i + 2):
                    xnT_low(i + 2, p)
                if exists(i):
                    middle(i)
                if exists(i + 3):
                    front_stats(i + 3, 1 - p)

            own.wait()
            dve.wait_ge(uvw_hi, 1)
            dve.tensor_tensor(uvw16[:, 1, :], uvw[:, :], uvw16[:, 0, :], ALU.subtract).then_inc(uvw_ready, 1)
            steps(dve, step)

        @block.scalar
        def _(act):
            act.wait_ge(w_in, 16 * N_W)
            act.wait_ge(setup_v, 9)
            act.activation(uvw16[:, 0, :], uvw[:, :], ACT.Copy).then_inc(uvw_hi, 1)

            def copy_text(grp):
                act.wait_ge(txt_done, grp + 1)
                if not (isinstance(grp, int) and grp == 0):
                    act.wait_ge(tr1_done, 2 * grp)
                act.activation(hT[:, :, :, 1 + PATCHES:SEQ],
                               tr1_bank[:, 0:P].rearrange("p (s i n) -> p s i n", s=2, i=2),
                               ACT.Copy).then_inc(txt_copied, 1)

            def copy_h(n, parity):
                act.wait_ge(tr1_done, n + 1)
                if reaches(n, 2):
                    act.wait_ge(residual_ready, n - 1)
                act.activation(hn[:, parity], tr1_bank[:, :].rearrange("p (c d) -> p c d", c=4),
                               ACT.Copy).then_inc(hn_ready, 1)

            def copy_xnT(n, parity):
                act.wait_ge(tr2_done, n + 1)
                if reaches(n, 2):
                    act.wait_ge(uv_done, 5 * n - 5)
                act.activation(xnT[:, parity, 0, :], tr2_bank[:, 0:PAIR_SEQ], ACT.Copy).then_inc(xnT_hi, 1)

            def copy_x2T(b):
                act.wait_ge(tr3_done, b + 1)
                if not (isinstance(b, int) and b == 0):
                    act.wait_ge(t_ready, b)
                    act.wait_ge(lg_done, b)
                act.activation(x2T[:, :], tr2_bank[:, 0:PAIR_SEQ], ACT.Copy).then_inc(x2T_ready, 1)

            def uv(i, parity, r):
                src = uv_bank[(parity + r) % 2]
                later = reaches(i, 1)
                act.wait_ge(uv_done, 5 * i + r + 1)
                if r == 0:
                    if later:
                        act.wait_ge(qk_ready, 2 * i)
                    act.activation(base_s[:, :], src[:, 0:PAIR_SEQ], ACT.Silu).then_inc(sil, 1)
                    act.wait_ge(sil, 5 * i + 1)
                    if later:
                        act.wait_ge(qk_done, 2 * i)
                    for n in range(2):
                        act.activation(qk_sb[:, n, :], base_s[:, :], ACT.Identity, bias=gb[:, 2 + n:3 + n],
                                       scale=gb[:, n:n + 1]).then_inc(qk_ready, 1)
                elif r < 3:
                    if reaches(i, 2):
                        act.wait_ge(uav_ready, 2 * i - 2)
                    act.activation(uT[:, parity, r - 1, :], src[:, 0:PAIR_SEQ], ACT.Silu).then_inc(sil, 1)
                else:
                    if later:
                        act.wait_ge(av_done, 2 * i)
                    act.activation(v_sb[:, r - 3], src[:, :].rearrange("p (c e) -> p c e", c=2),
                                   ACT.Silu).then_inc(sil, 1)

            def rows_hi(b, parity):
                act.wait_ge(x2_ready, b + 1)
                if reaches(b, 2):
                    act.wait_ge(r_out[parity], 8 * (b - parity))
                act.activation(x2r16[:, parity, :, 0, :], x2f[:, parity], ACT.Copy).then_inc(row_hi, 1)

            def columns_hi(b, parity):
                copy_x2T(b)
                act.wait_ge(x2T_ready, b + 1)
                if reaches(b, 2):
                    act.wait_ge(t_out[parity], 8 * (b - parity))
                act.activation(x2T16[:, parity, 0, :], x2T[:, :], ACT.Copy).then_inc(t_hi, 1)

            def weights_hi(i, parity):
                act.wait_ge(ws_in[parity], 8 * (i - parity) + 16)
                act.activation(w_hi[:, bass.ds(i * WBLOCK, WBLOCK)], wstage[:, parity, :], ACT.Copy).then_inc(ws_hi, 1)

            def step(i, p, j):
                if exists(i + 1):
                    uv(i + 1, 1 - p, 0)
                if exists(i - 1):
                    columns_hi(i - 1, 1 - p)
                    rows_hi(i - 1, 1 - p)
                if exists(i + 1):
                    uv(i + 1, 1 - p, 1)
                    uv(i + 1, 1 - p, 2)
                if exists(i + 3):
                    if p == 1:
                        copy_text(j + 2)
                    copy_h(i + 3, 1 - p)
                if exists(i + 2):
                    copy_xnT(i + 2, p)
                if exists(i + 1):
                    uv(i + 1, 1 - p, 3)
                    uv(i + 1, 1 - p, 4)
                if exists(i):
                    weights_hi(i, p)

            steps(act, step)

        @block.tensor
        def _(pe):
            def text(grp):
                pe.wait_ge(esum_ready, grp + 1)
                if not (isinstance(grp, int) and grp == 0):
                    pe.wait_ge(hn_ready, 2 * grp)
                pe.transpose(tr1_bank[:, 0:P], esum[:, :], ident[:, :]).then_inc(txt_done, 1)

            def patches(n, parity):
                pe.wait_ge(x_in[parity], 16 * (n - parity) + 32)
                if reaches(n, 1):
                    pe.wait_ge(hT_ready, n)
                if reaches(n, 5):
                    pe.wait_ge(lg_read, n - 4)
                for k in range(KN + 1):
                    rows = KP if k < KN else KREST
                    last = pe.matmul(tokb_bank[:, 0:PAIR_PATCHES], tokw[0:rows, k, :], xin[0:rows, parity, k, :],
                                     start=k == 0, stop=k == KN)
                last.then_inc(tok_done, 1)

            def to_rows(n, parity, grp):
                pe.wait_ge(hT_ready, n + 1)
                pe.wait_ge(txt_copied, grp + 1)
                if not (isinstance(n, int) and n == 0):
                    pe.wait_ge(hn_ready, n)
                for img in range(2):
                    for c, (at, rows) in enumerate(CHUNKS):
                        q = 2 * img + c
                        last = pe.transpose(tr1_bank[0:rows, q * HID:(q + 1) * HID],
                                            hT[:, parity, img, at:at + rows], ident[:, :])
                last.then_inc(tr1_done, 1)

            def to_columns(src, done):
                for img in range(2):
                    for c, (at, rows) in enumerate(CHUNKS):
                        last = pe.transpose(tr2_bank[:, img * SEQ + at:img * SEQ + at + rows],
                                            src[0:rows, 2 * img + c, :], ident[0:rows, 0:rows])
                last.then_inc(done, 1)

            def xn_columns(n):
                pe.wait_ge(xn_ready, n + 1)
                if reaches(n, 3):
                    pe.wait_ge(x2T_ready, n - 2)
                to_columns(xn, tr2_done)

            def x2_columns(b, parity):
                pe.wait_ge(x2_ready, b + 1)
                pe.wait_ge(xnT_ready, min(b + 3, PAIRS) if isinstance(b, int) else b + 3)
                to_columns(x2f[:, parity], tr3_done)

            def logits(b):
                pe.wait_ge(x2T_ready, b + 1)
                pe.wait_ge(hT_ready, min(b + 5, PAIRS) if isinstance(b, int) else b + 5)
                if reaches(b, 1):
                    pe.wait_ge(lg_read, b)
                for img in range(2):
                    for c, (at, rows) in enumerate(CHUNKS):
                        q = 2 * img + c
                        last = pe.matmul(tokb_bank[0:rows, LOGITS_AT + q * EXPERTS:LOGITS_AT + (q + 1) * EXPERTS],
                                         x2T[:, img * SEQ + at:img * SEQ + at + rows], gatew[:, :],
                                         start=True, stop=True)
                last.then_inc(lg_done, 1)

            def uv(i, parity, r):
                if not (isinstance(i, int) and i == 0 and r < 2):
                    pe.wait_ge(sil, 5 * i + r - 1)
                dst = uv_bank[(parity + r) % 2]
                if r == 0:
                    pe.wait_ge(xnT_ready, i + 1)
                parts = ((0, 0), (0, 1), (1, 0))
                if r < 3:
                    at = 2 * E_GAU if r == 0 else (r - 1) * P
                    for n, (w, x) in enumerate(parts):
                        last = pe.matmul(dst[:, 0:PAIR_SEQ], uvw16[:, w, at:at + P], xnT[:, parity, x, :],
                                         start=n == 0, stop=n == 2)
                else:
                    for c, (at, rows) in enumerate(CHUNKS):
                        at += (r - 3) * SEQ
                        for n, (w, x) in enumerate(parts):
                            last = pe.matmul(dst[0:rows, c * E_GAU:(c + 1) * E_GAU], xnT[:, parity, x, at:at + rows],
                                             uvw16[:, w, E_GAU:2 * E_GAU], start=n == 0, stop=n == 2)
                last.then_inc(uv_done, 1)

            def qk(i, img):
                pe.wait_ge(qk_ready, 2 * i + 2)
                if not (isinstance(i, int) and i == 0):
                    pe.wait_ge(uav_ready, 2 * i + img - 1)
                for c, (at, rows) in enumerate(CHUNKS):
                    last = pe.matmul(av_bank[img][0:rows, c * SEQ:(c + 1) * SEQ],
                                     qk_sb[:, 1, img * SEQ + at:img * SEQ + at + rows],
                                     qk_sb[:, 0, img * SEQ:(img + 1) * SEQ], start=True, stop=True)
                last.then_inc(qk_done, 1)

            def av(i, img):
                pe.wait_ge(kern_ready, 2 * i + img + 1)
                pe.wait_ge(sil, 5 * i + 5)
                for e in range(2):
                    for c, (at, rows) in enumerate(CHUNKS):
                        last = pe.matmul(av_bank[img][:, e * SEQ:(e + 1) * SEQ],
                                         v_sb[0:rows, img, c, e * P:(e + 1) * P], kern[0:rows, img, c, :],
                                         start=c == 0, stop=c == 1)
                last.then_inc(av_done, 1)

            def project(i, img):
                pe.wait_ge(uav_ready, 2 * i + img + 1)
                if img == 0 and reaches(i, 1):
                    pe.wait_ge(mid_ready, i)
                for c, (at, rows) in enumerate(CHUNKS):
                    q = 2 * img + c
                    for e in range(2):
                        last = pe.matmul(o_bank[0:rows, q * HID:(q + 1) * HID], uav[:, img, e, at:at + rows],
                                         ow[:, e, :], start=e == 0, stop=e == 1)
                if img == 1:
                    last.then_inc(o_done, 1)

            def step(i, p, j):
                if exists(i + 1):
                    uv(i + 1, 1 - p, 0)
                if exists(i):
                    av(i, 0)
                if exists(i + 3):
                    patches(i + 3, 1 - p)
                if exists(i):
                    av(i, 1)
                if exists(i - 1):
                    x2_columns(i - 1, 1 - p)
                if exists(i + 1):
                    uv(i + 1, 1 - p, 1)
                    qk(i + 1, 0)
                    uv(i + 1, 1 - p, 2)
                if exists(i):
                    project(i, 0)
                if exists(i + 1):
                    qk(i + 1, 1)
                if exists(i + 3):
                    if p == 1:
                        text(j + 2)
                    to_rows(i + 3, 1 - p, j + (p + 3) // 2)
                if exists(i):
                    project(i, 1)
                if exists(i - 1):
                    logits(i - 1)
                if exists(i + 2):
                    xn_columns(i + 2)
                if exists(i + 1):
                    uv(i + 1, 1 - p, 3)
                    uv(i + 1, 1 - p, 4)

            pe.wait_ge(tokw_in, 32)
            pe.wait_ge(tables, 1)
            pe.wait_ge(setup_v, 9)
            steps(pe, step)


class SharedExperts:
    NG = SHARED * NF

    def __init__(self, nc, ctx, tag, first, bank, acc, w_hi, w_lo, b1, b2, ones2, x2t_dram):
        def sb(name, shape, dt=FP32):
            return ctx.enter_context(nc.sbuf_tensor(f"{name}_{tag}", shape, dt))

        def sem(name):
            return ctx.enter_context(nc.semaphore(f"{name}_{tag}"))

        self.first, self.acc, self.x2t_dram = first, acc, x2t_dram
        self.w_hi, self.w_lo, self.b1, self.b2, self.ones2 = w_hi, w_lo, b1, b2, ones2
        self.xT = sb("xT", [P, 2, 2, PAIR_SEQ], FP16)
        self.gel = sb("gel", [P, 2, PAIR_SEQ])
        self.hid = sb("hid", [P, 2, 2, self.NG, PAIR_SEQ], FP16)
        self.up_bank, self.down_bank = bank[0:4], bank[4:6]
        self.xt_in = [sem(f"xt_in{n}") for n in range(2)]
        self.up_done, self.down_done = sem("up_done"), sem("down_done")
        self.gel_ready, self.hid_hi, self.hid_ready = sem("gel_ready"), sem("hid_hi"), sem("hid_ready")
        self.acc_done = sem("acc_done")

    def load(self, eng, k, parity):
        if not (isinstance(k, int) and k < 2):
            eng.wait_ge(self.up_done, self.NG * (k - 1))
        eng.dma_start(self.xT[:, parity].bitcast(FP32).rearrange("p h n -> p (h n)"), self.x2t_dram[self.first + k]
                     ).then_inc(self.xt_in[parity], 16)

    def up(self, pe, k, parity, f):
        if f == 0:
            pe.wait_ge(self.xt_in[parity], 8 * (k - parity) + 16)
        if not (isinstance(k, int) and k == 0 and f < 4):
            pe.wait_ge(self.gel_ready, self.NG * k + f - 3)
        dst = self.up_bank[f % 4][:, 0:PAIR_SEQ]
        w = slice(f * P, (f + 1) * P)
        pe.matmul(dst, self.w_hi[:, w], self.xT[:, parity, 0, :], start=True, stop=False)
        pe.matmul(dst, self.w_hi[:, w], self.xT[:, parity, 1, :], start=False, stop=False)
        pe.matmul(dst, self.w_lo[:, w], self.xT[:, parity, 0, :], start=False, stop=True).then_inc(self.up_done, 1)

    def gelu(self, act, k, f):
        act.wait_ge(self.up_done, self.NG * k + f + 1)
        if not (isinstance(k, int) and k == 0 and f < 2):
            act.wait_ge(self.hid_ready, self.NG * k + f - 1)
        act.activation(self.gel[:, f % 2, :], self.up_bank[f % 4][:, 0:PAIR_SEQ], ACT.Gelu,
                       bias=self.b1[:, f:f + 1]).then_inc(self.gel_ready, 1)

    def high_on_act(self, act, f):
        act.wait_ge(self.gel_ready, f + 1)
        act.activation(self.hid[:, 0, 0, f, :], self.gel[:, f % 2, :], ACT.Copy).then_inc(self.hid_hi, 1)

    def low_on_pool(self, pool, f):
        pool.wait_ge(self.hid_hi, f + 1)
        pool.tensor_tensor(self.hid[:, 0, 1, f, :], self.gel[:, f % 2, :], self.hid[:, 0, 0, f, :],
                           ALU.subtract).then_inc(self.hid_ready, 1)

    def split(self, dve, k, parity, f):
        dve.wait_ge(self.gel_ready, self.NG * k + f + 1)
        if not (isinstance(k, int) and k < 2) and f == 0:
            dve.wait_ge(self.down_done, 2 * k - 2)
        hi, lo = self.hid[:, parity, 0, f, :], self.hid[:, parity, 1, f, :]
        dve.tensor_copy(hi, self.gel[:, f % 2, :]).then_inc(self.hid_hi, 1)
        dve.wait_ge(self.hid_hi, self.NG * k + f + 1)
        dve.tensor_tensor(lo, self.gel[:, f % 2, :], hi, ALU.subtract).then_inc(self.hid_ready, 1)

    def down(self, pe, k, parity, c):
        img, (at, n) = c // 2, CHUNKS[c % 2]
        at += img * SEQ
        if c == 0:
            pe.wait_ge(self.hid_ready, self.NG * (k + 1))
        if c % 2 == 0 and not (isinstance(k, int) and k == 0):
            pe.wait_ge(self.acc_done, 2 * k + img - 1)
        dst = self.down_bank[img][0:n, (c % 2) * HID:(c % 2 + 1) * HID]
        pe.matmul(dst, self.ones2[:, 0:n], self.b2[:, :], start=True, stop=False)
        for f in range(self.NG):
            w = slice(W2_AT + f * P, W2_AT + (f + 1) * P)
            hi, lo = self.hid[:, parity, 0, f, at:at + n], self.hid[:, parity, 1, f, at:at + n]
            pe.matmul(dst, hi, self.w_hi[:, w], start=False, stop=False)
            pe.matmul(dst, hi, self.w_lo[:, w], start=False, stop=False)
            last = pe.matmul(dst, lo, self.w_hi[:, w], start=False, stop=f == self.NG - 1)
        if c % 2 == 1:
            last.then_inc(self.down_done, 1)

    def accumulate(self, dve, k, img):
        dve.wait_ge(self.down_done, 2 * k + img + 1)
        part = self.acc[:, bass.ds(4 * (self.first + k) + 2 * img, 2), :]
        dve.tensor_tensor(part, part, self.down_bank[img][:, 0:2 * HID].rearrange("p (c d) -> p c d", c=2),
                          ALU.add).then_inc(self.acc_done, 1)


def route_and_share(nc, bank, acc, w_hi, w_lo, b1, shared_b2, routed_b2, b2, b2_rows, ones2, top8, top_i,
                    token2, cw01, tile_e, experts_word, x2t_dram, x2r_dram, slots_dram):
    with ExitStack() as ctx:
        def sb(name, shape, dt=FP32):
            return ctx.enter_context(nc.sbuf_tensor(name, shape, dt))

        def sem(name):
            return ctx.enter_context(nc.semaphore(name))

        b2_in = sb("b2_in", [B2_ROWS, SHARED, HID])
        b2_high = sb("b2_high", [B2_ROWS, HID], FP16)
        expert_no = sb("expert_no", [P, EXPERTS])
        valid = sb("valid", [P, 2])
        hot = sb("hot", [P, 2, NCH, EXPERTS])
        both = sb("both", [P, NCH, EXPERTS], FP16)
        until = sb("until", [P, P], FP16)
        ones = sb("ones", [P, P], FP16)
        total = sb("total", [P, NCH, EXPERTS])
        upto = sb("upto", [P, NCH, EXPERTS])
        zeros = sb("zeros", [P, NCH])
        tiles_f = sb("tiles_f", [P, EXPERTS])
        tiles_i = sb("tiles_i", [P, EXPERTS], I32)
        ends = sb("ends", [P, EXPERTS])
        offset = sb("offset", [P, EXPERTS])
        picked = sb("picked", [P, NCH, EXPERTS])
        slot_f = sb("slot_f", [P, NCH, 2])
        slot_u = sb("slot_u", [P, NCH, 2], U32)
        tile_no = sb("tile_no", [P, TILES])
        expd = sb("expd", [P, NCH, 8])
        esum = sb("esum_r", [P, NCH])
        rows = sb("rows", [P, 2, 4, ROW])
        slot_now = sb("slot_now", [P, 2, 4, 2], U32)
        place, past = total, picked[:, 0:TILES, :]
        assert TILES <= NCH

        below_bank, total_bank = bank[6:8], bank[4:6]
        set_up, ones_up, own_s, both_up, counted, slots_ready = (
            sem("set_up"), sem("ones_up"), sem("own_s"), sem("both_up"), sem("counted"), sem("slots_ready"))
        b2_zeroed, b2_loaded, b2_own, b2_rows_in = sem("b2_zeroed"), sem("b2_loaded"), sem("b2_own"), sem("b2_rows_in")
        B2_STEPS = SHARED + 3
        rows_in = [sem(f"rows_in{n}") for n in range(2)]
        scattered = [sem(f"scattered{n}") for n in range(2)]
        totals_read = sem("totals_read")
        idx_set, centred, exps = sem("idx_set"), sem("centred"), sem("exps")
        experts = SharedExperts(nc, ctx, "a", 0, bank, acc, w_hi, w_lo, b1, b2, ones2, x2t_dram)
        NG = SharedExperts.NG
        block = ctx.enter_context(nc.Block())
        HALF = NCH // 2

        def spread(ap, n):
            return ap.rearrange("p (o e) -> p o e", o=1).to_broadcast([P, n, EXPERTS])

        def repeat(ap, n):
            return ap.rearrange("p (c o) -> p c o", o=1).to_broadcast([P, n, EXPERTS])

        @block.sync
        def _(sp):
            def load_rows(i, parity):
                if not (isinstance(i, int) and i < 2):
                    sp.wait_ge(scattered[parity], 64 * (i - parity))
                sp.dma_start(rows[:, parity, :, 0:HID], x2r_dram[i]).then_inc(rows_in[parity], 16)

            experts.load(sp, 0, 0)
            experts.load(sp, 1, 1)
            load_rows(0, 0)
            load_rows(1, 1)
            sp.wait_ge(b2_zeroed, 1)
            for row in (0, B2_LO):
                sp.dma_start(b2_in[row:row + 1, :, :], shared_b2).then_inc(b2_loaded, 16)
            sp.dma_start(b2_rows[:, :], routed_b2).then_inc(b2_rows_in, 16)
            pair_loop(sp, load_rows, 2, PAIRS)
            sp.wait_ge(b2_rows_in, 16)

        @block.gpsimd
        def _(pool):
            pool.iota(expert_no[:, :], pattern=[[1, EXPERTS]], base=0, channel_multiplier=0,
                      allow_small_or_imprecise_dtypes=True).then_inc(set_up, 1)
            pool.iota(tile_no[:, :], pattern=[[1, TILES]], base=0, channel_multiplier=0,
                      allow_small_or_imprecise_dtypes=True).then_inc(set_up, 1)
            pool.memset(ones[:, :], 1.0).then_inc(ones_up, 1)
            pool.memset(until[:, :], -1.0).then_inc(ones_up, 1)
            pool.memset(valid[:, :], 1.0).then_inc(ones_up, 1)
            pool.wait_ge(ones_up, 3)
            pool.affine_select(out=until[:, :], in_=until[:, :], compare_op=ALU.is_ge, fill=0.0, base=0,
                               pattern=[[-1, P]], channel_multiplier=1).then_inc(set_up, 1)
            pool.affine_select(out=valid[:, :], in_=valid[:, :], compare_op=ALU.is_gt, fill=0.0,
                               base=CHUNKS[0][1], pattern=[[CHUNKS[1][1] - CHUNKS[0][1], 2]],
                               channel_multiplier=-1).then_inc(set_up, 1)
            pool.memset(b2_in[:, :, :], 0.0).then_inc(b2_zeroed, 1)
            for f in range(NG):
                experts.low_on_pool(pool, f)
            own = Own(pool, b2_own)
            own.did(pool.memset(ones2[:, :], 1.0))
            pool.wait_ge(b2_loaded, 32)
            for e in range(1, SHARED):
                own.did(pool.tensor_tensor(b2_in[:, 0, :], b2_in[:, 0, :], b2_in[:, e, :], ALU.add))
                own.wait()
            own.did(pool.tensor_copy(b2[0:B2_LO, :], b2_in[0:B2_LO, 0, :]))
            own.did(pool.tensor_copy(b2_high[B2_LO:, :], b2_in[B2_LO:, 0, :]))
            own.wait()
            own.did(pool.tensor_tensor(b2[B2_LO:, :], b2_in[B2_LO:, 0, :], b2_high[B2_LO:, :], ALU.subtract))
            own.wait()
            assert own.n == B2_STEPS

            def step(i, parity):
                pool.wait_ge(rows_in[parity], 8 * (i - parity) + 16)
                settle(pool)
                pool.tensor_copy(rows[:, parity, :, HID:HID + 1],
                                 token2[:, bass.ds(4 * i, 4)].rearrange("p (c o) -> p c o", o=1)).then_inc(idx_set, 1)
                pool.tensor_copy(rows[:, parity, :, HID + 1:], top_i[:, bass.ds(4 * i, 4), 0:1]).then_inc(idx_set, 1)
                pool.tensor_copy(slot_now[:, parity], slot_u[:, bass.ds(4 * i, 4), :]).then_inc(idx_set, 1)
                pool.wait_ge(idx_set, 3 * (i + 1))
                settle(pool)
                for c in range(4):
                    n = CHUNKS[c % 2][1]
                    for k in range(2):
                        pool.indirect_dma_start(
                            out=slots_dram, in_=rows[0:n, parity, c, :], in_offset=None,
                            out_offset=bass.IndirectOffsetOnAxis(ap=slot_now[0:n, parity, c, k:k + 1], axis=0)
                        ).then_inc(scattered[parity], 16)

            pool.wait_ge(slots_ready, 1)
            pair_loop(pool, step, 0, PAIRS)
            for parity in range(2):
                pool.wait_ge(scattered[parity], 64 * PAIRS)

        @block.scalar
        def _(act):
            def step(i, parity):
                for f in range(NG):
                    experts.gelu(act, i, f)
                if not (isinstance(i, int) and i + 2 >= EARLY_PAIRS):
                    experts.load(act, i + 2, parity)

            for f in range(NG):
                experts.gelu(act, 0, f)
                experts.high_on_act(act, f)
            experts.load(act, 2, 0)
            act.wait_ge(centred, 1)
            act.activation(expd[:, :, :], expd[:, :, :], ACT.Exp).then_inc(exps, 1)
            step(1, 1)
            pair_loop(act, step, 2, EARLY_PAIRS - 2)
            step(EARLY_PAIRS - 2, 0)
            step(EARLY_PAIRS - 1, 1)

        @block.vector
        def _(dve):
            own = Own(dve, own_s)

            def after(instruction):
                own.did(instruction)
                own.wait()

            dve.wait_ge(set_up, 4)
            for k in range(2):
                own.did(dve.tensor_tensor(hot[:, k], spread(expert_no[:, :], NCH),
                                          repeat(top_i[:, :, k], NCH), ALU.is_equal))
            own.wait()
            after(dve.tensor_tensor(both[:, :, :], hot[:, 0], hot[:, 1], ALU.add))
            for c in range(2):
                dve.tensor_scalar(both[:, c:NCH:2, :], both[:, c:NCH:2, :], valid[:, c:c + 1],
                                  None, ALU.mult).then_inc(both_up, 1)
            dve.tensor_tensor(expd[:, :, :], top8[:, :, :], top8[:, :, 0:1].to_broadcast([P, NCH, 8]),
                              ALU.subtract).then_inc(centred, 1)
            own.did(dve.memset(zeros[:, :], 0.0))
            dve.wait_ge(counted, 1)
            for n in range(2):
                dve.tensor_copy(total[:, n * HALF:(n + 1) * HALF, :],
                                total_bank[n][:, :].rearrange("p (c e) -> p c e", e=EXPERTS)).then_inc(totals_read, 1)
            own.wait()
            dve.wait_ge(totals_read, 2)
            for e in range(EXPERTS):
                own.did(dve.tensor_tensor_scan(upto[:, :, e], total[:, :, e], zeros[:, :], 0.0, ALU.add, ALU.add))
            own.wait()
            after(dve.tensor_scalar(tiles_i[:, :], upto[:, NCH - 1, :], float(TILE - 1), None, ALU.add))
            after(dve.tensor_scalar(tiles_i[:, :], tiles_i[:, :], TILE.bit_length() - 1, None, ALU.arith_shift_right))
            after(dve.tensor_copy(tiles_f[:, :], tiles_i[:, :]))
            after(dve.tensor_tensor_scan(ends[:, :], tiles_f[:, :], zeros[:, 0:EXPERTS], 0.0, ALU.add, ALU.add))
            after(dve.tensor_tensor(offset[:, :], ends[:, :], tiles_f[:, :], ALU.subtract))
            after(dve.tensor_scalar(offset[:, :], offset[:, :], float(TILE), None, ALU.mult))
            after(dve.tensor_tensor(place[:, :, :], upto[:, :, :], spread(offset[:, :], NCH), ALU.add))
            for n in range(2):
                part = place[:, n * HALF:(n + 1) * HALF, :]
                own.did(dve.tensor_tensor(part, part, below_bank[n][:, :].rearrange("p (c e) -> p c e", e=EXPERTS), ALU.add))
            own.wait()
            for k in range(2):
                after(dve.tensor_tensor(picked[:, :, :], place[:, :, :], hot[:, k], ALU.mult))
                after(dve.reduce_sum(slot_f[:, :, k], picked[:, :, :], axis=AXX))
            dve.tensor_copy(slot_u[:, :, :], slot_f[:, :, :]).then_inc(slots_ready, 1)

            def step(i, parity):
                for f in range(NG):
                    experts.split(dve, i, parity, f)
                    if f == 4:
                        experts.accumulate(dve, i - 1, 0)
                experts.accumulate(dve, i - 1, 1)

            dve.wait_ge(exps, 1)
            after(dve.reduce_sum(esum[:, :], expd[:, :, :], axis=AXX))
            after(dve.reciprocal(esum[:, :], esum[:, :]))
            own.did(dve.tensor_tensor(cw01[:, :, :], expd[:, :, 0:2],
                                      esum[:, :].rearrange("p (c o) -> p c o", o=1).to_broadcast([P, NCH, 2]), ALU.mult))
            step(1, 1)
            own.did(dve.tensor_tensor(past, repeat(tile_no[:, :], TILES), spread(ends[:, :], TILES), ALU.is_ge))
            after(dve.memset(tile_e[:, :], 0.0))
            after(dve.reduce_sum(tile_e[:, 2:2 + TILES], past, axis=AXX))
            after(dve.tensor_scalar(tile_e[:, 2:2 + TILES], tile_e[:, 2:2 + TILES], float(EXPERTS - 1), None, ALU.min))
            word_f = tile_no[:, 0:WORDS]
            after(dve.tensor_copy(word_f, tile_e[:, 0:4 * WORDS:4]))
            for n in range(1, 6):
                after(dve.scalar_tensor_tensor(out=word_f, in0=tile_e[:, n:n + 4 * WORDS - 3:4], scalar=float(EXPERTS ** n),
                                               in1=word_f, op0=ALU.mult, op1=ALU.add))
            own.did(dve.tensor_copy(experts_word[:, :], word_f))
            pair_loop(dve, step, 2, EARLY_PAIRS)
            experts.accumulate(dve, EARLY_PAIRS - 1, 0)
            experts.accumulate(dve, EARLY_PAIRS - 1, 1)

        @block.tensor
        def _(pe):
            for f in range(4):
                experts.up(pe, 0, 0, f)
            pe.wait_ge(set_up, 4)
            pe.wait_ge(both_up, 2)
            for n in range(2):
                rhs = both[:, n * HALF:(n + 1) * HALF, :].rearrange("p c e -> p (c e)")
                pe.matmul(below_bank[n][:, :], until[:, :], rhs, start=True, stop=True)
                last = pe.matmul(total_bank[n][:, :], ones[:, :], rhs, start=True, stop=True)
            last.then_inc(counted, 1)

            for f in range(4, NG):
                experts.up(pe, 0, 0, f)

            def step(i, parity):
                for f in range(NG):
                    experts.up(pe, i, parity, f)
                    if f % 2 == 1:
                        experts.down(pe, i - 1, 1 - parity, f // 2)

            pe.wait_ge(b2_own, B2_STEPS)
            pe.wait_ge(totals_read, 2)
            step(1, 1)
            pair_loop(pe, step, 2, EARLY_PAIRS)
            for c in range(4):
                experts.down(pe, EARLY_PAIRS - 1, 1, c)


def routed_ffn(nc, bank, w_hi, w_lo, b1, b2_rows, ident, tile_e, experts_word, slots_dram, y_dram,
               y_out):
    LAG, AHEAD = 2, 2
    with ExitStack() as ctx:
        def sb(name, shape, dt=FP32):
            return ctx.enter_context(nc.sbuf_tensor(name, shape, dt))

        def sem(name):
            return ctx.enter_context(nc.semaphore(name))

        identh = sb("identh", [P, P], FP16)
        rows = sb("rows_r", [P, 4, TILE_CH, ROW])
        xT = sb("xT_r", [P, 4, 2, TILE], FP16)
        gel = sb("gel_r", [P, 2, NF, TILE])
        hid = sb("hid_r", [P, 4, 2, NF, TILE], FP16)
        y_sb = sb("y_sb", [P, 4, TILE_CH, HID])
        y_row = sb("y_row", [P, 4, TILE_CH], U32)

        tr_bank = [ctx_bank[:, :].bitcast(FP16) for ctx_bank in (bank[6], bank[7])]
        up_bank, down_bank = (bank[0:2], bank[2:4]), bank[4:6]
        ident_up = sem("ident_up")
        rows_in = [sem(f"rrows_in{n}") for n in range(4)]
        x_tr, x_ready, up_done, down_done = sem("x_tr"), sem("x_ready"), sem("rup_done"), sem("rdown_done")
        gel_ready, hid_hi, hid_ready = sem("rgel_ready"), sem("rhid_hi"), sem("rhid_ready")
        y_ready, row_set = sem("y_ready"), sem("row_set")
        block = ctx.enter_context(nc.Block())
        slot_v = slots_dram.rearrange("(t c p) w -> t p c w", p=P, c=TILE_CH)

        class Experts:

            def __init__(self, eng):
                self.eng = eng

            def load(self, j):
                self.word = self.eng.value_load(experts_word[0:1, bass.ds(j, 1)], min_val=0, max_val=EXPERTS ** 6 - 1)
                self.known = {}

            def of(self, n):
                if n not in self.known:
                    self.known[n] = self.eng.snap((self.word >> (3 * (n + 2))) & (EXPERTS - 1), min_val=0,
                                                  max_val=EXPERTS - 1)
                return self.known[n]

        def tiles(eng, step):
            whole = TILES // 4 // 2 * 2 - 1
            for t in range(4):
                step(t, t, 0)
            with eng.Fori(0, (whole - 1) // 2) as j:
                for n in range(8):
                    step(8 * j + 4 + n, n % 4, 2 * j + 1 + n // 4)
            for t in range(4 * whole, TILES):
                step(t, t % 4, t // 4)

        def reaches(t, n):
            return not (isinstance(t, int) and t < n)

        @block.sync
        def _(sp):
            def step(t, slot, four):
                if reaches(t, 4):
                    sp.wait_ge(x_tr, t - 3)
                    sp.wait_ge(row_set, t - 3)
                sp.dma_start(rows[:, slot], slot_v[t]).then_inc(rows_in[slot], 16)

            tiles(sp, step)

        @block.gpsimd
        def _(pool):
            def step(t, slot, four):
                pool.wait_ge(row_set, t + 1)
                pool.wait_ge(y_ready, t + 1)
                settle(pool)
                for c in range(TILE_CH):
                    pool.indirect_dma_start(
                        out=y_dram, in_=y_sb[:, slot, c, :], in_offset=None,
                        out_offset=bass.IndirectOffsetOnAxis(ap=y_row[:, slot, c:c + 1], axis=0),
                        bounds_check=2 * TOKENS - 1, oob_is_err=False).then_inc(y_out[slot], 16)

            tiles(pool, step)

        @block.scalar
        def _(act):
            act.activation(identh[:, :], ident[:, :], ACT.Copy).then_inc(ident_up, 1)

            def columns(t, slot):
                act.wait_ge(x_tr, t + 1)
                if reaches(t, 4):
                    act.wait_ge(up_done, 2 * (t - 3))
                act.activation(xT[:, slot].rearrange("p h n -> p (h n)"),
                               tr_bank[slot % 2][:, 0:2 * TILE], ACT.Copy).then_inc(x_ready, 1)

            def gelu(t, slot, e, half):
                act.wait_ge(up_done, 2 * t + half + 1)
                if reaches(t, 2):
                    act.wait_ge(hid_ready, 2 * t - 3 + half)
                for f in (2 * half, 2 * half + 1):
                    act.activation(gel[:, slot % 2, f, :], up_bank[slot % 2][half][:, (f % 2) * TILE:(f % 2 + 1) * TILE],
                                   ACT.Gelu, bias=b1[:, bass.ds((e + SHARED) * NF + f, 1)]).then_inc(gel_ready, 1)

            def step(t, slot, four):
                if slot == 0:
                    experts.load(four)
                e = experts.of(slot)
                gelu(t, slot, e, 0)
                gelu(t, slot, e, 1)
                if not (isinstance(t, int) and t + AHEAD >= TILES):
                    columns(t + AHEAD, (slot + AHEAD) % 4)

            experts = Experts(act)
            for t in range(AHEAD):
                columns(t, t)
            tiles(act, step)

        @block.vector
        def _(dve):
            def y_rows(t, slot):
                dve.wait_ge(rows_in[slot], 4 * (t - slot) + 16)
                if reaches(t, 4):
                    dve.wait_ge(y_out[slot], 4 * TILE_CH * (t - slot))
                dve.scalar_tensor_tensor(out=y_row[:, slot, :], in0=rows[:, slot, :, HID + 1],
                                         scalar=tile_e[:, bass.ds(t + 2, 1)], in1=rows[:, slot, :, HID],
                                         op0=ALU.not_equal, op1=ALU.add).then_inc(row_set, 1)

            def split(t, slot, half):
                f = slice(2 * half, 2 * half + 2)
                dve.wait_ge(gel_ready, NF * t + 2 * half + 2)
                if reaches(t, 4) and half == 0:
                    dve.wait_ge(down_done, t - 3)
                dve.tensor_copy(hid[:, slot, 0, f, :], gel[:, slot % 2, f, :]).then_inc(hid_hi, 1)
                dve.wait_ge(hid_hi, 2 * t + half + 1)
                dve.tensor_tensor(hid[:, slot, 1, f, :], gel[:, slot % 2, f, :], hid[:, slot, 0, f, :],
                                  ALU.subtract).then_inc(hid_ready, 1)

            def out_y(t, slot, e):
                dve.wait_ge(down_done, t + 1)
                if reaches(t, 4):
                    dve.wait_ge(y_out[slot], 4 * TILE_CH * (t - slot))
                settle(dve)
                bias = b2_rows[:, bass.ds(e * HID, HID)].rearrange("p (o d) -> p o d", o=1)
                dve.tensor_tensor(y_sb[:, slot], down_bank[slot % 2][:, 0:TILE_CH * HID].rearrange(
                    "p (c d) -> p c d", c=TILE_CH), bias.to_broadcast([P, TILE_CH, HID]), ALU.add).then_inc(y_ready, 1)

            experts = Experts(dve)

            def step(t, slot, four):
                if slot == 0:
                    experts.load(four)
                split(t, slot, 0)
                split(t, slot, 1)
                y_rows(t, slot)
                if reaches(t, LAG):
                    out_y(t - LAG, (slot - LAG) % 4, experts.of(slot - LAG))

            tiles(dve, step)
            for t in range(TILES - LAG, TILES):
                out_y(t, t % 4, experts.of(t - (TILES - 1) // 4 * 4))

        @block.tensor
        def _(pe):
            def transposes(t, slot):
                pe.wait_ge(rows_in[slot], 4 * (t - slot) + 16)
                if reaches(t, 2):
                    pe.wait_ge(x_ready, t - 1)
                for h in range(2):
                    for c in range(TILE_CH):
                        x16 = rows[:, slot, c, h * HID // 2:(h + 1) * HID // 2].bitcast(FP16)
                        last = pe.transpose(tr_bank[slot % 2][:, h * TILE + c * P:h * TILE + (c + 1) * P], x16, identh[:, :])
                last.then_inc(x_tr, 1)

            def up(t, slot, e, f):
                if f == 0:
                    pe.wait_ge(x_ready, t + 1)
                if f % 2 == 0 and reaches(t, 2):
                    pe.wait_ge(gel_ready, NF * (t - 2) + f + 2)
                dst = up_bank[slot % 2][f // 2][:, (f % 2) * TILE:(f % 2 + 1) * TILE]
                w1 = bass.ds((e + SHARED) * F, F)
                hi = w_hi[:, w1][:, f * P:(f + 1) * P]
                lo = w_lo[:, w1][:, f * P:(f + 1) * P]
                pe.matmul(dst, hi, xT[:, slot, 0, :], start=True, stop=False)
                pe.matmul(dst, hi, xT[:, slot, 1, :], start=False, stop=False)
                last = pe.matmul(dst, lo, xT[:, slot, 0, :], start=False, stop=True)
                if f % 2 == 1:
                    last.then_inc(up_done, 1)

            def down(t, slot, e):
                pe.wait_ge(hid_ready, 2 * t + 2)
                if reaches(t, 2):
                    pe.wait_ge(y_ready, t - 1)
                dsts = [down_bank[slot % 2][:, c * HID:(c + 1) * HID] for c in range(TILE_CH)]
                for c, dst in enumerate(dsts):
                    for f in range(NF):
                        w2 = bass.ds(W2_AT + (e + SHARED) * F, F)
                        w2_hi, w2_lo = w_hi[:, w2][:, f * P:(f + 1) * P], w_lo[:, w2][:, f * P:(f + 1) * P]
                        h_hi, h_lo = hid[:, slot, 0, f, c * P:(c + 1) * P], hid[:, slot, 1, f, c * P:(c + 1) * P]
                        pe.matmul(dst, h_hi, w2_hi, start=f == 0, stop=False)
                        pe.matmul(dst, h_hi, w2_lo, start=False, stop=False)
                        last = pe.matmul(dst, h_lo, w2_hi, start=False, stop=f == NF - 1)
                last.then_inc(down_done, 1)

            experts = Experts(pe)

            def step(t, slot, four):
                if slot == 0:
                    experts.load(four)
                e = experts.of(slot)
                up(t, slot, e, 0)
                up(t, slot, e, 1)
                if not (isinstance(t, int) and t + AHEAD >= TILES):
                    transposes(t + AHEAD, (slot + AHEAD) % 4)
                up(t, slot, e, 2)
                up(t, slot, e, 3)
                if reaches(t, LAG):
                    down(t - LAG, (slot - LAG) % 4, experts.of(slot - LAG))

            pe.wait_ge(ident_up, 1)
            for t in range(AHEAD):
                transposes(t, t)
            tiles(pe, step)
            for t in range(TILES - LAG, TILES):
                down(t, t % 4, experts.of(t % 4))


def share_and_combine(nc, bank, acc, w_hi, w_lo, b1, b2, ones2, cw01, x2t_dram, y_dram, y_out, out):
    LATE = PAIRS - EARLY_PAIRS
    WEIGH_AFTER = (0, 1, 2, 3, 4, 5, 7)
    PER_STEP = len(WEIGH_AFTER)
    assert all(PER_STEP * k + PER_STEP - 1 < EARLY_PAIRS + max(k - 1, 0) for k in range(LATE))
    with ExitStack() as ctx:
        def sem(name):
            return ctx.enter_context(nc.semaphore(name))

        y = ctx.enter_context(nc.sbuf_tensor("y", [P, PER_STEP, 2, 2, 2 * HID], FP32))
        y_in = [sem(f"y_in{n}") for n in range(PER_STEP)]
        weighted, added0, added1, stored = sem("weighted"), sem("added0"), sem("added1"), sem("stored")
        experts = SharedExperts(nc, ctx, "b", EARLY_PAIRS, bank, acc, w_hi, w_lo, b1, b2, ones2, x2t_dram)
        NG = SharedExperts.NG
        block = ctx.enter_context(nc.Block())
        y_v = y_dram.rearrange("(b i s k) d -> b s i (k d)", i=2, s=SEQ, k=2)
        out_v = out.rearrange("(b i) s d -> b s i d", i=2)

        @block.sync
        def _(sp):
            def load_y(i):
                for c, (at, n) in enumerate(CHUNKS):
                    sp.dma_start(y[0:n, i % PER_STEP, :, c], y_v[i, at:at + n]).then_inc(y_in[i % PER_STEP], 16)

            def store(i):
                sp.wait_ge(added1, 2 * i + 2)
                for c, (at, n) in enumerate(CHUNKS):
                    sp.dma_start(out_v[i, at:at + n], acc[0:n, 4 * i:4 * i + 4, :].rearrange("p (i c) d -> p i c d", c=2)[:, :, c, :]
                                 ).then_inc(stored, 16)

            experts.load(sp, 0, 0)
            experts.load(sp, 1, 1)
            for slot in range(4):
                sp.wait_ge(y_out[slot], 16 * TILE_CH * len(range(slot, TILES, 4)))
            for i in range(PER_STEP):
                load_y(i)
            for k in range(LATE):
                for i in range(PER_STEP * k, PER_STEP * (k + 1)):
                    store(i)
                    if i + PER_STEP < PAIRS:
                        load_y(i + PER_STEP)
                if k + 2 < LATE:
                    experts.load(sp, k + 2, k % 2)
            for i in range(PER_STEP * LATE, PAIRS):
                store(i)
            sp.wait_ge(stored, 32 * PAIRS)

        @block.scalar
        def _(act):
            def weigh1(i, k, j):
                act.wait_ge(y_in[j], 32 * (k + 1))
                for c in range(4):
                    n = CHUNKS[c % 2][1]
                    part = y[0:n, j, c // 2, c % 2, HID:]
                    last = act.activation(part, part, ACT.Copy, scale=cw01[0:n, 4 * i + c, 1:2])
                last.then_inc(weighted, 1)

            def step(k, parity):
                for f in range(NG):
                    experts.gelu(act, k, f)
                    if f in WEIGH_AFTER:
                        j = WEIGH_AFTER.index(f)
                        weigh1(PER_STEP * k + j, k, j)

            for k in range(LATE):
                step(k, k % 2)
            for j in range(PAIRS - PER_STEP * LATE):
                weigh1(PER_STEP * LATE + j, LATE, j)

        @block.vector
        def _(dve):
            def weigh0(i, k, j):
                dve.wait_ge(y_in[j], 32 * (k + 1))
                if i >= EARLY_PAIRS:
                    dve.wait_ge(experts.acc_done, 2 * (i - EARLY_PAIRS + 1))
                for c in range(4):
                    n = CHUNKS[c % 2][1]
                    row = acc[0:n, 4 * i + c, :]
                    last = dve.scalar_tensor_tensor(
                        out=row, in0=y[0:n, j, c // 2, c % 2, 0:HID], scalar=cw01[0:n, 4 * i + c, 0:1],
                        in1=row, op0=ALU.mult, op1=ALU.add)
                last.then_inc(added0, 1)

            def step(k, parity):
                for f in range(NG):
                    experts.split(dve, k, parity, f)
                    if k > 0 and f in (6, 7):
                        experts.accumulate(dve, k - 1, f - 6)
                    if f in WEIGH_AFTER:
                        j = WEIGH_AFTER.index(f)
                        weigh0(PER_STEP * k + j, k, j)

            for k in range(LATE):
                step(k, k % 2)
            for i in range(PER_STEP * LATE, PAIRS):
                if i == PAIRS - 1:
                    for img in range(2):
                        experts.accumulate(dve, LATE - 1, img)
                weigh0(i, LATE, i - PER_STEP * LATE)

        @block.gpsimd
        def _(pool):
            for i in range(PAIRS):
                pool.wait_ge(added0, i + 1)
                pool.wait_ge(weighted, i + 1)
                for c, (_, n) in enumerate(CHUNKS):
                    part = acc[0:n, 4 * i + c:4 * i + 4:2, :]
                    pool.tensor_tensor(part, part, y[0:n, i % PER_STEP, :, c, HID:], ALU.add).then_inc(added1, 1)

        @block.tensor
        def _(pe):
            for k in range(LATE + 1):
                for f in range(NG):
                    if k < LATE:
                        experts.up(pe, k, k % 2, f)
                    if k > 0 and f >= 4:
                        experts.down(pe, k - 1, (k - 1) % 2, f - 4)


def layouts(x, x_txt, L0_tok_W, L0_tok_b, L0_tok_token, L0_tok_pos, L0_txt_emb2, L0_txt_emb3,
            L0_txt_emb4, L0_attn_w, L0_attn_uv_w, L0_attn_o_w, L0_attn_gamma, L0_attn_beta,
            L0_attn_g, L0_attn_res_scale, L0_ffn_gate_w, L0_ffn_gate_b, L0_ffn_sw1, L0_ffn_sb1,
            L0_ffn_sw2, L0_ffn_sb2, L0_ffn_rw1, L0_ffn_rb1, L0_ffn_rw2, L0_ffn_rb2):
    side = SIDE // GRID
    cols = (np.asarray(x).reshape(PAIRS, 2, CHANNELS, GRID, side, GRID, side)
            .transpose(0, 2, 4, 6, 1, 3, 5).reshape(PAIRS, PATCH_DIM, PAIR_PATCHES))
    tokw = np.asarray(L0_tok_W).T
    w1 = np.concatenate([np.asarray(L0_ffn_sw1), np.asarray(L0_ffn_rw1)])
    w2 = np.concatenate([np.asarray(L0_ffn_sw2), np.asarray(L0_ffn_rw2)])
    b1 = np.concatenate([np.asarray(L0_ffn_sb1), np.asarray(L0_ffn_rb1)])
    arrays = {
        "xmain": cols[:, :KN * KP].reshape(PAIRS, KN, KP, PAIR_PATCHES).transpose(0, 2, 1, 3),
        "xrest": cols[:, KN * KP:],
        "tokw_main": tokw[:KN * KP].reshape(KN, KP, HID).transpose(1, 0, 2),
        "tokw_rest": tokw[KN * KP:],
        "txt": np.stack([np.pad(np.asarray(x_txt), ((0, 0), (k, 0)))[:, :TEXT].reshape(16, 4, TEXT)
                         .transpose(1, 2, 0).reshape(P, 16) for k in range(4)], axis=1),
        "tokb": np.asarray(L0_tok_b).reshape(P, 1),
        "token": np.asarray(L0_tok_token).reshape(P, 1),
        "pos": np.asarray(L0_tok_pos).T,
        "emb2": np.asarray(L0_txt_emb2),
        "emb3": np.asarray(L0_txt_emb3),
        "emb4": np.asarray(L0_txt_emb4),
        "w_rel": np.asarray(L0_attn_w)[SEQ - 1 + np.arange(SEQ)[:, None] - np.arange(SEQ)[None, :]],
        "uv_w": np.asarray(L0_attn_uv_w),
        "o_w": np.asarray(L0_attn_o_w).reshape(2, P, HID).transpose(1, 0, 2),
        "gamma": np.asarray(L0_attn_gamma).T,
        "beta": np.asarray(L0_attn_beta).T,
        "g": np.broadcast_to(np.asarray(L0_attn_g).reshape(1, 1), (P, 1)),
        "res": np.broadcast_to(np.asarray(L0_attn_res_scale), (P, HID)),
        "gate_w": np.asarray(L0_ffn_gate_w).T,
        "gate_b": np.broadcast_to(np.asarray(L0_ffn_gate_b), (P, EXPERTS)),
        "ffn_w": np.concatenate([w1.transpose(2, 0, 1).reshape(P, -1),
                                 w2.transpose(0, 2, 1).reshape(ALL_EXPERTS, NF, P, HID).transpose(2, 0, 1, 3)
                                 .reshape(P, -1)], axis=1),
        "ffn_b1": b1.reshape(ALL_EXPERTS * NF, P).T,
        "shared_b2": np.asarray(L0_ffn_sb2).reshape(1, SHARED, HID),
        "routed_b2": np.broadcast_to(np.asarray(L0_ffn_rb2).reshape(1, -1), (P, EXPERTS * HID)),
    }
    return {name: np.ascontiguousarray(a) for name, a in arrays.items()}


def kernel(**inputs):
    import concourse.bacc as bacc
    from concourse.bass_utils import run_bass_kernel_spmd

    arrays = layouts(**inputs)
    nc = bacc.Bacc("TRN2", target_bir_lowering=False, num_devices=1)
    args = [nc.dram_tensor(f"in_{name}", a.shape, mybir.dt.from_np(a.dtype), kind="ExternalInput").ap()
            for name, a in arrays.items()]
    out = nc.dram_tensor("out", (IMGS, SEQ, HID), FP32, kind="ExternalOutput").ap()
    build(nc, *args, out)
    r = run_bass_kernel_spmd(nc, [{f"in_{name}": a for name, a in arrays.items()}], core_ids=[0])
    return r.results[0]["out"]
```
